# Optimizing a Trainium2 kernel written in Bass

```python
import numpy as np
import jax
import jax.numpy as jnp

def _softmax(x, axis=-1):
    return jax.nn.softmax(x, axis=axis)

def _gelu(x):
    return jax.nn.gelu(x, approximate=True)

def _silu(x):
    return jax.nn.silu(x)

def _sigmoid(x):
    return jax.nn.sigmoid(x)

def _layernorm(x, axis=-1, eps=1e-05):
    m = jnp.mean(x, axis=axis, keepdims=True)
    v = jnp.var(x, axis=axis, keepdims=True)
    return (x - m) / jnp.sqrt(v + eps)

def _scatter_add(tgt, idx, src, axis=0):
    return tgt.at[idx].add(src)

def _segment_sum(src, seg, n):
    return jax.ops.segment_sum(src, seg, n)
kernel_name = 'mk_pixart_seq_d2_seqx_r8_0aa68d'

def setup_inputs(seed: int=0):
    np.random.seed(seed)
    _w = jnp.asarray

    def _rec_inputs():
        import jax
        import jax.numpy as jnp
        _rk = jax.random.key(seed)
        x = -0.0003929 + 0.9999 * jax.random.normal(jax.random.fold_in(_rk, 1), (2, 512, 128), jnp.float32)
        _lenS = 512 - jax.random.randint(jax.random.fold_in(_rk, 7), (2,), 0, max(1, 512 // 4) + 1, jnp.int32)
        _lenS2 = 77 - jax.random.randint(jax.random.fold_in(_rk, 8), (2,), 0, max(1, 77 // 4) + 1, jnp.int32)
        cond_1024 = 0.00782532 + 1.00527 * jax.random.normal(jax.random.fold_in(_rk, 11), (2, 128), jnp.float32)
        _ctx_1024P = jax.random.normal(jax.random.fold_in(_rk, 12), (2, 16, 128), jnp.float32)
        _ctx_1024c = jax.random.dirichlet(jax.random.fold_in(_rk, 512), 0.3 * jnp.ones((16,), jnp.float32), (2, 77))
        _ctx_1024t = jnp.einsum('bsk,bkd->bsd', _ctx_1024c, _ctx_1024P)
        _ctx_1024t = _ctx_1024t * jax.lax.rsqrt(jnp.mean(jnp.square(_ctx_1024t)) + 1e-12) * 0.953939
        ctx_1024 = -0.000761806 + 0.999296 * (_ctx_1024t + 0.3 * jax.random.normal(jax.random.fold_in(_rk, 612), (2, 77, 128), jnp.float32))
        return (x, cond_1024, ctx_1024)
    x, cond_1024, ctx_1024 = _rec_inputs()

    def _L0_xcond_setup():
        import jax, jax.numpy as jnp
        import numpy as np
        H = 128
        RH = 2 * H
        E = 3
        B, T, P = (8, 256, 64)
        LN_EPS = 1e-05

        def _layer_norm(x, gamma, beta):
            mu = jnp.mean(x, axis=-1, keepdims=True)
            var = jnp.mean(jnp.square(x - mu), axis=-1, keepdims=True)
            return (x - mu) * jax.lax.rsqrt(var + LN_EPS) * gamma + beta
        key = jax.random.key(seed)
        ks = jax.random.split(key, 24)
        s = lambda fan_in: 1.0 / np.sqrt(fan_in)
        inp = {'mix_hidden_states': jax.random.normal(ks[0], (B, T, H), jnp.float32), 'global_anchor': jax.random.normal(ks[1], (B, H), jnp.float32), 'prototype_bank': jax.random.normal(ks[2], (B, P, H), jnp.float32), 'ln_gamma': jnp.ones((H,), jnp.float32), 'ln_beta': jnp.zeros((H,), jnp.float32), 'Wq': jax.random.normal(ks[3], (H, H), jnp.float32) * s(H), 'Wk': jax.random.normal(ks[4], (H, H), jnp.float32) * s(H), 'Wv': jax.random.normal(ks[5], (H, H), jnp.float32) * s(H), 'router_W': jax.random.normal(ks[6], (3 * H, E), jnp.float32) * s(3 * H), 'router_b': jnp.zeros((E,), jnp.float32), 'e_w1': jax.random.normal(ks[7], (E, 3 * H, RH), jnp.float32) * s(3 * H), 'e_b1': jnp.zeros((E, RH), jnp.float32), 'e_w2': jax.random.normal(ks[8], (E, RH, H), jnp.float32) * s(RH), 'e_b2': jnp.zeros((E, H), jnp.float32), 'gate_w1': jax.random.normal(ks[9], (3 * H, H), jnp.float32) * s(3 * H), 'gate_b1': jnp.zeros((H,), jnp.float32), 'gate_w2': jax.random.normal(ks[10], (H, H), jnp.float32) * s(H), 'gate_b2': jnp.zeros((H,), jnp.float32), 'out_w': jax.random.normal(ks[11], (H, H), jnp.float32) * s(H), 'out_b': jnp.zeros((H,), jnp.float32)}
        return inp
    _L0_xcond_all = _L0_xcond_setup()
    _L0_xcond_in = {k: v for k, v in _L0_xcond_all.items() if k in ('ln_gamma', 'ln_beta', 'Wq', 'Wk', 'Wv', 'router_W', 'router_b', 'e_w1', 'e_b1', 'e_w2', 'e_b2', 'gate_w1', 'gate_b1', 'gate_w2', 'gate_b2', 'out_w', 'out_b')}
    del _L0_xcond_all

    def _L1_xcond_setup():
        import jax, jax.numpy as jnp
        import numpy as np
        EPS = 1e-06
        H = 16

        def layer_norm(x, gamma=None, beta=None):
            x32 = x.astype(jnp.float32)
            mu = jnp.mean(x32, axis=-1, keepdims=True)
            var = jnp.var(x32, axis=-1, keepdims=True)
            y = (x32 - mu) * jax.lax.rsqrt(var + EPS)
            if gamma is not None:
                y = y * gamma + beta
            return y.astype(x.dtype)

        def mha(q, k, v):
            B, Nq, C = q.shape
            d = C // H
            qh = q.reshape(B, Nq, H, d)
            kh = k.reshape(B, k.shape[1], H, d)
            vh = v.reshape(B, v.shape[1], H, d)
            scores = jnp.einsum('bqhd,bkhd->bhqk', qh, kh) / jnp.sqrt(jnp.asarray(d, q.dtype))
            attn = jax.nn.softmax(scores, axis=-1)
            out = jnp.einsum('bhqk,bkhd->bqhd', attn, vh)
            return out.reshape(B, Nq, C)
        key = jax.random.key(seed)
        ks = jax.random.split(key, 24)
        B, N, C, M, Cc = (4, 256, 128, 128, 128)
        hid = 4 * C
        s = 0.02
        return {'x': jax.random.normal(ks[0], (B, N, C), jnp.float32), 'mod': jax.random.normal(ks[1], (B, C), jnp.float32), 'context': jax.random.normal(ks[2], (B, M, Cc), jnp.float32), 'ada_w': jax.random.normal(ks[3], (C, 6 * C), jnp.float32) * s, 'ada_b': jnp.zeros((6 * C,), jnp.float32), 'qkv_w': jax.random.normal(ks[4], (C, 3 * C), jnp.float32) * s, 'qkv_b': jnp.zeros((3 * C,), jnp.float32), 'self_o_w': jax.random.normal(ks[5], (C, C), jnp.float32) * s, 'self_o_b': jnp.zeros((C,), jnp.float32), 'norm2_g': jnp.ones((C,), jnp.float32), 'norm2_b': jnp.zeros((C,), jnp.float32), 'q_w': jax.random.normal(ks[6], (C, C), jnp.float32) * s, 'q_b': jnp.zeros((C,), jnp.float32), 'kv_w': jax.random.normal(ks[7], (Cc, 2 * C), jnp.float32) * s, 'kv_b': jnp.zeros((2 * C,), jnp.float32), 'cross_o_w': jax.random.normal(ks[8], (C, C), jnp.float32) * s, 'cross_o_b': jnp.zeros((C,), jnp.float32), 'mlp_w1': jax.random.normal(ks[9], (C, hid), jnp.float32) * s, 'mlp_b1': jnp.zeros((hid,), jnp.float32), 'mlp_w2': jax.random.normal(ks[10], (hid, C), jnp.float32) * s, 'mlp_b2': jnp.zeros((C,), jnp.float32)}
    _L1_xcond_all = _L1_xcond_setup()
    _L1_xcond_in = {k: v for k, v in _L1_xcond_all.items() if k in ('ada_w', 'ada_b', 'qkv_w', 'qkv_b', 'self_o_w', 'self_o_b', 'norm2_g', 'norm2_b', 'q_w', 'q_b', 'kv_w', 'kv_b', 'cross_o_w', 'cross_o_b', 'mlp_w1', 'mlp_b1', 'mlp_w2', 'mlp_b2')}
    del _L1_xcond_all
    return {'x': x, 'cond_1024': cond_1024, 'ctx_1024': ctx_1024, 'L0_xcond_ln_gamma': _L0_xcond_in['ln_gamma'], 'L0_xcond_ln_beta': _L0_xcond_in['ln_beta'], 'L0_xcond_Wq': _L0_xcond_in['Wq'], 'L0_xcond_Wk': _L0_xcond_in['Wk'], 'L0_xcond_Wv': _L0_xcond_in['Wv'], 'L0_xcond_router_W': _L0_xcond_in['router_W'], 'L0_xcond_router_b': _L0_xcond_in['router_b'], 'L0_xcond_e_w1': _L0_xcond_in['e_w1'], 'L0_xcond_e_b1': _L0_xcond_in['e_b1'], 'L0_xcond_e_w2': _L0_xcond_in['e_w2'], 'L0_xcond_e_b2': _L0_xcond_in['e_b2'], 'L0_xcond_gate_w1': _L0_xcond_in['gate_w1'], 'L0_xcond_gate_b1': _L0_xcond_in['gate_b1'], 'L0_xcond_gate_w2': _L0_xcond_in['gate_w2'], 'L0_xcond_gate_b2': _L0_xcond_in['gate_b2'], 'L0_xcond_out_w': _L0_xcond_in['out_w'], 'L0_xcond_out_b': _L0_xcond_in['out_b'], 'L1_xcond_ada_w': _L1_xcond_in['ada_w'], 'L1_xcond_ada_b': _L1_xcond_in['ada_b'], 'L1_xcond_qkv_w': _L1_xcond_in['qkv_w'], 'L1_xcond_qkv_b': _L1_xcond_in['qkv_b'], 'L1_xcond_self_o_w': _L1_xcond_in['self_o_w'], 'L1_xcond_self_o_b': _L1_xcond_in['self_o_b'], 'L1_xcond_norm2_g': _L1_xcond_in['norm2_g'], 'L1_xcond_norm2_b': _L1_xcond_in['norm2_b'], 'L1_xcond_q_w': _L1_xcond_in['q_w'], 'L1_xcond_q_b': _L1_xcond_in['q_b'], 'L1_xcond_kv_w': _L1_xcond_in['kv_w'], 'L1_xcond_kv_b': _L1_xcond_in['kv_b'], 'L1_xcond_cross_o_w': _L1_xcond_in['cross_o_w'], 'L1_xcond_cross_o_b': _L1_xcond_in['cross_o_b'], 'L1_xcond_mlp_w1': _L1_xcond_in['mlp_w1'], 'L1_xcond_mlp_b1': _L1_xcond_in['mlp_b1'], 'L1_xcond_mlp_w2': _L1_xcond_in['mlp_w2'], 'L1_xcond_mlp_b2': _L1_xcond_in['mlp_b2']}

def reference(x, cond_1024, ctx_1024, L0_xcond_ln_gamma, L0_xcond_ln_beta, L0_xcond_Wq, L0_xcond_Wk, L0_xcond_Wv, L0_xcond_router_W, L0_xcond_router_b, L0_xcond_e_w1, L0_xcond_e_b1, L0_xcond_e_w2, L0_xcond_e_b2, L0_xcond_gate_w1, L0_xcond_gate_b1, L0_xcond_gate_w2, L0_xcond_gate_b2, L0_xcond_out_w, L0_xcond_out_b, L1_xcond_ada_w, L1_xcond_ada_b, L1_xcond_qkv_w, L1_xcond_qkv_b, L1_xcond_self_o_w, L1_xcond_self_o_b, L1_xcond_norm2_g, L1_xcond_norm2_b, L1_xcond_q_w, L1_xcond_q_b, L1_xcond_kv_w, L1_xcond_kv_b, L1_xcond_cross_o_w, L1_xcond_cross_o_b, L1_xcond_mlp_w1, L1_xcond_mlp_b1, L1_xcond_mlp_w2, L1_xcond_mlp_b2):
    import jax
    import jax.numpy as jnp

    def _L0_xcond_ref(mix_hidden_states, global_anchor, prototype_bank, ln_gamma, ln_beta, Wq, Wk, Wv, router_W, router_b, e_w1, e_b1, e_w2, e_b2, gate_w1, gate_b1, gate_w2, gate_b2, out_w, out_b):
        import jax, jax.numpy as jnp
        import numpy as np
        H = 128
        RH = 2 * H
        E = 3
        B, T, P = (8, 256, 64)
        LN_EPS = 1e-05

        def _layer_norm(x, gamma, beta):
            mu = jnp.mean(x, axis=-1, keepdims=True)
            var = jnp.mean(jnp.square(x - mu), axis=-1, keepdims=True)
            return (x - mu) * jax.lax.rsqrt(var + LN_EPS) * gamma + beta
        x = mix_hidden_states
        nx = _layer_norm(x, ln_gamma, ln_beta)
        q = nx @ Wq
        k = prototype_bank @ Wk
        v = prototype_bank @ Wv
        scores = jnp.einsum('bth,bph->btp', q, k) * H ** (-0.5)
        weights = jax.nn.softmax(scores, axis=-1)
        evidence = jnp.einsum('btp,bph->bth', weights, v)
        anchor = jnp.broadcast_to(global_anchor[:, None, :], nx.shape)
        combined = jnp.concatenate([nx, evidence, anchor], axis=-1)
        router_logits = combined @ router_W + router_b
        router_probs = jax.nn.softmax(router_logits, axis=-1)
        h = jax.nn.silu(jnp.einsum('btc,ecr->bter', combined, e_w1) + e_b1)
        expert_out = jnp.einsum('bter,erh->bteh', h, e_w2) + e_b2
        routed = jnp.sum(expert_out * router_probs[..., None], axis=-2)
        g = jax.nn.sigmoid(jax.nn.silu(combined @ gate_w1 + gate_b1) @ gate_w2 + gate_b2)
        refined_delta = g * (routed @ out_w + out_b)
        return x + refined_delta

    def _L1_xcond_ref(x, mod, context, ada_w, ada_b, qkv_w, qkv_b, self_o_w, self_o_b, norm2_g, norm2_b, q_w, q_b, kv_w, kv_b, cross_o_w, cross_o_b, mlp_w1, mlp_b1, mlp_w2, mlp_b2):
        import jax, jax.numpy as jnp
        import numpy as np
        EPS = 1e-06
        H = 16

        def layer_norm(x, gamma=None, beta=None):
            x32 = x.astype(jnp.float32)
            mu = jnp.mean(x32, axis=-1, keepdims=True)
            var = jnp.var(x32, axis=-1, keepdims=True)
            y = (x32 - mu) * jax.lax.rsqrt(var + EPS)
            if gamma is not None:
                y = y * gamma + beta
            return y.astype(x.dtype)

        def mha(q, k, v):
            B, Nq, C = q.shape
            d = C // H
            qh = q.reshape(B, Nq, H, d)
            kh = k.reshape(B, k.shape[1], H, d)
            vh = v.reshape(B, v.shape[1], H, d)
            scores = jnp.einsum('bqhd,bkhd->bhqk', qh, kh) / jnp.sqrt(jnp.asarray(d, q.dtype))
            attn = jax.nn.softmax(scores, axis=-1)
            out = jnp.einsum('bhqk,bkhd->bqhd', attn, vh)
            return out.reshape(B, Nq, C)
        C = x.shape[-1]
        m = jax.nn.silu(mod) @ ada_w + ada_b
        shift_msa, scale_msa, gate_msa, shift_mlp, scale_mlp, gate_mlp = [c[:, None, :] for c in jnp.split(m, 6, axis=-1)]
        h = layer_norm(x)
        h = h * (1.0 + scale_msa) + shift_msa
        qkv = h @ qkv_w + qkv_b
        q, k, v = jnp.split(qkv, 3, axis=-1)
        h = mha(q, k, v) @ self_o_w + self_o_b
        x = x + h * gate_msa
        h = layer_norm(x, norm2_g, norm2_b)
        q = h @ q_w + q_b
        kv = context @ kv_w + kv_b
        k, v = jnp.split(kv, 2, axis=-1)
        h = mha(q, k, v) @ cross_o_w + cross_o_b
        x = x + h
        h = layer_norm(x)
        h = h * (1.0 + scale_mlp) + shift_mlp
        h = jax.nn.gelu(h @ mlp_w1 + mlp_b1) @ mlp_w2 + mlp_b2
        x = x + h * gate_mlp
        return x
    x = _L0_xcond_ref(x, cond_1024, ctx_1024, L0_xcond_ln_gamma, L0_xcond_ln_beta, L0_xcond_Wq, L0_xcond_Wk, L0_xcond_Wv, L0_xcond_router_W, L0_xcond_router_b, L0_xcond_e_w1, L0_xcond_e_b1, L0_xcond_e_w2, L0_xcond_e_b2, L0_xcond_gate_w1, L0_xcond_gate_b1, L0_xcond_gate_w2, L0_xcond_gate_b2, L0_xcond_out_w, L0_xcond_out_b)
    x = _L1_xcond_ref(x, cond_1024, ctx_1024, L1_xcond_ada_w, L1_xcond_ada_b, L1_xcond_qkv_w, L1_xcond_qkv_b, L1_xcond_self_o_w, L1_xcond_self_o_b, L1_xcond_norm2_g, L1_xcond_norm2_b, L1_xcond_q_w, L1_xcond_q_b, L1_xcond_kv_w, L1_xcond_kv_b, L1_xcond_cross_o_w, L1_xcond_cross_o_b, L1_xcond_mlp_w1, L1_xcond_mlp_b1, L1_xcond_mlp_w2, L1_xcond_mlp_b2)
    return x

_drawn_inputs = setup_inputs


def setup_inputs(seed=0):
    import zlib

    import numpy as np

    out = dict(_drawn_inputs(seed))
    spreads = {'L0_xcond_ln_gamma': (1.0, 0.2),
     'L0_xcond_ln_beta': (0.0, 0.59),
     'L0_xcond_router_b': (0.0, 0.8),
     'L0_xcond_e_b1': (0.0, 0.35),
     'L0_xcond_e_b2': (0.0, 0.1),
     'L0_xcond_gate_b1': (0.0, 0.8),
     'L0_xcond_gate_b2': (0.0, 0.8),
     'L0_xcond_out_b': (0.0, 0.1),
     'L1_xcond_ada_b': (0.0, 0.581),
     'L1_xcond_qkv_b': (0.0, 0.8),
     'L1_xcond_self_o_b': (0.0, 0.591),
     'L1_xcond_norm2_g': (1.0, 0.6),
     'L1_xcond_norm2_b': (0.0, 2.0),
     'L1_xcond_q_b': (0.0, 2.0),
     'L1_xcond_kv_b': (0.0, 0.971),
     'L1_xcond_cross_o_b': (0.0, 0.268),
     'L1_xcond_mlp_b1': (0.0, 0.8),
     'L1_xcond_mlp_b2': (0.0, 0.494)}
    factors = {'L1_xcond_ada_w': 3.026,
     'L1_xcond_qkv_w': 8.0,
     'L1_xcond_self_o_w': 8.0,
     'L1_xcond_q_w': 64.0,
     'L1_xcond_mlp_w1': 6.474,
     'L1_xcond_mlp_w2': 6.12,
     'L1_xcond_kv_w': 6.922}
    for name, (base, spread) in spreads.items():
        noise = np.random.default_rng([zlib.crc32(name.encode()), seed]).standard_normal(out[name].shape)
        drawn = base * np.exp(spread * noise) if base else spread * noise
        out[name] = jnp.asarray(drawn.astype(out[name].dtype))
    for name, factor in factors.items():
        out[name] = (out[name] * factor).astype(out[name].dtype)
    return out
```

```python
import concourse.bass as bass
from concourse import mybir
from contextlib import ExitStack

B, T, C, L = 2, 512, 128, 77
P = 128
NT = T // P
NEXP = 3
RH = 2 * C
HC = NEXP * RH // P + 1
NH = 16
D = C // NH
HG = 4
NG = NH // HG
MC = 4 * C // P
VS = D + 1
VW = NH * VS + 32 - VS
NPART = 3
MROW = NPART * NPART * D
KS = 96
LP = 96
LN_EPS = (1e-5, 1e-6, 1e-6, 1e-6)
UNITS = 4

COLS = ["cond0", "cond1", "ln_gamma", "ln_beta", "e_b1_0", "e_b1_1", "e_b1_2", "e_b1_3", "e_b1_4", "e_b1_5",
        "gate_b1", "shift_msa", "scale_msa", "shift_mlp", "scale_mlp", "qkv_q", "qkv_k", "qkv_v", "norm2_g",
        "norm2_b", "q_b", "kv_k", "kv_v", "mlp_b1_0", "mlp_b1_1", "mlp_b1_2", "mlp_b1_3", "e_b2_0", "e_b2_1",
        "e_b2_2"]
ROWS = ["gate_b2", "out_b", "gate_msa", "gate_mlp", "self_o_b", "cross_o_b", "mlp_b2"]
PACKS = {
    "w_early": [("cols", len(COLS)), ("ctxT", B * L), ("WqT", C), ("Wk", C), ("Wv", C), ("router", 3 * NEXP)],
    "w_hidden": [("gate_w1", 3 * C), ("e_w1", 3 * NEXP * RH)],
    "w_out": [("e_w2T", NEXP * RH), ("out_w", C), ("gate_w2", C)],
    "w_attn": [("ada", 6 * C), ("wq", C), ("wk", C), ("wv", C), ("self_o", C), ("q_w", C), ("kv_k", C),
               ("kv_v", C), ("cross_o", C)],
    "w_mlp": [("w1", MC * C), ("w2", MC * C)],
}


def spans(pack):
    at, found = 0, {}
    for name, n in PACKS[pack]:
        found[name] = (at, at + n)
        at += n
    return found, at


def mixed_expert_attention_kernel(nc, d_x, d_w, d_rows, d_router_b, d_ident, d_ident16, d_pad, d_out):
    F32, BF16 = mybir.dt.float32, mybir.dt.bfloat16
    ALU, ACT, AX = mybir.AluOpType, mybir.ActivationFunctionType, mybir.AxisListType.X

    with ExitStack() as ctx:
        def sb(name, shape, dt=F32):
            return ctx.enter_context(nc.sbuf_tensor(name, shape, dt))

        def sem(name):
            return ctx.enter_context(nc.semaphore(name))

        x_sb = sb("x_sb", [P, B, NT, C])
        w_tiles = {n: sb(n, [P, spans(n)[1]]) for n in PACKS if n != "w_hidden"}
        rows = sb("rows", [P, len(ROWS), C])
        router_b = sb("router_b", [P, NEXP])
        ident = sb("ident", [P, P])
        ident16 = sb("ident16", [P, P], BF16)

        region = sb("region", [P, UNITS * HG * T])
        at = [0]

        def carve(n):
            at[0] += n
            assert at[0] <= UNITS * HG * T
            return region[:, at[0] - n:at[0]]

        w_hidden = carve(spans("w_hidden")[1])
        hidden = carve(HC * T).rearrange("p (c n) -> p c n", c=HC)
        evT = [carve(T) for _ in range(B)]
        attn0 = [carve(NT * LP).rearrange("p (t l) -> p t l", t=NT) for _ in range(B)]
        probs = region[:, :].rearrange("p (u j n) -> p u j n", u=UNITS, j=HG)

        def w(pack, name):
            a, z = spans(pack)[0][name]
            return w_hidden[:, a:z] if pack == "w_hidden" else w_tiles[pack][:, a:z]

        def col(name):
            return w("w_early", "cols")[:, COLS.index(name):COLS.index(name) + 1]

        def row(name):
            return rows[:, ROWS.index(name), :]

        ctxT = w("w_early", "ctxT")
        router_w = w("w_early", "router").rearrange("p (k e) -> p k e", k=3)
        gate_w1 = w("w_hidden", "gate_w1").rearrange("p (k m) -> p k m", k=3)
        e_w1 = w("w_hidden", "e_w1").rearrange("p (e k r) -> p e k r", e=NEXP, k=3)
        mlp_w1 = w("w_mlp", "w1").rearrange("p (c m) -> p c m", c=MC)
        mlp_w2 = w("w_mlp", "w2").rearrange("p (c m) -> p c m", c=MC)
        ada_w = w("w_attn", "ada").rearrange("p (k m) -> p k m", k=6)
        ADA_COLS, ADA_ROWS = (0, 1, 3, 4), (2, 5)

        def hidden_w(c, k):
            if c == HC - 1:
                return gate_w1[:, k, :]
            return e_w1[:, c // 2, k, (c % 2) * P:(c % 2 + 1) * P]

        kT0 = sb("kT0", [P, B * L])
        score_w = sb("score_w", [P, B, L + NEXP])
        v0 = sb("v0", [LP, B, C])
        cond_bc = sb("cond_bc", [P, B, P])
        hidden_b = sb("hidden_b", [P, HC, B])
        router_bc = sb("router_bc", [P, B, NEXP])
        e_b2_bc = sb("e_b2_bc", [P, NEXP, P])
        e_out_b = sb("e_out_b", [P, NEXP, C])
        e_out_w = sb("e_out_w", [P, NEXP * RH // P, C])
        silu_cond = sb("silu_cond", [P, B])
        silu_bc = sb("silu_bc", [P, B, P])
        ada_cols = sb("ada_cols", [P, 4, B])
        gates = sb("gates", [P, B, 2, C])
        v_b_bc = sb("v_b_bc", [P, 2, P])
        o_bias = sb("o_bias", [P, 2, C])
        self_o = sb("self_o", [P, B, C])
        self_ob = sb("self_ob", [P, B, C])
        mlp_w2g = sb("mlp_w2g", [P, B, MC, C])
        mlp_b2g = sb("mlp_b2g", [P, B, C])

        stats = sb("stats", [P, B, NT, 6])
        mean_var = sb("mean_var", [P, B, NT, 2])
        var_eps = sb("var_eps", [P, B, NT])
        rstd = sb("rstd", [P, B, NT])
        minus_half = sb("minus_half", [P, NT])
        normed = [sb(f"normed{b}", [P, NT, C]) for b in range(B)]
        nT = [sb(f"nT{b}", [P, T]) for b in range(B)]
        red0 = sb("red0", [P, B, 3, NT])
        router_x = sb("router_x", [P, B, NT, NEXP])
        route = sb("route", [P, B, NT, NEXP])
        attn0T = sb("attn0T", [LP, T])
        gate = sb("gate", [P, NT, C])
        routed = sb("routed", [P, NT, C])
        pool_tmp = sb("pool_tmp", [P, NT, C])
        x_bias = sb("x_bias", [P, B, NT, C])
        qf = sb("qf", [P, T])
        kf = sb("kf", [P, T])
        q_rest = sb("q_rest", [P, T])
        k_rest = sb("k_rest", [P, T])
        q_parts = sb("q_parts", [P, NPART, T], BF16)
        k_parts = sb("k_parts", [P, NPART, T], BF16)
        kcf = sb("kcf", [P, B * L])
        kc_rest = sb("kc_rest", [P, B * L])
        kc_parts = sb("kc_parts", [P, NPART, B * L], BF16)
        Qs = [sb(f"Qs{b}", [KS, NH, T], BF16) for b in range(B)]
        k_room = [sb(f"k_room{b}", [P, NH * T], BF16) for b in range(B)]
        Ks = [k[0:KS, :].rearrange("p (h n) -> p h n", h=NH) for k in k_room]
        Kc = sb("Kc", [KS, NH, B, LP], BF16)
        mlp_h = [k[:, :].bitcast(F32)[:, 0:MC * T].rearrange("p (c n) -> p c n", c=MC) for k in k_room]
        V = [sb(f"V{b}", [P, NT, VW]) for b in range(B)]
        Vc = [sb(f"Vc{b}", [LP, VW]) for b in range(B)]
        neg_max = sb("neg_max", [P, B, NT, NH])
        max_rest = sb("max_rest", [P, NT, NH])
        max_parts = sb("max_parts", [P, NT, NPART * NH], BF16)
        max_rows = sb("max_rows", [NPART * NH, 2, T], BF16)
        pv_sb = sb("pv_sb", [P, T])
        inv_sum = sb("inv_sum", [P, NT, HG])
        heads = [sb(f"heads{b}", [P, NT, C]) for b in range(B)]
        headsT = sb("headsT", [P, T])

        q_scr = nc.dram_tensor("q_scr", (2 * B, NPART, P, T), BF16, kind="Internal").ap()
        k_scr = nc.dram_tensor("k_scr", (B, NPART, P, T), BF16, kind="Internal").ap()
        kc_scr = nc.dram_tensor("kc_scr", (NPART, P, B * L), BF16, kind="Internal").ap()

        ps = ctx.enter_context(nc.psum_tensor("ps", [P, 8, T], F32))
        MAX0, EXP0, PVB, MISC = 0, 2, 6, 7

        early_in, x_in, const_in, hidden_in, out_in, rows_in, attn_in, mlp_in, pad_in = (
            sem(n) for n in ("early_in", "x_in", "const_in", "hidden_in", "out_in", "rows_in", "attn_in", "mlp_in",
                             "pad_in"))
        x1_in = sem("x1_in")
        vec_own, pool_own = sem("vec_own"), sem("pool_own")
        zeroed, con_raw, con_sb, con_bc, silu_done, folded = (
            sem(n) for n in ("zeroed", "con_raw", "con_sb", "con_bc", "silu_done", "folded"))
        var_ready, rstd_ready, normed_ready, nT_raw, nT_ready = (
            sem(n) for n in ("var_ready", "rstd_ready", "normed_ready", "nT_raw", "nT_ready"))
        s0_raw, s0_sub, s0_exp, s0_norm, s0T_raw, s0T_ready = (
            sem(n) for n in ("s0_raw", "s0_sub", "s0_exp", "s0_norm", "s0T_raw", "s0T_ready"))
        ev_raw, ev_ready, rt_raw, rt_read, rt_sub, rt_exp, rt_ready = (
            sem(n) for n in ("ev_raw", "ev_ready", "rt_raw", "rt_read", "rt_sub", "rt_exp", "rt_ready"))
        hid_raw, hid_ready, g2_raw, g2_sum, g2_tanh, e2_raw, e2_read, e_bias, x1_ready = (
            sem(n) for n in ("hid_raw", "hid_ready", "g2_raw", "g2_sum", "g2_tanh", "e2_raw", "e2_read", "e_bias",
                             "x1_ready"))
        q_raw, k_raw, v_raw, qf_ready, kf_ready, v_ready, q_hi, k_hi, q_split, k_split, kc_split = (
            sem(n) for n in ("q_raw", "k_raw", "v_raw", "qf_ready", "kf_ready", "v_ready", "q_hi", "k_hi",
                             "q_split", "k_split", "kc_split"))
        q_out, k_out, kc_out, kc_in, q_zero = (sem(n) for n in ("q_out", "k_out", "kc_out", "kc_in", "q_zero"))
        stack_in = [sem(f"stack_in{i}") for i in range(2 * B)]
        max_raw, max_read, max_split, mT_raw, mT_ready = (
            sem(n) for n in ("max_raw", "max_read", "max_split", "mT_raw", "mT_ready"))
        m_in = [sem("m_in0"), sem("m_in1")]
        exp_raw, exp_ready, pv_raw, pv_ready, pvT_raw, heads_ready = (
            sem(n) for n in ("exp_raw", "exp_ready", "pv_raw", "pv_ready", "pvT_raw", "heads_ready"))
        hT_raw, hT_ready, o_raw, x_ready, xb_ready = (
            sem(n) for n in ("hT_raw", "hT_ready", "o_raw", "x_ready", "xb_ready"))
        m1_raw, m1_ready, m2_raw, y_ready, out_done = (
            sem(n) for n in ("m1_raw", "m1_ready", "m2_raw", "y_ready", "out_done"))

        CON = ["kT0", "score_w", "v0", "hidden_b", "e_out_b", "e_out_w0", "e_out_w1", "ada", "gates", "o_bias",
               "kTc", "Vc"]
        BC = ["cond_bc", "e_b2_bc", "v_b_bc", "silu_bc"]

        def made(name):
            return CON.index(name) + 1

        def spread(name):
            return BC.index(name) + 1

        SELF_G = B * NG
        SELF_S = SELF_G * NT
        SELF_MAX = B * NH * NT

        def tile(s):
            if s < SELF_S:
                return False, s // (NG * NT), s // NT % NG, s % NT, s // NT
            c = s - SELF_S
            return True, c // NG, c % NG, 0, SELF_G + c

        def last_tile(group):
            return NT * group + NT - 1 if group < SELF_G else SELF_S + group - SELF_G

        LN_ORDER = [(k, b) for k in range(4) for b in range(B)]

        block = ctx.enter_context(nc.Block())

        @block.sync
        def _(sp):
            sp.dma_start(w_tiles["w_early"][:, :], d_w["w_early"]).then_inc(early_in, 16)
            sp.dma_start(x_sb[:, 0, :, :], d_x[0].rearrange("(p t) c -> p t c", t=NT)).then_inc(x_in, 16)
            sp.dma_start(x_sb[:, 1, :, :], d_x[1].rearrange("(p t) c -> p t c", t=NT)).then_inc(x1_in, 16)
            sp.dma_start(ident[:, :], d_ident).then_inc(const_in, 16)
            sp.dma_start(ident16[:, :], d_ident16).then_inc(const_in, 16)
            sp.dma_start(router_b[:, :], d_router_b.partition_broadcast(P)).then_inc(const_in, 16)
            sp.dma_start(w_hidden, d_w["w_hidden"]).then_inc(hidden_in, 16)
            sp.dma_start(w_tiles["w_out"][:, :], d_w["w_out"]).then_inc(out_in, 16)
            sp.dma_start(rows[:, :, :], d_rows.partition_broadcast(P)).then_inc(rows_in, 16)
            sp.dma_start(w_tiles["w_attn"][:, :], d_w["w_attn"]).then_inc(attn_in, 16)
            sp.dma_start(w_tiles["w_mlp"][:, :], d_w["w_mlp"]).then_inc(mlp_in, 16)
            sp.wait_ge(zeroed, 1)
            sp.dma_start(Kc[MROW:KS, :, :, 0:L].rearrange("p h b n -> p (h b) n"),
                         d_pad[0][:, 0:L].unsqueeze(1).to_broadcast([KS - MROW, NH * B, L])).then_inc(pad_in, 16)
            for b in range(B):
                sp.dma_start(Ks[b][MROW:KS, :, :],
                             d_pad[0].unsqueeze(1).to_broadcast([KS - MROW, NH, T])).then_inc(pad_in, 16)
                sp.dma_start(Qs[b][MROW:KS, :, :],
                             d_pad[1].unsqueeze(1).to_broadcast([KS - MROW, NH, T])).then_inc(pad_in, 16)

            def q_rows(b, n):
                for i in range(NPART):
                    sp.dma_start(Qs[b][NPART * D * i:NPART * D * (i + 1), :, :].rearrange("p h n -> p (h n)"),
                                 q_scr[n, i].rearrange("(d h) n -> d (h n)", d=D).unsqueeze(0)
                                 .to_broadcast([NPART, D, NH * T])).then_inc(stack_in[n], 16)

            def restack_self(b):
                sp.wait_ge(q_split, b + 1)
                sp.dma_start(q_scr[b].rearrange("i p n -> p i n"), q_parts[:, :, :]).then_inc(q_out, 16)
                sp.wait_ge(k_split, b + 1)
                sp.dma_start(k_scr[b].rearrange("i p n -> p i n"), k_parts[:, :, :]).then_inc(k_out, 16)
                sp.wait_ge(q_out, 16 * (b + 1))
                q_rows(b, b)
                sp.wait_ge(k_out, 16 * (b + 1))
                for i in range(NPART):
                    sp.dma_start(Ks[b][NPART * D * i:NPART * D * (i + 1), :, :].rearrange("p h n -> p (h n)"),
                                 k_scr[b].rearrange("j (d h) n -> (j d) (h n)", d=D)).then_inc(stack_in[b], 16)

            def maximum_rows(n):
                b, h0, nh = (n // NG, n % NG * HG, HG) if n < SELF_G else (n - SELF_G, 0, NH)
                sp.wait_ge(mT_ready, n + 1)
                sp.dma_start(Qs[b][MROW:MROW + NPART, h0:h0 + nh, :],
                             max_rows[0:NPART * nh, n % 2, :]).then_inc(m_in[n % 2], 16)

            def restack_cross(b):
                sp.wait_ge(q_split, B + b + 1)
                sp.dma_start(q_scr[B + b].rearrange("i p n -> p i n"), q_parts[:, :, :]).then_inc(q_out, 16)
                sp.wait_ge(exp_raw, 2 * NT * NG * (b + 1))
                sp.dma_start(Qs[b][MROW:MROW + NPART, :, :],
                             d_pad[1][0:NPART].unsqueeze(1).to_broadcast([NPART, NH, T])).then_inc(q_zero, 16)
                sp.wait_ge(q_out, 16 * (B + b + 1))
                q_rows(b, B + b)

            sp.wait_ge(kc_split, 1)
            sp.dma_start(kc_scr.rearrange("i p n -> p i n"), kc_parts[:, :, :]).then_inc(kc_out, 16)
            sp.wait_ge(kc_out, 16)
            for i in range(NPART):
                sp.dma_start(Kc[NPART * D * i:NPART * D * (i + 1), :, :, 0:L].rearrange("p h b n -> p (h b) n"),
                             kc_scr.rearrange("j (d h) (b n) -> (j d) (h b) n", d=D, b=B)).then_inc(kc_in, 16)
            restack_self(0)
            restack_self(1)
            for n in range(NG + 2):
                maximum_rows(n)
            restack_cross(0)
            for n in range(NG + 2, SELF_G + 1):
                maximum_rows(n)
            restack_cross(1)
            for b in range(B):
                if b == B - 1:
                    maximum_rows(SELF_G + 1)
                sp.wait_ge(y_ready, b + 1)
                sp.dma_start(d_out[b].rearrange("(p t) c -> p t c", t=NT), x_sb[:, b, :, :]).then_inc(out_done, 16)
            sp.wait_ge(out_done, 16 * B)

        @block.gpsimd
        def _(pool):
            count = [0]

            def own(ins):
                count[0] += 1
                ins.then_inc(pool_own, 1)
                pool.wait_ge(pool_own, count[0])

            def tell(ins, signal, n):
                ins.then_inc(signal, 1)
                pool.wait_ge(signal, n)

            def over_tiles(v):
                return v.unsqueeze(1).to_broadcast([P, NT, C])

            own(nc.gpsimd.memset(minus_half[:, :], -0.5))
            own(nc.gpsimd.memset(v0[64:LP, :, :], 0.0))
            for b in range(B):
                own(nc.gpsimd.memset(attn0[b][:, :, L:LP], 0.0))
                own(nc.gpsimd.memset(V[b][:, :, :], 1.0))
                own(nc.gpsimd.memset(Vc[b][64:LP, :], 0.0))
                own(nc.gpsimd.memset(Vc[b][64:L, :], 1.0))
                own(nc.gpsimd.memset(Vc[b][0:64, :], 1.0))
            tell(nc.gpsimd.memset(Kc[:, :, :, :].rearrange("p h b n -> p (h b n)").bitcast(F32), 0.0), zeroed, 1)

            def inverse_deviation(n):
                _, b = LN_ORDER[n]
                pool.wait_ge(var_ready, n + 1)
                tell(nc.gpsimd.tensor_tensor(rstd[:, b, :], var_eps[:, b, :], minus_half[:, :], ALU.pow),
                     rstd_ready, n + 1)

            def spread_column(dst, name, last=None):
                ins = nc.gpsimd.tensor_copy(dst, name.to_broadcast([P, P]))
                own(ins) if last is None else tell(ins, con_bc, last)

            inverse_deviation(0)
            inverse_deviation(1)
            pool.wait_ge(early_in, 16)
            spread_column(cond_bc[:, 0, :], col("cond0"))
            spread_column(cond_bc[:, 1, :], col("cond1"), spread("cond_bc"))
            for e in range(NEXP):
                spread_column(e_b2_bc[:, e, :], col(f"e_b2_{e}"), spread("e_b2_bc") if e == NEXP - 1 else None)
            spread_column(v_b_bc[:, 0, :], col("qkv_v"))
            spread_column(v_b_bc[:, 1, :], col("kv_v"), spread("v_b_bc"))

            def expert_bias(b):
                pool.wait_ge(con_sb, made("e_out_b"))
                pool.wait_ge(rt_ready, b + 1)
                for e in range(NEXP):
                    dst = x_bias[:, b, :, :] if e == 0 else pool_tmp[:, :, :]
                    own(nc.gpsimd.tensor_tensor(dst, over_tiles(e_out_b[:, e, :]),
                                                route[:, b, :, e:e + 1].to_broadcast([P, NT, C]), ALU.mult))
                    if e:
                        ins = nc.gpsimd.tensor_tensor(x_bias[:, b, :, :], x_bias[:, b, :, :], pool_tmp[:, :, :],
                                                      ALU.add)
                        own(ins) if e < NEXP - 1 else tell(ins, e_bias, b + 1)

            expert_bias(0)
            pool.wait_ge(silu_done, 1)
            spread_column(silu_bc[:, 0, :], silu_cond[:, 0:1])
            spread_column(silu_bc[:, 1, :], silu_cond[:, 1:2], spread("silu_bc"))
            expert_bias(1)

            def fold_gates(b):
                pool.wait_ge(con_sb, made("o_bias"))
                pool.wait_ge(mlp_in, 16)
                own(nc.gpsimd.tensor_tensor(self_o[:, b, :], w("w_attn", "self_o"), gates[:, b, 0, :], ALU.mult))
                own(nc.gpsimd.tensor_tensor(self_ob[:, b, :], o_bias[:, 0, :], gates[:, b, 0, :], ALU.mult))
                own(nc.gpsimd.tensor_tensor(mlp_w2g[:, b, :, :], mlp_w2,
                                            gates[:, b, 1, :].unsqueeze(1).to_broadcast([P, MC, C]), ALU.mult))
                tell(nc.gpsimd.tensor_tensor(mlp_b2g[:, b, :], row("mlp_b2"), gates[:, b, 1, :], ALU.mult),
                     folded, b + 1)

            def split_k(b):
                pool.wait_ge(kf_ready, b + 1)
                pool.wait_ge(k_hi, b + 1)
                own(nc.gpsimd.tensor_tensor(k_rest[:, :], kf[:, :], k_parts[:, 0, :], ALU.subtract))
                own(nc.gpsimd.tensor_tensor(k_parts[:, 1, :], kf[:, :], k_parts[:, 0, :], ALU.subtract))
                tell(nc.gpsimd.tensor_tensor(k_parts[:, 2, :], k_rest[:, :], k_parts[:, 1, :], ALU.subtract),
                     k_split, b + 1)

            def add_bias(n):
                stage, b = divmod(n, B)
                if stage == 0:
                    pool.wait_ge(x1_ready, b + 1)
                else:
                    pool.wait_ge(x_ready, n - B + 1)
                bias = (self_ob[:, b, :], o_bias[:, 1, :], mlp_b2g[:, b, :])[stage]
                tell(nc.gpsimd.tensor_tensor(x_bias[:, b, :, :], x_sb[:, b, :, :], over_tiles(bias), ALU.add),
                     xb_ready, n + 1)

            inverse_deviation(2)
            split_k(0)
            fold_gates(0)
            fold_gates(1)
            inverse_deviation(3)
            split_k(1)
            add_bias(0)
            add_bias(1)
            inverse_deviation(4)
            add_bias(2)
            inverse_deviation(5)
            add_bias(3)
            inverse_deviation(6)
            add_bias(4)
            inverse_deviation(7)
            add_bias(5)

        @block.scalar
        def _(act):
            def norm_affine(n):
                k, b = LN_ORDER[n]
                act.wait_ge(nT_raw, n + 1)
                if k == 0:
                    act.wait_ge(early_in, 16)
                if k == 1:
                    act.wait_ge(con_sb, made("ada"))
                scale, bias = {
                    0: (col("ln_gamma"), col("ln_beta")),
                    1: (ada_cols[:, 1, b:b + 1], ada_cols[:, 0, b:b + 1]),
                    2: (col("norm2_g"), col("norm2_b")),
                    3: (ada_cols[:, 3, b:b + 1], ada_cols[:, 2, b:b + 1]),
                }[k]
                nc.scalar.activation(nT[b][:, :], ps[:, MISC, :], ACT.Identity, scale=scale,
                                     bias=bias).then_inc(nT_ready, 1)

            norm_affine(0)
            norm_affine(1)
            for b in range(B):
                act.wait_ge(s0_sub, b + 1)
                nc.scalar.activation(attn0[b][:, :, 0:L], attn0[b][:, :, 0:L], ACT.Exp,
                                     scale=float(C) ** -0.5).then_inc(s0_exp, 1)
            for b in range(B):
                act.wait_ge(ev_raw, b + 1)
                nc.scalar.activation(evT[b], ps[:, PVB, :], ACT.Copy).then_inc(ev_ready, 1)
                act.wait_ge(rt_sub, b + 1)
                nc.scalar.activation(route[:, b, :, :], route[:, b, :, :], ACT.Exp).then_inc(rt_exp, 1)
            nc.scalar.activation(silu_cond[:, :], w("w_early", "cols")[:, 0:B], ACT.Silu).then_inc(silu_done, 1)

            def hidden_layer(b):
                act.wait_ge(con_sb, made("hidden_b"))
                if b:
                    act.wait_ge(e2_raw, NT * b)
                for c in range(HC):
                    act.wait_ge(hid_raw, HC * b + c + 1)
                    nc.scalar.activation(hidden[:, c, :], ps[:, EXP0 + c % 4, :], ACT.Silu,
                                         bias=hidden_b[:, c, b:b + 1]).then_inc(hid_ready, 1)

            def gate_tanh(b):
                act.wait_ge(g2_sum, b + 1)
                nc.scalar.activation(gate[:, :, :], gate[:, :, :], ACT.Tanh, scale=0.5).then_inc(g2_tanh, 1)

            def high_part_q(n):
                act.wait_ge(qf_ready, n + 1)
                if n:
                    act.wait_ge(q_out, 16 * n)
                nc.scalar.activation(q_parts[:, 0, :], qf[:, :], ACT.Copy).then_inc(q_hi, 1)

            def attention_inputs(b):
                norm_affine(2 + b)
                high_part_q(b)
                act.wait_ge(kf_ready, b + 1)
                if b:
                    act.wait_ge(k_out, 16 * b)
                nc.scalar.activation(k_parts[:, 0, :], kf[:, :], ACT.Copy).then_inc(k_hi, 1)
                act.wait_ge(v_raw, b + 1)
                act.wait_ge(zeroed, 1)
                nc.scalar.activation(
                    V[b][:, :, 0:NH * VS].rearrange("p t (h s) -> p t h s", s=VS)[:, :, :, 0:D],
                    ps[:, MAX0 + 1, :].rearrange("p (t h d) -> p t h d", t=NT, d=D), ACT.Copy).then_inc(v_ready, 1)

            hidden_layer(0)
            gate_tanh(0)
            hidden_layer(1)
            attention_inputs(0)
            gate_tanh(1)
            attention_inputs(1)

            def maximum_row_copy(n):
                nr = NPART * (HG if n < SELF_G else NH)
                act.wait_ge(mT_raw, n + 1)
                if n >= 2:
                    act.wait_ge(m_in[n % 2], 16 * (n // 2))
                nc.scalar.activation(max_rows[0:nr, n % 2, :], ps[0:nr, MISC, :].bitcast(BF16)[:, 0:T],
                                     ACT.Copy).then_inc(mT_ready, 1)

            def exps(s):
                cross = tile(s)[0]
                rows_ = LP if cross else P
                if s >= UNITS:
                    act.wait_ge(pv_raw, s - UNITS + 1)
                for pr in range(2):
                    e = 2 * s + pr
                    act.wait_ge(exp_raw, e + 1)
                    bank = EXP0 + 2 * (e % 2)
                    nc.scalar.activation(probs[0:rows_, s % UNITS, 2 * pr:2 * pr + 2, :],
                                         ps[0:rows_, bank:bank + 2, :], ACT.Exp,
                                         scale=float(D) ** -0.5).then_inc(exp_ready, 1)

            def keep_heads(group):
                act.wait_ge(pv_raw, last_tile(group) + 1)
                if group:
                    act.wait_ge(pvT_raw, group)
                nc.scalar.activation(pv_sb[:, :], ps[:, PVB, :], ACT.Copy).then_inc(pv_ready, 1)

            def keep_headsT(n):
                act.wait_ge(hT_raw, n + 1)
                if n:
                    act.wait_ge(o_raw, n)
                nc.scalar.activation(headsT[:, :], ps[:, MISC, :], ACT.Copy).then_inc(hT_ready, 1)

            def gelu(b):
                for c in range(MC):
                    act.wait_ge(m1_raw, MC * b + c + 1)
                    nc.scalar.activation(mlp_h[b][:, c, :], ps[:, EXP0 + c, :], ACT.Gelu_apprx_tanh,
                                         bias=col(f"mlp_b1_{c}")).then_inc(m1_ready, 1)

            maximum_row_copy(0)
            maximum_row_copy(1)
            act.wait_ge(e2_raw, NT * B)
            for s in range(SELF_S):
                group, kt = divmod(s, NT)
                exps(s)
                if kt == 0 and group:
                    keep_heads(group - 1)
                if kt == 1 and 2 <= group + 1 < SELF_G:
                    maximum_row_copy(group + 1)
                if s == NG * NT + 2:
                    keep_headsT(0)
                if s == NG * NT + 4:
                    norm_affine(4)
                if s == NG * NT + 5:
                    high_part_q(2)
            maximum_row_copy(SELF_G)
            keep_heads(SELF_G - 1)
            exps(SELF_S)
            exps(SELF_S + 1)
            keep_heads(SELF_G)
            keep_headsT(1)
            exps(SELF_S + 2)
            keep_heads(SELF_G + 1)
            norm_affine(5)
            exps(SELF_S + 3)
            keep_heads(SELF_G + 2)
            high_part_q(3)
            keep_heads(SELF_G + 3)
            keep_headsT(2)
            norm_affine(6)
            gelu(0)
            maximum_row_copy(SELF_G + 1)
            for g in range(NG):
                exps(SELF_S + NG + g)
                if g:
                    keep_heads(SELF_G + NG + g - 1)
            keep_heads(SELF_G + 2 * NG - 1)
            keep_headsT(3)
            norm_affine(7)
            gelu(1)

        @block.vector
        def _(dve):
            count = [0]

            def own(ins):
                count[0] += 1
                ins.then_inc(vec_own, 1)
                dve.wait_ge(vec_own, count[0])

            def tell(ins, signal, n):
                ins.then_inc(signal, 1)
                dve.wait_ge(signal, n)

            def layer_norm(n):
                k, b = LN_ORDER[n]
                if k == 0:
                    dve.wait_ge((x_in, x1_in)[b], 16)
                for t in range(NT):
                    last = nc.vector.bn_stats(stats[:, b, t, :], x_sb[:, b, t, :])
                own(last)
                for t in range(NT):
                    last = nc.vector.bn_aggr(mean_var[:, b, t, :], stats[:, b, t, :])
                own(last)
                tell(nc.vector.tensor_scalar(var_eps[:, b, :], mean_var[:, b, :, 1], LN_EPS[k], None, ALU.add),
                     var_ready, n + 1)
                dve.wait_ge(rstd_ready, n + 1)
                for t in range(NT):
                    last = nc.vector.tensor_scalar(normed[b][:, t, :], x_sb[:, b, t, :], mean_var[:, b, t, 0:1],
                                                   rstd[:, b, t:t + 1], ALU.subtract, ALU.mult)
                tell(last, normed_ready, n + 1)

            def keep(name, *steps):
                dve.wait_ge(con_raw, made(name))
                for step in steps[:-1]:
                    own(step())
                tell(steps[-1](), con_sb, made(name))

            def grid(bank, a, n, p=P):
                return ps[0:p, bank, 0:a * n].rearrange("p (a n) -> p a n", a=a)

            layer_norm(0)
            layer_norm(1)
            keep("kT0", lambda: nc.vector.tensor_copy(kT0[:, :], ps[:, 2, 0:B * L]))
            keep("score_w",
                 lambda: nc.vector.tensor_copy(score_w[:, :, L:L + NEXP],
                                               router_w[:, 0:1, :].to_broadcast([P, B, NEXP])),
                 lambda: nc.vector.tensor_copy(score_w[:, :, 0:L], grid(3, B, L)))
            dve.wait_ge(zeroed, 1)
            keep("v0", lambda: nc.vector.tensor_copy(v0[0:L, :, :], grid(4, B, C, L)))

            def first_softmax(b):
                dve.wait_ge(s0_raw, b + 1)
                scores = ps[:, MISC, :].rearrange("p (t n) -> p t n", t=NT)
                own(nc.vector.tensor_reduce(red0[:, b, 0, :], scores[:, :, 0:L], axis=AX, op=ALU.max, negate=True))
                own(nc.vector.tensor_copy(router_x[:, b, :, :], scores[:, :, L:L + NEXP]))
                tell(nc.vector.tensor_tensor(attn0[b][:, :, 0:L], scores[:, :, 0:L],
                                             red0[:, b, 0, :].unsqueeze(2).to_broadcast([P, NT, L]), ALU.add),
                     s0_sub, b + 1)

            def first_softmax_norm(b):
                dve.wait_ge(s0_exp, b + 1)
                own(nc.vector.tensor_reduce(red0[:, b, 1, :], attn0[b][:, :, 0:L], axis=AX, op=ALU.add))
                own(nc.vector.reciprocal(red0[:, b, 2, :], red0[:, b, 1, :]))
                tell(nc.vector.tensor_tensor(attn0[b][:, :, 0:L], attn0[b][:, :, 0:L],
                                             red0[:, b, 2, :].unsqueeze(2).to_broadcast([P, NT, L]), ALU.mult),
                     s0_norm, b + 1)

            for b in range(B):
                first_softmax(b)
            for b in range(B):
                first_softmax_norm(b)

            dve.wait_ge(const_in, 48)
            keep("hidden_b",
                 lambda: nc.vector.tensor_tensor(
                     hidden_b[:, :, :], grid(2, HC, B),
                     w("w_early", "cols")[:, COLS.index("e_b1_0"):COLS.index("e_b1_0") + HC].unsqueeze(2)
                     .to_broadcast([P, HC, B]), ALU.add),
                 lambda: nc.vector.tensor_tensor(
                     router_bc[:, :, :], ps[:, 2, 16:16 + B * NEXP].rearrange("p (b e) -> p b e", b=B),
                     router_b[:, :].unsqueeze(1).to_broadcast([P, B, NEXP]), ALU.add))

            def evidence_router(b):
                dve.wait_ge(s0T_raw, b + 1)
                if b:
                    dve.wait_ge(ev_raw, b)
                tell(nc.vector.tensor_copy(attn0T[:, :], ps[0:LP, MISC, :]), s0T_ready, b + 1)
                dve.wait_ge(rt_raw, b + 1)
                r = route[:, b, :, :]
                tell(nc.vector.tensor_tensor(r, ps[:, MISC, 0:4 * NT].rearrange("p (t n) -> p t n", n=4)[:, :, 0:NEXP],
                                             router_x[:, b, :, :], ALU.add), rt_read, b + 1)
                own(nc.vector.tensor_tensor(r, r, router_bc[:, b, :].unsqueeze(1).to_broadcast([P, NT, NEXP]),
                                            ALU.add))
                own(nc.vector.tensor_reduce(red0[:, b, 0, :], r, axis=AX, op=ALU.max, negate=True))
                tell(nc.vector.tensor_tensor(r, r, red0[:, b, 0, :].unsqueeze(2).to_broadcast([P, NT, NEXP]),
                                             ALU.add), rt_sub, b + 1)
                dve.wait_ge(rt_exp, b + 1)
                own(nc.vector.tensor_reduce(red0[:, b, 1, :], r, axis=AX, op=ALU.add))
                own(nc.vector.reciprocal(red0[:, b, 2, :], red0[:, b, 1, :]))
                tell(nc.vector.tensor_tensor(r, r, red0[:, b, 2, :].unsqueeze(2).to_broadcast([P, NT, NEXP]),
                                             ALU.mult), rt_ready, b + 1)

            evidence_router(0)
            evidence_router(1)
            dve.wait_ge(rows_in, 16)
            keep("e_out_b", lambda: nc.vector.tensor_tensor(
                e_out_b[:, :, :], grid(3, NEXP, C), row("out_b").unsqueeze(1).to_broadcast([P, NEXP, C]), ALU.add))
            keep("e_out_w0", lambda: nc.vector.tensor_copy(e_out_w[:, 0:4, :], grid(4, 4, C)))
            keep("e_out_w1", lambda: nc.vector.tensor_copy(e_out_w[:, 4:6, :], grid(5, 2, C)))
            shift0 = COLS.index("shift_msa")
            keep("ada",
                 lambda: nc.vector.tensor_tensor(
                     ada_cols[:, :, :], grid(0, 4, B),
                     w("w_early", "cols")[:, shift0:shift0 + 4].unsqueeze(2).to_broadcast([P, 4, B]), ALU.add),
                 lambda: nc.vector.tensor_scalar(ada_cols[:, 1:4:2, :], ada_cols[:, 1:4:2, :], 1.0, None, ALU.add))
            gate0, o0 = ROWS.index("gate_msa"), ROWS.index("self_o_b")
            keep("gates", *[
                lambda b=b: nc.vector.tensor_tensor(gates[:, b, :, :], grid(1, 2 * B, C)[:, 2 * b:2 * b + 2, :],
                                                    rows[:, gate0:gate0 + 2, :], ALU.add) for b in range(B)])
            keep("o_bias", lambda: nc.vector.tensor_tensor(o_bias[:, :, :], grid(0, 2, C), rows[:, o0:o0 + 2, :],
                                                           ALU.add))
            keep("kTc", lambda: nc.vector.tensor_scalar(kcf[:, :], ps[:, PVB, 0:B * L], col("kv_k"), None, ALU.add))
            keep("Vc", *[
                lambda b=b: nc.vector.tensor_copy(
                    Vc[b][0:L, 0:NH * VS].rearrange("p (h s) -> p h s", s=VS)[:, :, 0:D],
                    ps[0:L, 1, b * C:(b + 1) * C].rearrange("p (h d) -> p h d", d=D)) for b in range(B)])
            own(nc.vector.tensor_copy(kc_parts[:, 0, :], kcf[:, :]))
            own(nc.vector.tensor_tensor(kc_rest[:, :], kcf[:, :], kc_parts[:, 0, :], ALU.subtract))
            own(nc.vector.tensor_copy(kc_parts[:, 1, :], kc_rest[:, :]))
            tell(nc.vector.tensor_tensor(kc_parts[:, 2, :], kc_rest[:, :], kc_parts[:, 1, :], ALU.subtract),
                 kc_split, 1)

            def expert_sum(b):
                dve.wait_ge(g2_raw, b + 1)
                tell(nc.vector.tensor_tensor(gate[:, :, :], grid(PVB, NT, C),
                                             row("gate_b2").unsqueeze(1).to_broadcast([P, NT, C]), ALU.add),
                     g2_sum, b + 1)
                dve.wait_ge(e_bias, b + 1)
                for t in range(NT):
                    n = NT * b + t
                    dve.wait_ge(e2_raw, n + 1)
                    for e in range(NEXP):
                        ins = nc.vector.scalar_tensor_tensor(
                            routed[:, t, :], ps[:, MAX0 + n % 2, e * C:(e + 1) * C], route[:, b, t, e:e + 1],
                            x_bias[:, b, t, :] if e == 0 else routed[:, t, :], op0=ALU.mult, op1=ALU.add)
                        own(ins) if e < NEXP - 1 else tell(ins, e2_read, n + 1)
                dve.wait_ge(g2_tanh, b + 1)
                own(nc.vector.scalar_tensor_tensor(routed[:, :, :], gate[:, :, :], 1.0, routed[:, :, :],
                                                   op0=ALU.add, op1=ALU.mult))
                tell(nc.vector.scalar_tensor_tensor(x_sb[:, b, :, :], routed[:, :, :], 0.5, x_sb[:, b, :, :],
                                                    op0=ALU.mult, op1=ALU.add), x1_ready, b + 1)

            def split_q(n, bank, bias):
                dve.wait_ge(q_raw, n + 1)
                tell(nc.vector.tensor_scalar(qf[:, :], ps[:, bank, :], bias, None, ALU.add), qf_ready, n + 1)

            def split_q_rest(n):
                dve.wait_ge(q_hi, n + 1)
                own(nc.vector.tensor_tensor(q_rest[:, :], qf[:, :], q_parts[:, 0, :], ALU.subtract))
                own(nc.vector.tensor_tensor(q_parts[:, 1, :], qf[:, :], q_parts[:, 0, :], ALU.subtract))
                tell(nc.vector.tensor_tensor(q_parts[:, 2, :], q_rest[:, :], q_parts[:, 1, :], ALU.subtract),
                     q_split, n + 1)

            def attention_inputs(b):
                layer_norm(2 + b)
                split_q(b, PVB, col("qkv_q"))
                dve.wait_ge(k_raw, b + 1)
                if b:
                    dve.wait_ge(k_split, b)
                tell(nc.vector.tensor_scalar(kf[:, :], ps[:, MAX0, :], col("qkv_k"), None, ALU.add),
                     kf_ready, b + 1)
                split_q_rest(b)

            expert_sum(0)
            attention_inputs(0)
            expert_sum(1)
            attention_inputs(1)

            def self_maxima(i):
                b, h, qt = i // (NH * NT), i // NT % NH, i % NT
                dve.wait_ge(max_raw, i + 1)
                nc.vector.tensor_reduce(neg_max[:, b, qt, h:h + 1], ps[:, MAX0 + i % 2, :], axis=AX, op=ALU.max,
                                        negate=True).then_inc(max_read, 1)

            def cross_maxima(j):
                b, h = divmod(j, NH)
                i = SELF_MAX + j
                dve.wait_ge(max_raw, i + 1)
                nc.vector.tensor_reduce(
                    neg_max[:, b, :, h], ps[:, MAX0 + i % 2, :].rearrange("p (t n) -> p t n", t=NT)[:, :, 0:L],
                    axis=AX, op=ALU.max, negate=True).then_inc(max_read, 1)

            def split_maxima(n):
                b, h0, nh = (n // NG, n % NG * HG, HG) if n < SELF_G else (n - SELF_G, 0, NH)
                m = neg_max[:, b, :, h0:h0 + nh]
                rest = max_rest[:, :, 0:nh]
                part = [max_parts[:, :, i * nh:(i + 1) * nh] for i in range(NPART)]
                dve.wait_ge(max_read, NH * (n + 1) if n < SELF_G else SELF_MAX + NH * (n - SELF_G + 1))
                if n:
                    dve.wait_ge(mT_raw, n)
                own(nc.vector.tensor_copy(part[0], m))
                own(nc.vector.tensor_tensor(rest, m, part[0], ALU.subtract))
                own(nc.vector.tensor_copy(part[1], rest))
                tell(nc.vector.tensor_tensor(part[2], rest, part[1], ALU.subtract), max_split, n + 1)

            def normalize_heads(group):
                b, g = (group // NG % B, group % NG)
                dve.wait_ge(pvT_raw, group + 1)
                pv = ps[:, MISC, :].rearrange("p (t j s) -> p t j s", t=NT, j=HG)
                own(nc.vector.reciprocal(inv_sum[:, :, :], pv[:, :, :, D]))
                tell(nc.vector.tensor_tensor(
                    heads[b][:, :, g * HG * D:(g + 1) * HG * D].rearrange("p t (j d) -> p t j d", d=D),
                    pv[:, :, :, 0:D], inv_sum[:, :, :].unsqueeze(3).to_broadcast([P, NT, HG, D]), ALU.mult),
                    heads_ready, group + 1)

            def residual(n):
                b = n % B
                dve.wait_ge(xb_ready, n + 1)
                dve.wait_ge(o_raw, n + 1)
                tell(nc.vector.tensor_tensor(x_sb[:, b, :, :], grid(MISC, NT, C), x_bias[:, b, :, :], ALU.add),
                     x_ready, n + 1)

            def output(b):
                dve.wait_ge(xb_ready, 2 * B + b + 1)
                dve.wait_ge(m2_raw, b + 1)
                tell(nc.vector.tensor_tensor(x_sb[:, b, :, :], grid(MISC, NT, C), x_bias[:, b, :, :], ALU.add),
                     y_ready, b + 1)

            GM = HG * NT
            for group in range(2):
                for i in range(GM * group, GM * (group + 1)):
                    self_maxima(i)
                split_maxima(group)
            for s in range(SELF_S):
                group, kt = divmod(s, NT)
                if group + 2 < SELF_G:
                    for i in range(GM * (group + 2) + HG * kt, GM * (group + 2) + HG * (kt + 1)):
                        self_maxima(i)
                    if kt == NT - 1:
                        split_maxima(group + 2)
                elif s < SELF_S:
                    for j in (2 * (s - SELF_S + 2 * NT), 2 * (s - SELF_S + 2 * NT) + 1):
                        cross_maxima(j)
                    if s == SELF_S - 1:
                        split_maxima(SELF_G)
                if kt == 1 and group:
                    normalize_heads(group - 1)
                if s == NG * NT + 2:
                    residual(0)
                    layer_norm(4)
                if s == NG * NT + 5:
                    split_q(2, MISC, col("q_b"))
                    split_q_rest(2)
            normalize_heads(SELF_G - 1)
            residual(1)
            normalize_heads(SELF_G)
            layer_norm(5)
            normalize_heads(SELF_G + 1)
            normalize_heads(SELF_G + 2)
            split_q(3, MISC, col("q_b"))
            split_q_rest(3)
            normalize_heads(SELF_G + 3)
            residual(2)
            layer_norm(6)
            for j in range(NH, 2 * NH):
                cross_maxima(j)
            split_maxima(SELF_G + 1)
            output(0)
            for g in range(NG):
                normalize_heads(SELF_G + NG + g)
            residual(3)
            layer_norm(7)
            output(1)

        @block.tensor
        def _(pe):
            reader = {}

            def claim(bank):
                if bank in reader:
                    pe.wait_ge(*reader[bank])

            def read_by(bank, signal, n):
                reader[bank] = (signal, n)

            def tiles_of(t):
                return slice(t * P, (t + 1) * P)

            def mm(out, lhsT, rhs, start=True, stop=True):
                return nc.tensor.matmul(out, lhsT, rhs, start=start, stop=stop)

            def product(name, bank, emit):
                claim(bank)
                emit().then_inc(con_raw, 1)
                read_by(bank, con_sb, made(name))

            pe.wait_ge(early_in, 16)
            product("kT0", 2, lambda: mm(ps[:, 2, 0:B * L], w("w_early", "Wk"), ctxT))
            pe.wait_ge(con_sb, made("kT0"))
            product("score_w", 3, lambda: mm(ps[:, 3, 0:B * L], w("w_early", "WqT"), kT0[:, :]))

            def per_sequence(bank, rhs):
                for b in range(B):
                    last = mm(ps[0:L, bank, b * C:(b + 1) * C], ctxT[:, b * L:(b + 1) * L], rhs)
                return last

            product("v0", 4, lambda: per_sequence(4, w("w_early", "Wv")))

            def transpose_normed(n):
                _, b = LN_ORDER[n]
                pe.wait_ge(normed_ready, n + 1)
                claim(MISC)
                for t in range(NT):
                    last = nc.tensor.transpose(ps[:, MISC, tiles_of(t)], normed[b][:, t, :], ident[:, :])
                last.then_inc(nT_raw, 1)
                read_by(MISC, nT_ready, n + 1)

            pe.wait_ge(const_in, 48)
            for b in range(B):
                transpose_normed(b)
                pe.wait_ge(nT_ready, b + 1)
                pe.wait_ge(con_sb, made("score_w"))
                claim(MISC)
                for t in range(NT):
                    last = mm(ps[:, MISC, t * P:t * P + L + NEXP], nT[b][:, tiles_of(t)], score_w[:, b, :])
                last.then_inc(s0_raw, 1)
                read_by(MISC, s0_sub, b + 1)

            def hidden_bias():
                cond = w("w_early", "cols")[:, 0:B]
                for c in range(HC):
                    mm(ps[:, 2, B * c:B * (c + 1)], hidden_w(c, 2), cond)
                for b in range(B):
                    last = mm(ps[:, 2, 16 + NEXP * b:16 + NEXP * (b + 1)], cond_bc[:, b, :], router_w[:, 2, :])
                return last

            pe.wait_ge(hidden_in, 16)
            pe.wait_ge(con_bc, spread("cond_bc"))
            product("hidden_b", 2, hidden_bias)

            for b in range(B):
                pe.wait_ge(s0_norm, b + 1)
                claim(MISC)
                for t in range(NT):
                    last = nc.tensor.transpose(ps[0:LP, MISC, tiles_of(t)], attn0[b][:, t, :], ident[:, :])
                last.then_inc(s0T_raw, 1)
                read_by(MISC, s0T_ready, b + 1)
                pe.wait_ge(con_sb, made("v0"))
                pe.wait_ge(s0T_ready, b + 1)
                claim(PVB)
                mm(ps[:, PVB, :], v0[:, b, :], attn0T[:, :]).then_inc(ev_raw, 1)
                read_by(PVB, ev_ready, b + 1)
                pe.wait_ge(ev_ready, b + 1)
                claim(MISC)
                for t in range(NT):
                    last = mm(ps[:, MISC, 4 * t:4 * t + NEXP], evT[b][:, tiles_of(t)], router_w[:, 1, :])
                last.then_inc(rt_raw, 1)
                read_by(MISC, rt_read, b + 1)

            def chunk_products(bank, n, lhsT, rhs):
                for i in range(n):
                    last = mm(ps[:, bank, i * C:(i + 1) * C], lhsT(i), rhs(i))
                return last

            pe.wait_ge(out_in, 16)
            pe.wait_ge(con_bc, spread("e_b2_bc"))
            product("e_out_b", 3, lambda: chunk_products(3, NEXP, lambda i: e_b2_bc[:, i, :],
                                                         lambda i: w("w_out", "out_w")))
            e_w2T = w("w_out", "e_w2T")
            product("e_out_w0", 4, lambda: chunk_products(4, 4, lambda i: e_w2T[:, tiles_of(i)],
                                                          lambda i: w("w_out", "out_w")))
            product("e_out_w1", 5, lambda: chunk_products(5, 2, lambda i: e_w2T[:, tiles_of(4 + i)],
                                                          lambda i: w("w_out", "out_w")))

            def hidden_layer(b):
                for c in range(HC):
                    bank = EXP0 + c % 4
                    claim(bank)
                    mm(ps[:, bank, :], hidden_w(c, 0), nT[b][:, :], stop=False)
                    mm(ps[:, bank, :], hidden_w(c, 1), evT[b], start=False).then_inc(hid_raw, 1)
                    read_by(bank, hid_ready, HC * b + c + 1)

            def expert_outputs(b):
                pe.wait_ge(hid_ready, HC * (b + 1))
                claim(PVB)
                for t in range(NT):
                    last = mm(ps[:, PVB, tiles_of(t)], hidden[:, HC - 1, tiles_of(t)], w("w_out", "gate_w2"))
                last.then_inc(g2_raw, 1)
                read_by(PVB, g2_sum, b + 1)
                pe.wait_ge(con_sb, made("e_out_w1"))
                for t in range(NT):
                    n = NT * b + t
                    claim(MAX0 + n % 2)
                    for e in range(NEXP):
                        for k in range(2):
                            last = mm(ps[:, MAX0 + n % 2, e * C:(e + 1) * C], hidden[:, 2 * e + k, tiles_of(t)],
                                      e_out_w[:, 2 * e + k, :], start=k == 0, stop=k == 1)
                    last.then_inc(e2_raw, 1)
                    read_by(MAX0 + n % 2, e2_read, n + 1)

            def attention_inputs(b):
                transpose_normed(2 + b)
                pe.wait_ge(nT_ready, 2 + b + 1)
                claim(PVB)
                mm(ps[:, PVB, :], w("w_attn", "wq"), nT[b][:, :]).then_inc(q_raw, 1)
                read_by(PVB, qf_ready, b + 1)
                claim(MAX0)
                mm(ps[:, MAX0, :], w("w_attn", "wk"), nT[b][:, :]).then_inc(k_raw, 1)
                read_by(MAX0, kf_ready, b + 1)
                claim(MAX0 + 1)
                for t in range(NT):
                    last = mm(ps[:, MAX0 + 1, tiles_of(t)], nT[b][:, tiles_of(t)], w("w_attn", "wv"))
                last.then_inc(v_raw, 1)
                read_by(MAX0 + 1, v_ready, b + 1)

            hidden_layer(0)
            pe.wait_ge(attn_in, 16)
            pe.wait_ge(silu_done, 1)

            def ada_columns():
                for j, k in enumerate(ADA_COLS):
                    last = mm(ps[:, 0, B * j:B * (j + 1)], ada_w[:, k, :], silu_cond[:, :])
                return last

            product("ada", 0, ada_columns)
            pe.wait_ge(con_bc, spread("silu_bc"))
            product("gates", 1, lambda: chunk_products(1, 2 * B, lambda i: silu_bc[:, i // 2, :],
                                                       lambda i: ada_w[:, ADA_ROWS[i % 2], :]))
            product("o_bias", 0, lambda: chunk_products(0, 2, lambda i: v_b_bc[:, i, :],
                                                        lambda i: w("w_attn", ("self_o", "cross_o")[i])))
            product("kTc", PVB, lambda: mm(ps[:, PVB, 0:B * L], w("w_attn", "kv_k"), ctxT))
            product("Vc", 1, lambda: per_sequence(1, w("w_attn", "kv_v")))
            expert_outputs(0)
            hidden_layer(1)
            attention_inputs(0)
            expert_outputs(1)
            attention_inputs(1)

            def self_max_scores(i):
                b, h, qt = i // (NH * NT), i // NT % NH, i % NT
                if i % (NH * NT) == 0:
                    pe.wait_ge(stack_in[b], 16 * 2 * NPART)
                claim(MAX0 + i % 2)
                mm(ps[:, MAX0 + i % 2, :], Qs[b][:, h, tiles_of(qt)], Ks[b][:, h, :]).then_inc(max_raw, 1)
                read_by(MAX0 + i % 2, max_read, i + 1)

            def cross_max_scores(j):
                b, h = divmod(j, NH)
                i = SELF_MAX + j
                if h == 0:
                    pe.wait_ge(kc_in, 16 * NPART)
                    pe.wait_ge(q_zero, 16 * (b + 1))
                    pe.wait_ge(stack_in[B + b], 16 * NPART)
                claim(MAX0 + i % 2)
                for t in range(NT):
                    last = mm(ps[:, MAX0 + i % 2, t * P:t * P + L], Qs[b][:, h, tiles_of(t)], Kc[:, h, b, 0:L])
                last.then_inc(max_raw, 1)
                read_by(MAX0 + i % 2, max_read, i + 1)

            def transpose_maxima(n):
                nr = NPART * (HG if n < SELF_G else NH)
                pe.wait_ge(max_split, n + 1)
                claim(MISC)
                for t in range(NT):
                    last = nc.tensor.transpose(ps[0:nr, MISC, :].bitcast(BF16)[:, tiles_of(t)],
                                               max_parts[:, t, 0:nr], ident16[:, :])
                last.then_inc(mT_raw, 1)
                read_by(MISC, mT_ready, n + 1)

            def exp_scores(s, pr):
                cross, b, g, kt, group = tile(s)
                if pr == 0 and kt == 0:
                    n = group if not cross else SELF_G + b
                    pe.wait_ge(m_in[n % 2], 16 * (n // 2 + 1))
                e = 2 * s + pr
                for j in range(2):
                    h = HG * g + 2 * pr + j
                    bank = EXP0 + 2 * (e % 2) + j
                    claim(bank)
                    if cross:
                        last = mm(ps[0:LP, bank, :], Kc[:, h, b, :], Qs[b][:, h, :])
                    else:
                        last = mm(ps[:, bank, :], Ks[b][:, h, tiles_of(kt)], Qs[b][:, h, :])
                    read_by(bank, exp_ready, e + 1)
                last.then_inc(exp_raw, 1)

            def weigh_values(s):
                cross, b, g, kt, group = tile(s)
                pe.wait_ge(exp_ready, 2 * s + 2)
                if kt == 0:
                    if not cross and g == 0:
                        pe.wait_ge(v_ready, b + 1)
                    claim(PVB)
                for j in range(HG):
                    h = HG * g + j
                    if cross:
                        last = mm(ps[32 * j:32 * j + 32, PVB, :], Vc[b][:, VS * h:VS * h + 32],
                                  probs[0:LP, s % UNITS, j, :])
                    else:
                        last = mm(ps[32 * j:32 * j + 32, PVB, :], V[b][:, kt, VS * h:VS * h + 32],
                                  probs[:, s % UNITS, j, :], start=kt == 0, stop=kt == NT - 1)
                last.then_inc(pv_raw, 1)
                read_by(PVB, pv_ready, group + 1)

            def transpose_heads(group):
                pe.wait_ge(pv_ready, group + 1)
                claim(MISC)
                for t in range(NT):
                    last = nc.tensor.transpose(ps[:, MISC, tiles_of(t)], pv_sb[:, tiles_of(t)], ident[:, :])
                last.then_inc(pvT_raw, 1)
                read_by(MISC, heads_ready, group + 1)

            def project_heads(n):
                b = n % B
                pe.wait_ge(heads_ready, NG * (n + 1))
                claim(MISC)
                for t in range(NT):
                    last = nc.tensor.transpose(ps[:, MISC, tiles_of(t)], heads[b][:, t, :], ident[:, :])
                last.then_inc(hT_raw, 1)
                read_by(MISC, hT_ready, n + 1)
                if n < B:
                    pe.wait_ge(folded, b + 1)
                claim(MISC)
                for t in range(NT):
                    last = mm(ps[:, MISC, tiles_of(t)], headsT[:, tiles_of(t)],
                              self_o[:, b, :] if n < B else w("w_attn", "cross_o"))
                last.then_inc(o_raw, 1)
                read_by(MISC, x_ready, n + 1)

            def cross_queries(b):
                pe.wait_ge(nT_ready, 2 * B + b + 1)
                claim(MISC)
                mm(ps[:, MISC, :], w("w_attn", "q_w"), nT[b][:, :]).then_inc(q_raw, 1)
                read_by(MISC, qf_ready, B + b + 1)

            def mlp_up(b):
                pe.wait_ge(nT_ready, 3 * B + b + 1)
                pe.wait_ge(mlp_in, 16)
                for c in range(MC):
                    claim(EXP0 + c)
                    mm(ps[:, EXP0 + c, :], mlp_w1[:, c, :], nT[b][:, :]).then_inc(m1_raw, 1)
                    read_by(EXP0 + c, m1_ready, MC * b + c + 1)

            def mlp_down(b):
                pe.wait_ge(m1_ready, MC * (b + 1))
                claim(MISC)
                for t in range(NT):
                    for c in range(MC):
                        last = mm(ps[:, MISC, tiles_of(t)], mlp_h[b][:, c, tiles_of(t)], mlp_w2g[:, b, c, :],
                                  start=c == 0, stop=c == MC - 1)
                last.then_inc(m2_raw, 1)
                read_by(MISC, y_ready, b + 1)

            GM = HG * NT
            pe.wait_ge(pad_in, 16 * (2 * B + 1))
            for group in range(2):
                for i in range(GM * group, GM * (group + 1)):
                    self_max_scores(i)
                transpose_maxima(group)
            for s in range(SELF_S):
                group, kt = divmod(s, NT)
                for pr in range(2):
                    exp_scores(s, pr)
                    if group + 2 < SELF_G:
                        first = GM * (group + 2) + HG * kt + 2 * pr
                        self_max_scores(first)
                        self_max_scores(first + 1)
                    else:
                        cross_max_scores(2 * (s - SELF_S + 2 * NT) + pr)
                if s:
                    weigh_values(s - 1)
                if kt == 1 and 2 <= group + 1 < SELF_G:
                    transpose_maxima(group + 1)
                if kt == 1 and group:
                    transpose_heads(group - 1)
                if s == NG * NT + 2:
                    project_heads(0)
                if s == NG * NT + 4:
                    transpose_normed(4)
                if s == NG * NT + 5:
                    cross_queries(0)
            weigh_values(SELF_S - 1)
            transpose_maxima(SELF_G)
            transpose_heads(SELF_G - 1)

            def cross_tile(s):
                for pr in range(2):
                    exp_scores(s, pr)

            cross_tile(SELF_S)
            cross_tile(SELF_S + 1)
            weigh_values(SELF_S)
            project_heads(1)
            transpose_heads(SELF_G)
            cross_tile(SELF_S + 2)
            weigh_values(SELF_S + 1)
            transpose_normed(5)
            transpose_heads(SELF_G + 1)
            cross_tile(SELF_S + 3)
            weigh_values(SELF_S + 2)
            transpose_heads(SELF_G + 2)
            cross_queries(1)
            weigh_values(SELF_S + 3)
            transpose_heads(SELF_G + 3)
            project_heads(2)
            transpose_normed(6)
            mlp_up(0)
            for j in range(NH, 2 * NH):
                cross_max_scores(j)
            transpose_maxima(SELF_G + 1)
            mlp_down(0)
            for g in range(NG):
                cross_tile(SELF_S + NG + g)
                if g:
                    weigh_values(SELF_S + NG + g - 1)
                    transpose_heads(SELF_G + NG + g - 1)
            weigh_values(SELF_S + 2 * NG - 1)
            transpose_heads(SELF_G + 2 * NG - 1)
            project_heads(3)
            transpose_normed(7)
            mlp_up(1)
            mlp_down(1)


def kernel(**inputs):
    import numpy as np
    import ml_dtypes
    import concourse.bacc as bacc
    from concourse.bass_utils import run_bass_kernel_spmd

    a = {k: np.asarray(v) for k, v in inputs.items()}
    l0 = {k[len("L0_xcond_"):]: v for k, v in a.items() if k.startswith("L0_xcond_")}
    l1 = {k[len("L1_xcond_"):]: v for k, v in a.items() if k.startswith("L1_xcond_")}

    def by_dim(v):
        return v.reshape(v.shape[:-1] + (NH, D)).swapaxes(-1, -2).reshape(v.shape)

    def rows_first(v, k):
        return v.reshape(k, P, -1).transpose(1, 0, 2).reshape(P, -1)

    qkv_b = l1["qkv_b"].reshape(3, C)
    kv_b = l1["kv_b"].reshape(2, C)
    ada_b = l1["ada_b"].reshape(6, C)
    e_b1 = l0["e_b1"].reshape(HC - 1, P)
    mlp_b1 = l1["mlp_b1"].reshape(MC, P)
    columns = {
        "cond0": a["cond_1024"][0], "cond1": a["cond_1024"][1], "ln_gamma": l0["ln_gamma"],
        "ln_beta": l0["ln_beta"], "gate_b1": l0["gate_b1"], "shift_msa": ada_b[0], "scale_msa": ada_b[1],
        "shift_mlp": ada_b[3], "scale_mlp": ada_b[4], "qkv_q": by_dim(qkv_b[0]), "qkv_k": by_dim(qkv_b[1]),
        "qkv_v": qkv_b[2], "norm2_g": l1["norm2_g"], "norm2_b": l1["norm2_b"], "q_b": by_dim(l1["q_b"]),
        "kv_k": by_dim(kv_b[0]), "kv_v": kv_b[1],
        **{f"e_b1_{i}": e_b1[i] for i in range(HC - 1)}, **{f"mlp_b1_{i}": mlp_b1[i] for i in range(MC)},
        **{f"e_b2_{i}": l0["e_b2"][i] for i in range(NEXP)},
    }
    free_rows = {
        "gate_b2": l0["gate_b2"], "out_b": l0["out_b"], "gate_msa": ada_b[2], "gate_mlp": ada_b[5],
        "self_o_b": l1["self_o_b"], "cross_o_b": l1["cross_o_b"], "mlp_b2": l1["mlp_b2"],
    }
    qkv_w, kv_w = l1["qkv_w"], l1["kv_w"]
    parts = {
        "cols": np.stack([columns[n] for n in COLS], axis=1),
        "ctxT": a["ctx_1024"].transpose(2, 0, 1).reshape(C, B * L),
        "WqT": l0["Wq"].T, "Wk": l0["Wk"], "Wv": l0["Wv"], "router": rows_first(l0["router_W"], 3),
        "gate_w1": rows_first(l0["gate_w1"], 3),
        "e_w1": l0["e_w1"].reshape(NEXP, 3, P, RH).transpose(2, 0, 1, 3).reshape(P, -1),
        "e_w2T": l0["e_w2"].transpose(2, 0, 1).reshape(C, NEXP * RH), "out_w": l0["out_w"],
        "gate_w2": l0["gate_w2"], "ada": l1["ada_w"],
        "wq": by_dim(qkv_w[:, 0:C]), "wk": by_dim(qkv_w[:, C:2 * C]), "wv": qkv_w[:, 2 * C:3 * C],
        "self_o": l1["self_o_w"], "q_w": by_dim(l1["q_w"]), "kv_k": by_dim(kv_w[:, 0:C]),
        "kv_v": kv_w[:, C:2 * C], "cross_o": l1["cross_o_w"], "w1": l1["mlp_w1"],
        "w2": rows_first(l1["mlp_w2"], MC),
    }
    pad = np.zeros((2, KS - MROW, T), ml_dtypes.bfloat16)
    pad[0, 0:NPART] = 1
    arrays = {"x": a["x"], "rows": np.concatenate([free_rows[n] for n in ROWS]),
              "router_b": l0["router_b"], "ident": np.eye(P, dtype=np.float32),
              "ident16": np.eye(P, dtype=ml_dtypes.bfloat16), "pad": pad}
    for pack, fields in PACKS.items():
        arrays[pack] = np.concatenate([parts[n] for n, _ in fields], axis=1)

    nc = bacc.Bacc("TRN2", target_bir_lowering=False, num_devices=1)
    arrays = {f"in_{n}": np.ascontiguousarray(v) for n, v in arrays.items()}
    d = {n[3:]: nc.dram_tensor(n, v.shape, mybir.dt.from_np(v.dtype), kind="ExternalInput").ap()
         for n, v in arrays.items()}
    out = nc.dram_tensor("out_0", (B, T, C), mybir.dt.float32, kind="ExternalOutput").ap()
    mixed_expert_attention_kernel(nc, d["x"], {n: d[n] for n in PACKS},
                                  d["rows"].rearrange("(r c) -> r c", c=C), d["router_b"], d["ident"],
                                  d["ident16"], d["pad"], out)
    result = run_bass_kernel_spmd(nc, [arrays], core_ids=[0])
    return result.results[0]["out_0"]
```

```python
import concourse.bass as bass
from concourse import mybir
from contextlib import ExitStack

B, T, C, L = 2, 512, 128, 77
P = 128
NT = T // P
NEXP = 3
RH = 2 * C
HC = NEXP * RH // P + 1
NH = 16
D = C // NH
HG = 4
NG = NH // HG
MC = 4 * C // P
VS = D + 1
VW = NH * VS + 32 - VS
NPART = 3
MROW = NPART * NPART * D
KS = 96
LP = 96
LN_EPS = (1e-5, 1e-6, 1e-6, 1e-6)
UNITS = 4

COLS = ["cond0", "cond1", "ln_gamma", "ln_beta", "e_b1_0", "e_b1_1", "e_b1_2", "e_b1_3", "e_b1_4", "e_b1_5",
        "gate_b1", "shift_msa", "scale_msa", "shift_mlp", "scale_mlp", "qkv_q", "qkv_k", "qkv_v", "norm2_g",
        "norm2_b", "q_b", "kv_k", "kv_v", "mlp_b1_0", "mlp_b1_1", "mlp_b1_2", "mlp_b1_3", "e_b2_0", "e_b2_1",
        "e_b2_2"]
ROWS = ["gate_b2", "out_b", "gate_msa", "gate_mlp", "self_o_b", "cross_o_b", "mlp_b2"]
PACKS = {
    "w_early": [("cols", len(COLS)), ("ctxT", B * L), ("WqT", C), ("Wk", C), ("Wv", C), ("router", 3 * NEXP)],
    "w_hidden": [("gate_w1", 3 * C), ("e_w1", 3 * NEXP * RH)],
    "w_out": [("e_w2T", NEXP * RH), ("out_w", C), ("gate_w2", C)],
    "w_attn": [("ada", 6 * C), ("wq", C), ("wk", C), ("wv", C), ("self_o", C), ("q_w", C), ("kv_k", C),
               ("kv_v", C), ("cross_o", C)],
    "w_mlp": [("w1", MC * C), ("w2", MC * C)],
}


def spans(pack):
    at, found = 0, {}
    for name, n in PACKS[pack]:
        found[name] = (at, at + n)
        at += n
    return found, at


def mixed_expert_attention_kernel(nc, d_x, d_w, d_rows, d_router_b, d_ident, d_ident16, d_pad, d_out):
    F32, BF16 = mybir.dt.float32, mybir.dt.bfloat16
    ALU, ACT, AX = mybir.AluOpType, mybir.ActivationFunctionType, mybir.AxisListType.X

    with ExitStack() as ctx:
        def sb(name, shape, dt=F32):
            return ctx.enter_context(nc.sbuf_tensor(name, shape, dt))

        def sem(name):
            return ctx.enter_context(nc.semaphore(name))

        x_sb = sb("x_sb", [P, B, NT, C])
        w_tiles = {n: sb(n, [P, spans(n)[1]]) for n in PACKS if n != "w_hidden"}
        rows = sb("rows", [P, len(ROWS), C])
        router_b = sb("router_b", [P, NEXP])
        ident = sb("ident", [P, P])
        ident16 = sb("ident16", [P, P], BF16)

        region = sb("region", [P, UNITS * HG * T])
        at = [0]

        def carve(n):
            at[0] += n
            assert at[0] <= UNITS * HG * T
            return region[:, at[0] - n:at[0]]

        w_hidden = carve(spans("w_hidden")[1])
        hidden = carve(HC * T).rearrange("p (c n) -> p c n", c=HC)
        evT = [carve(T) for _ in range(B)]
        attn0 = [carve(NT * LP).rearrange("p (t l) -> p t l", t=NT) for _ in range(B)]
        probs = region[:, :].rearrange("p (u j n) -> p u j n", u=UNITS, j=HG)

        def w(pack, name):
            a, z = spans(pack)[0][name]
            return w_hidden[:, a:z] if pack == "w_hidden" else w_tiles[pack][:, a:z]

        def col(name):
            return w("w_early", "cols")[:, COLS.index(name):COLS.index(name) + 1]

        def row(name):
            return rows[:, ROWS.index(name), :]

        ctxT = w("w_early", "ctxT")
        router_w = w("w_early", "router").rearrange("p (k e) -> p k e", k=3)
        gate_w1 = w("w_hidden", "gate_w1").rearrange("p (k m) -> p k m", k=3)
        e_w1 = w("w_hidden", "e_w1").rearrange("p (e k r) -> p e k r", e=NEXP, k=3)
        mlp_w1 = w("w_mlp", "w1").rearrange("p (c m) -> p c m", c=MC)
        mlp_w2 = w("w_mlp", "w2").rearrange("p (c m) -> p c m", c=MC)
        ada_w = w("w_attn", "ada").rearrange("p (k m) -> p k m", k=6)
        ADA_COLS, ADA_ROWS = (0, 1, 3, 4), (2, 5)

        def hidden_w(c, k):
            if c == HC - 1:
                return gate_w1[:, k, :]
            return e_w1[:, c // 2, k, (c % 2) * P:(c % 2 + 1) * P]

        kT0 = sb("kT0", [P, B * L])
        score_w = sb("score_w", [P, B, L + NEXP])
        v0 = sb("v0", [LP, B, C])
        hidden_b = sb("hidden_b", [P, HC, B])
        router_bc = sb("router_bc", [P, B, NEXP])
        e_out_b = sb("e_out_b", [P, NEXP, C])
        e_out_w = sb("e_out_w", [P, NEXP * RH // P, C])
        silu_cond = sb("silu_cond", [P, B])
        ada_cols = sb("ada_cols", [P, 4, B])
        gates = sb("gates", [P, B, 2, C])
        o_bias = sb("o_bias", [P, 2, C])
        self_o = sb("self_o", [P, B, C])
        self_ob = sb("self_ob", [P, B, C])
        mlp_w2g = sb("mlp_w2g", [P, B, MC, C])
        mlp_b2g = sb("mlp_b2g", [P, B, C])

        stats = sb("stats", [P, B, NT, 6])
        mean_var = sb("mean_var", [P, B, NT, 2])
        var_eps = sb("var_eps", [P, B, NT])
        rstd = sb("rstd", [P, B, NT])
        minus_half = sb("minus_half", [P, NT])
        normed = [sb(f"normed{b}", [P, NT, C]) for b in range(B)]
        nT = [sb(f"nT{b}", [P, T]) for b in range(B)]
        red0 = sb("red0", [P, B, 3, NT])
        router_x = sb("router_x", [P, B, NT, NEXP])
        route = sb("route", [P, B, NT, NEXP])
        attn0T = [sb(f"attn0T{b}", [LP, T]) for b in range(B)]
        gate = sb("gate", [P, NT, C])
        routed = sb("routed", [P, NT, C])
        pool_tmp = sb("pool_tmp", [P, NT, C])
        x_bias = sb("x_bias", [P, B, NT, C])
        qf = sb("qf", [P, T])
        kf = sb("kf", [P, T])
        q_rest = sb("q_rest", [P, T])
        k_rest = sb("k_rest", [P, T])
        q_parts = sb("q_parts", [P, NPART, T], BF16)
        k_parts = sb("k_parts", [P, NPART, T], BF16)
        kcf = sb("kcf", [P, B * L])
        kc_rest = sb("kc_rest", [P, B * L])
        kc_parts = sb("kc_parts", [P, NPART, B * L], BF16)
        Qs = [sb(f"Qs{b}", [KS, NH, T], BF16) for b in range(B)]
        k_room = [sb(f"k_room{b}", [P, NH * T], BF16) for b in range(B)]
        Ks = [k[0:KS, :].rearrange("p (h n) -> p h n", h=NH) for k in k_room]
        Kc = sb("Kc", [KS, NH, B, LP], BF16)
        mlp_h = [k[:, :].bitcast(F32)[:, 0:MC * T].rearrange("p (c n) -> p c n", c=MC) for k in k_room]
        V = [sb(f"V{b}", [P, NT, VW]) for b in range(B)]
        Vc = [sb(f"Vc{b}", [LP, VW]) for b in range(B)]
        neg_max = sb("neg_max", [P, B, NT, NH])
        max_rest = sb("max_rest", [P, NT, NH])
        max_parts = sb("max_parts", [P, NT, NPART * NH], BF16)
        max_rows = sb("max_rows", [NPART * NH, 2, T], BF16)
        pv_sb = sb("pv_sb", [P, T])
        inv_sum = sb("inv_sum", [P, NT, HG])
        heads = [sb(f"heads{b}", [P, NT, C]) for b in range(B)]
        headsT = sb("headsT", [P, T])

        q_scr = nc.dram_tensor("q_scr", (2 * B, NPART, P, T), BF16, kind="Internal").ap()
        k_scr = nc.dram_tensor("k_scr", (B, NPART, P, T), BF16, kind="Internal").ap()
        kc_scr = nc.dram_tensor("kc_scr", (NPART, P, B * L), BF16, kind="Internal").ap()

        ps = ctx.enter_context(nc.psum_tensor("ps", [P, 8, T], F32))
        MAX0, EXP0, PVB, MISC = 0, 2, 6, 7

        early_in, x_in, const_in, hidden_in, out_in, rows_in, attn_in, mlp_in, pad_in = (
            sem(n) for n in ("early_in", "x_in", "const_in", "hidden_in", "out_in", "rows_in", "attn_in", "mlp_in",
                             "pad_in"))
        x1_in = sem("x1_in")
        vec_own, pool_own = sem("vec_own"), sem("pool_own")
        zeroed, ones_set, con_raw, con_sb, silu_done, folded = (
            sem(n) for n in ("zeroed", "ones_set", "con_raw", "con_sb", "silu_done", "folded"))
        var_ready, rstd_ready, normed_ready, nT_raw, nT_ready = (
            sem(n) for n in ("var_ready", "rstd_ready", "normed_ready", "nT_raw", "nT_ready"))
        s0_raw, s0_sub, s0_exp, s0_norm, s0T_raw, s0T_ready = (
            sem(n) for n in ("s0_raw", "s0_sub", "s0_exp", "s0_norm", "s0T_raw", "s0T_ready"))
        ev_raw, ev_ready, rt_raw, rt_read, rt_sub, rt_exp, rt_ready = (
            sem(n) for n in ("ev_raw", "ev_ready", "rt_raw", "rt_read", "rt_sub", "rt_exp", "rt_ready"))
        hid_raw, hid_ready, g2_raw, g2_sum, g2_tanh, e2_raw, e2_read, e_bias, x1_ready = (
            sem(n) for n in ("hid_raw", "hid_ready", "g2_raw", "g2_sum", "g2_tanh", "e2_raw", "e2_read", "e_bias",
                             "x1_ready"))
        q_raw, k_raw, v_raw, qf_ready, kf_ready, v_ready, q_hi, k_hi, q_split, k_split, kc_split = (
            sem(n) for n in ("q_raw", "k_raw", "v_raw", "qf_ready", "kf_ready", "v_ready", "q_hi", "k_hi",
                             "q_split", "k_split", "kc_split"))
        q_out, k_out, kc_out, kc_in, q_zero = (sem(n) for n in ("q_out", "k_out", "kc_out", "kc_in", "q_zero"))
        stack_in = [sem(f"stack_in{i}") for i in range(2 * B)]
        max_raw, max_read, max_split, mT_raw, mT_ready = (
            sem(n) for n in ("max_raw", "max_read", "max_split", "mT_raw", "mT_ready"))
        m_in = [sem("m_in0"), sem("m_in1")]
        exp_raw, exp_ready, pv_raw, pv_ready, pvT_raw, heads_ready = (
            sem(n) for n in ("exp_raw", "exp_ready", "pv_raw", "pv_ready", "pvT_raw", "heads_ready"))
        hT_raw, hT_ready, o_raw, x_ready, xb_ready = (
            sem(n) for n in ("hT_raw", "hT_ready", "o_raw", "x_ready", "xb_ready"))
        m1_raw, m1_ready, m2_raw, y_ready, out_done = (
            sem(n) for n in ("m1_raw", "m1_ready", "m2_raw", "y_ready", "out_done"))

        CON = ["kT0", "score_w", "v0", "hidden_b", "e_out_b", "e_out_w0", "e_out_w1", "ada", "gates", "o_bias",
               "kTc", "Vc"]
        def made(name):
            return CON.index(name) + 1

        def con_bank(name):
            return MAX0 + CON.index(name) % 2

        SIDE = (MISC, PVB)
        OUT_BANK = [[MAX0 + t % 2 for t in range(NT)], [EXP0 + t for t in range(NT)]]
        QKV_BANK = [(PVB, MISC, MAX0), (PVB, MISC, PVB)]

        def spread(column):
            return column.to_broadcast([P, P])

        SELF_G = B * NG
        SELF_S = SELF_G * NT
        SELF_MAX = B * NH * NT

        LEAD = 2
        LAG = 2
        CLOSE = NG * NT + 3
        CROSS_MAX = dict(zip(range(SELF_S - 6, SELF_S), (2, 2, 3, 3, 3, 3)))

        def cross_heads(s):
            first = sum(n for at, n in CROSS_MAX.items() if at < s)
            return list(range(first, first + CROSS_MAX.get(s, 0)))

        def tile(s):
            if s < SELF_S:
                return False, s // (NG * NT), s // NT % NG, s % NT, s // NT
            c = s - SELF_S
            return True, c // NG, c % NG, 0, SELF_G + c

        def last_tile(group):
            return NT * group + NT - 1 if group < SELF_G else SELF_S + group - SELF_G

        LN_ORDER = [(k, b) for k in range(4) for b in range(B)]

        block = ctx.enter_context(nc.Block())

        @block.sync
        def _(sp):
            sp.dma_start(w_tiles["w_early"][:, :], d_w["w_early"]).then_inc(early_in, 16)
            sp.dma_start(x_sb[:, 0, :, :], d_x[0].rearrange("(p t) c -> p t c", t=NT)).then_inc(x_in, 16)
            sp.dma_start(x_sb[:, 1, :, :], d_x[1].rearrange("(p t) c -> p t c", t=NT)).then_inc(x1_in, 16)
            sp.dma_start(ident[:, :], d_ident).then_inc(const_in, 16)
            sp.dma_start(ident16[:, :], d_ident16).then_inc(const_in, 16)
            sp.dma_start(router_b[:, :], d_router_b.partition_broadcast(P)).then_inc(const_in, 16)
            sp.dma_start(w_hidden, d_w["w_hidden"]).then_inc(hidden_in, 16)
            sp.dma_start(w_tiles["w_out"][:, :], d_w["w_out"]).then_inc(out_in, 16)
            sp.dma_start(rows[:, :, :], d_rows.partition_broadcast(P)).then_inc(rows_in, 16)
            sp.dma_start(w_tiles["w_attn"][:, :], d_w["w_attn"]).then_inc(attn_in, 16)
            sp.dma_start(w_tiles["w_mlp"][:, :], d_w["w_mlp"]).then_inc(mlp_in, 16)
            sp.wait_ge(zeroed, 1)
            sp.dma_start(Kc[MROW:KS, :, :, 0:L].rearrange("p h b n -> p (h b) n"),
                         d_pad[0][:, 0:L].unsqueeze(1).to_broadcast([KS - MROW, NH * B, L])).then_inc(pad_in, 16)
            for b in range(B):
                sp.dma_start(Ks[b][MROW:KS, :, :],
                             d_pad[0].unsqueeze(1).to_broadcast([KS - MROW, NH, T])).then_inc(pad_in, 16)
                sp.dma_start(Qs[b][MROW:KS, :, :],
                             d_pad[1].unsqueeze(1).to_broadcast([KS - MROW, NH, T])).then_inc(pad_in, 16)

            def q_rows(b, n):
                for i in range(NPART):
                    sp.dma_start(Qs[b][NPART * D * i:NPART * D * (i + 1), :, :].rearrange("p h n -> p (h n)"),
                                 q_scr[n, i].rearrange("(d h) n -> d (h n)", d=D).unsqueeze(0)
                                 .to_broadcast([NPART, D, NH * T])).then_inc(stack_in[n], 16)

            def restack_self(b):
                sp.wait_ge(q_split, b + 1)
                sp.dma_start(q_scr[b].rearrange("i p n -> p i n"), q_parts[:, :, :]).then_inc(q_out, 16)
                sp.wait_ge(k_split, b + 1)
                sp.dma_start(k_scr[b].rearrange("i p n -> p i n"), k_parts[:, :, :]).then_inc(k_out, 16)
                sp.wait_ge(q_out, 16 * (b + 1))
                q_rows(b, b)
                sp.wait_ge(k_out, 16 * (b + 1))
                for i in range(NPART):
                    sp.dma_start(Ks[b][NPART * D * i:NPART * D * (i + 1), :, :].rearrange("p h n -> p (h n)"),
                                 k_scr[b].rearrange("j (d h) n -> (j d) (h n)", d=D)).then_inc(stack_in[b], 16)

            def maximum_rows(n):
                b, h0, nh = (n // NG, n % NG * HG, HG) if n < SELF_G else (n - SELF_G, 0, NH)
                sp.wait_ge(mT_ready, n + 1)
                sp.dma_start(Qs[b][MROW:MROW + NPART, h0:h0 + nh, :],
                             max_rows[0:NPART * nh, n % 2, :]).then_inc(m_in[n % 2], 16)

            def restack_cross(b):
                sp.wait_ge(q_split, B + b + 1)
                sp.dma_start(q_scr[B + b].rearrange("i p n -> p i n"), q_parts[:, :, :]).then_inc(q_out, 16)
                sp.wait_ge(exp_raw, 2 * NT * NG * (b + 1))
                sp.dma_start(Qs[b][MROW:MROW + NPART, :, :],
                             d_pad[1][0:NPART].unsqueeze(1).to_broadcast([NPART, NH, T])).then_inc(q_zero, 16)
                sp.wait_ge(q_out, 16 * (B + b + 1))
                q_rows(b, B + b)

            sp.wait_ge(kc_split, 1)
            sp.dma_start(kc_scr.rearrange("i p n -> p i n"), kc_parts[:, :, :]).then_inc(kc_out, 16)
            sp.wait_ge(kc_out, 16)
            for i in range(NPART):
                sp.dma_start(Kc[NPART * D * i:NPART * D * (i + 1), :, :, 0:L].rearrange("p h b n -> p (h b) n"),
                             kc_scr.rearrange("j (d h) (b n) -> (j d) (h b) n", d=D, b=B)).then_inc(kc_in, 16)
            restack_self(0)
            restack_self(1)
            for n in range(NG + 2):
                maximum_rows(n)
            restack_cross(0)
            for n in range(NG + 2, SELF_G + 1):
                maximum_rows(n)
            restack_cross(1)
            for b in range(B):
                if b == B - 1:
                    maximum_rows(SELF_G + 1)
                sp.wait_ge(y_ready, b + 1)
                sp.dma_start(d_out[b].rearrange("(p t) c -> p t c", t=NT), x_sb[:, b, :, :]).then_inc(out_done, 16)
            sp.wait_ge(out_done, 16 * B)

        @block.gpsimd
        def _(pool):
            count = [0]

            def own(ins):
                count[0] += 1
                ins.then_inc(pool_own, 1)
                pool.wait_ge(pool_own, count[0])

            def tell(ins, signal, n):
                ins.then_inc(signal, 1)
                pool.wait_ge(signal, n)

            def over_tiles(v):
                return v.unsqueeze(1).to_broadcast([P, NT, C])

            def inverse_deviation(n):
                _, b = LN_ORDER[n]
                pool.wait_ge(var_ready, n + 1)
                tell(nc.gpsimd.tensor_tensor(rstd[:, b, :], var_eps[:, b, :], minus_half[:, :], ALU.pow),
                     rstd_ready, n + 1)

            own(nc.gpsimd.memset(minus_half[:, :], -0.5))
            inverse_deviation(0)
            inverse_deviation(1)
            tell(nc.gpsimd.memset(Kc[:, :, :, :].rearrange("p h b n -> p (h b n)").bitcast(F32), 0.0), zeroed, 1)

            def expert_bias(b):
                pool.wait_ge(con_sb, made("e_out_b"))
                pool.wait_ge(rt_ready, b + 1)
                for e in range(NEXP):
                    dst = x_bias[:, b, :, :] if e == 0 else pool_tmp[:, :, :]
                    own(nc.gpsimd.tensor_tensor(dst, over_tiles(e_out_b[:, e, :]),
                                                route[:, b, :, e:e + 1].to_broadcast([P, NT, C]), ALU.mult))
                    if e:
                        ins = nc.gpsimd.tensor_tensor(x_bias[:, b, :, :], x_bias[:, b, :, :], pool_tmp[:, :, :],
                                                      ALU.add)
                        own(ins) if e < NEXP - 1 else tell(ins, e_bias, b + 1)

            expert_bias(0)
            expert_bias(1)

            def fold_gates(b):
                pool.wait_ge(con_sb, made("o_bias"))
                pool.wait_ge(mlp_in, 16)
                own(nc.gpsimd.tensor_tensor(self_o[:, b, :], w("w_attn", "self_o"), gates[:, b, 0, :], ALU.mult))
                own(nc.gpsimd.tensor_tensor(self_ob[:, b, :], o_bias[:, 0, :], gates[:, b, 0, :], ALU.mult))
                own(nc.gpsimd.tensor_tensor(mlp_w2g[:, b, :, :], mlp_w2,
                                            gates[:, b, 1, :].unsqueeze(1).to_broadcast([P, MC, C]), ALU.mult))
                tell(nc.gpsimd.tensor_tensor(mlp_b2g[:, b, :], row("mlp_b2"), gates[:, b, 1, :], ALU.mult),
                     folded, b + 1)

            def split_k(b):
                pool.wait_ge(kf_ready, b + 1)
                pool.wait_ge(k_hi, b + 1)
                own(nc.gpsimd.tensor_tensor(k_rest[:, :], kf[:, :], k_parts[:, 0, :], ALU.subtract))
                own(nc.gpsimd.tensor_tensor(k_parts[:, 1, :], kf[:, :], k_parts[:, 0, :], ALU.subtract))
                tell(nc.gpsimd.tensor_tensor(k_parts[:, 2, :], k_rest[:, :], k_parts[:, 1, :], ALU.subtract),
                     k_split, b + 1)

            def add_bias(n):
                stage, b = divmod(n, B)
                if stage == 0:
                    pool.wait_ge(x1_ready, b + 1)
                else:
                    pool.wait_ge(x_ready, n - B + 1)
                bias = (self_ob[:, b, :], o_bias[:, 1, :], mlp_b2g[:, b, :])[stage]
                tell(nc.gpsimd.tensor_tensor(x_bias[:, b, :, :], x_sb[:, b, :, :], over_tiles(bias), ALU.add),
                     xb_ready, n + 1)

            inverse_deviation(2)
            split_k(0)
            fold_gates(0)
            fold_gates(1)
            inverse_deviation(3)
            split_k(1)
            add_bias(0)
            add_bias(1)
            inverse_deviation(4)
            add_bias(2)
            inverse_deviation(5)
            add_bias(3)
            inverse_deviation(6)
            add_bias(4)
            inverse_deviation(7)
            add_bias(5)

        @block.scalar
        def _(act):
            def norm_affine(n):
                k, b = LN_ORDER[n]
                act.wait_ge(nT_raw, n + 1)
                if k == 0:
                    act.wait_ge(early_in, 16)
                if k == 1:
                    act.wait_ge(con_sb, made("ada"))
                scale, bias = {
                    0: (col("ln_gamma"), col("ln_beta")),
                    1: (ada_cols[:, 1, b:b + 1], ada_cols[:, 0, b:b + 1]),
                    2: (col("norm2_g"), col("norm2_b")),
                    3: (ada_cols[:, 3, b:b + 1], ada_cols[:, 2, b:b + 1]),
                }[k]
                bank = SIDE[b] if k == 0 else MISC
                nc.scalar.activation(nT[b][:, :], ps[:, bank, :], ACT.Identity, scale=scale,
                                     bias=bias).then_inc(nT_ready, 1)

            norm_affine(0)
            norm_affine(1)
            for b in range(B):
                act.wait_ge(s0_sub, b + 1)
                nc.scalar.activation(attn0[b][:, :, 0:L], attn0[b][:, :, 0:L], ACT.Exp,
                                     scale=float(C) ** -0.5).then_inc(s0_exp, 1)
            for b in range(B):
                act.wait_ge(ev_raw, b + 1)
                nc.scalar.activation(evT[b], ps[:, SIDE[b], :], ACT.Copy).then_inc(ev_ready, 1)
            for b in range(B):
                act.wait_ge(rt_sub, b + 1)
                nc.scalar.activation(route[:, b, :, :], route[:, b, :, :], ACT.Exp).then_inc(rt_exp, 1)
            nc.scalar.activation(silu_cond[:, :], w("w_early", "cols")[:, 0:B], ACT.Silu).then_inc(silu_done, 1)

            def hidden_layer(b, chunks):
                act.wait_ge(con_sb, made("hidden_b"))
                if b:
                    act.wait_ge(e2_raw, NT * b)
                for c in chunks:
                    act.wait_ge(hid_raw, HC * b + c + 1)
                    nc.scalar.activation(hidden[:, c, :], ps[:, EXP0 + c % 4, :], ACT.Silu,
                                         bias=hidden_b[:, c, b:b + 1]).then_inc(hid_ready, 1)

            def gate_tanh(b):
                act.wait_ge(g2_sum, b + 1)
                nc.scalar.activation(gate[:, :, :], gate[:, :, :], ACT.Tanh, scale=0.5).then_inc(g2_tanh, 1)

            def high_part_q(n):
                act.wait_ge(qf_ready, n + 1)
                if n:
                    act.wait_ge(q_out, 16 * n)
                nc.scalar.activation(q_parts[:, 0, :], qf[:, :], ACT.Copy).then_inc(q_hi, 1)

            def attention_inputs(b):
                high_part_q(b)
                act.wait_ge(kf_ready, b + 1)
                if b:
                    act.wait_ge(k_out, 16 * b)
                nc.scalar.activation(k_parts[:, 0, :], kf[:, :], ACT.Copy).then_inc(k_hi, 1)
                act.wait_ge(v_raw, b + 1)
                act.wait_ge(ones_set, B)
                nc.scalar.activation(
                    V[b][:, :, 0:NH * VS].rearrange("p t (h s) -> p t h s", s=VS)[:, :, :, 0:D],
                    ps[:, QKV_BANK[b][2], :].rearrange("p (t h d) -> p t h d", t=NT, d=D), ACT.Copy).then_inc(v_ready, 1)

            hidden_layer(0, range(HC))
            gate_tanh(0)
            hidden_layer(1, range(4))
            norm_affine(2)
            hidden_layer(1, range(4, 5))
            attention_inputs(0)
            hidden_layer(1, range(5, HC))
            gate_tanh(1)
            norm_affine(3)
            attention_inputs(1)

            def maximum_row_copy(n):
                nr = NPART * (HG if n < SELF_G else NH)
                act.wait_ge(mT_raw, n + 1)
                if n >= 2:
                    act.wait_ge(m_in[n % 2], 16 * (n // 2))
                nc.scalar.activation(max_rows[0:nr, n % 2, :], ps[0:nr, MISC, :].bitcast(BF16)[:, 0:T],
                                     ACT.Copy).then_inc(mT_ready, 1)

            def exps(s):
                cross = tile(s)[0]
                rows_ = LP if cross else P
                if s >= UNITS:
                    act.wait_ge(pv_raw, s - UNITS + 1)
                for pr in range(2):
                    e = 2 * s + pr
                    act.wait_ge(exp_raw, e + 1)
                    bank = EXP0 + 2 * (e % 2)
                    nc.scalar.activation(probs[0:rows_, s % UNITS, 2 * pr:2 * pr + 2, :],
                                         ps[0:rows_, bank:bank + 2, :], ACT.Exp,
                                         scale=float(D) ** -0.5).then_inc(exp_ready, 1)

            def keep_heads(group):
                act.wait_ge(pv_raw, last_tile(group) + 1)
                if group:
                    act.wait_ge(pvT_raw, group)
                nc.scalar.activation(pv_sb[:, :], ps[:, PVB, :], ACT.Copy).then_inc(pv_ready, 1)

            def keep_headsT(n):
                act.wait_ge(hT_raw, n + 1)
                if n:
                    act.wait_ge(o_raw, n)
                nc.scalar.activation(headsT[:, :], ps[:, MISC, :], ACT.Copy).then_inc(hT_ready, 1)

            def gelu(b):
                for c in range(MC):
                    act.wait_ge(m1_raw, MC * b + c + 1)
                    nc.scalar.activation(mlp_h[b][:, c, :], ps[:, EXP0 + c, :], ACT.Gelu_apprx_tanh,
                                         bias=col(f"mlp_b1_{c}")).then_inc(m1_ready, 1)

            maximum_row_copy(0)
            maximum_row_copy(1)
            act.wait_ge(e2_raw, NT * B)
            for s in range(SELF_S):
                group, kt = divmod(s, NT)
                exps(s)
                if kt == 0 and LEAD <= group + 1 < SELF_G:
                    maximum_row_copy(group + 1)
                if kt == 1 and group:
                    keep_heads(group - 1)
                if s == CLOSE:
                    keep_headsT(0)
                if s == CLOSE + 2:
                    norm_affine(4)
                if s == CLOSE + 3:
                    high_part_q(2)
            maximum_row_copy(SELF_G)
            keep_heads(SELF_G - 1)
            exps(SELF_S)
            exps(SELF_S + 1)
            keep_heads(SELF_G)
            keep_headsT(1)
            exps(SELF_S + 2)
            keep_heads(SELF_G + 1)
            norm_affine(5)
            exps(SELF_S + 3)
            keep_heads(SELF_G + 2)
            high_part_q(3)
            keep_heads(SELF_G + 3)
            keep_headsT(2)
            norm_affine(6)
            gelu(0)
            maximum_row_copy(SELF_G + 1)
            for g in range(NG):
                exps(SELF_S + NG + g)
                if g:
                    keep_heads(SELF_G + NG + g - 1)
            keep_heads(SELF_G + 2 * NG - 1)
            keep_headsT(3)
            norm_affine(7)
            gelu(1)

        @block.vector
        def _(dve):
            count = [0]

            def own(ins):
                count[0] += 1
                ins.then_inc(vec_own, 1)
                dve.wait_ge(vec_own, count[0])

            def tell(ins, signal, n):
                ins.then_inc(signal, 1)
                dve.wait_ge(signal, n)

            def norm_stats(n):
                k, b = LN_ORDER[n]
                if k == 0:
                    dve.wait_ge((x_in, x1_in)[b], 16)
                for t in range(NT):
                    last = nc.vector.bn_stats(stats[:, b, t, :], x_sb[:, b, t, :])
                own(last)
                for t in range(NT):
                    last = nc.vector.bn_aggr(mean_var[:, b, t, :], stats[:, b, t, :])
                own(last)
                nc.vector.tensor_scalar(var_eps[:, b, :], mean_var[:, b, :, 1], LN_EPS[k], None,
                                        ALU.add).then_inc(var_ready, 1)

            def norm_apply(n):
                _, b = LN_ORDER[n]
                dve.wait_ge(rstd_ready, n + 1)
                if n >= B:
                    dve.wait_ge(nT_raw, n - B + 1)
                for t in range(NT):
                    last = nc.vector.tensor_scalar(normed[b][:, t, :], x_sb[:, b, t, :], mean_var[:, b, t, 0:1],
                                                   rstd[:, b, t:t + 1], ALU.subtract, ALU.mult)
                last.then_inc(normed_ready, 1)

            def keep(name, *steps):
                dve.wait_ge(con_raw, made(name))
                for step in steps[:-1]:
                    own(step())
                tell(steps[-1](), con_sb, made(name))

            def grid(bank, a, n, p=P):
                return ps[0:p, bank, 0:a * n].rearrange("p (a n) -> p a n", a=a)

            def bank_of(name, a, n, p=P):
                return grid(con_bank(name), a, n, p)

            for b in range(B):
                own(nc.vector.memset(attn0[b][:, :, L:LP], 0.0))
                own(nc.vector.memset(Vc[b][64:LP, :], 0.0))
                own(nc.vector.memset(Vc[b][64:L, :], 1.0))
                own(nc.vector.memset(Vc[b][0:64, :], 1.0))
            own(nc.vector.memset(v0[64:LP, :, :], 0.0))
            norm_stats(0)
            keep("kT0", lambda: nc.vector.tensor_copy(kT0[:, :], ps[:, con_bank("kT0"), 0:B * L]))
            norm_stats(1)
            keep("score_w",
                 lambda: nc.vector.tensor_copy(score_w[:, :, L:L + NEXP],
                                               router_w[:, 0:1, :].to_broadcast([P, B, NEXP])),
                 lambda: nc.vector.tensor_copy(score_w[:, :, 0:L], bank_of("score_w", B, L)))
            norm_apply(0)
            norm_apply(1)
            keep("v0", lambda: nc.vector.tensor_copy(v0[0:L, :, :], bank_of("v0", B, C, L)))
            for b in range(B):
                nc.vector.memset(V[b][:, :, :], 1.0).then_inc(ones_set, 1)

            def first_softmax(b):
                dve.wait_ge(s0_raw, b + 1)
                scores = ps[:, SIDE[b], :].rearrange("p (t n) -> p t n", t=NT)
                own(nc.vector.tensor_reduce(red0[:, b, 0, :], scores[:, :, 0:L], axis=AX, op=ALU.max, negate=True))
                own(nc.vector.tensor_copy(router_x[:, b, :, :], scores[:, :, L:L + NEXP]))
                tell(nc.vector.tensor_tensor(attn0[b][:, :, 0:L], scores[:, :, 0:L],
                                             red0[:, b, 0, :].unsqueeze(2).to_broadcast([P, NT, L]), ALU.add),
                     s0_sub, b + 1)

            def first_softmax_norm(b):
                dve.wait_ge(s0_exp, b + 1)
                own(nc.vector.tensor_reduce(red0[:, b, 1, :], attn0[b][:, :, 0:L], axis=AX, op=ALU.add))
                own(nc.vector.reciprocal(red0[:, b, 2, :], red0[:, b, 1, :]))
                tell(nc.vector.tensor_tensor(attn0[b][:, :, 0:L], attn0[b][:, :, 0:L],
                                             red0[:, b, 2, :].unsqueeze(2).to_broadcast([P, NT, L]), ALU.mult),
                     s0_norm, b + 1)

            for b in range(B):
                first_softmax(b)
            dve.wait_ge(const_in, 48)
            keep("hidden_b",
                 lambda: nc.vector.tensor_tensor(
                     hidden_b[:, :, :], bank_of("hidden_b", HC, B),
                     w("w_early", "cols")[:, COLS.index("e_b1_0"):COLS.index("e_b1_0") + HC].unsqueeze(2)
                     .to_broadcast([P, HC, B]), ALU.add),
                 lambda: nc.vector.tensor_tensor(
                     router_bc[:, :, :],
                     ps[:, con_bank("hidden_b"), 16:16 + B * NEXP].rearrange("p (b e) -> p b e", b=B),
                     router_b[:, :].unsqueeze(1).to_broadcast([P, B, NEXP]), ALU.add))
            for b in range(B):
                first_softmax_norm(b)

            for b in range(B):
                dve.wait_ge(s0T_raw, b + 1)
                nc.vector.tensor_copy(attn0T[b][:, :], ps[0:LP, SIDE[b], :]).then_inc(s0T_ready, 1)

            dve.wait_ge(rows_in, 16)
            keep("e_out_b", lambda: nc.vector.tensor_tensor(
                e_out_b[:, :, :], bank_of("e_out_b", NEXP, C),
                row("out_b").unsqueeze(1).to_broadcast([P, NEXP, C]), ALU.add))
            keep("e_out_w0", lambda: nc.vector.tensor_copy(e_out_w[:, 0:4, :], bank_of("e_out_w0", 4, C)))
            keep("e_out_w1", lambda: nc.vector.tensor_copy(e_out_w[:, 4:6, :], bank_of("e_out_w1", 2, C)))

            for b in range(B):
                dve.wait_ge(rt_raw, b + 1)
                r = route[:, b, :, :]
                tell(nc.vector.tensor_tensor(
                    r, ps[:, SIDE[b], 0:4 * NT].rearrange("p (t n) -> p t n", n=4)[:, :, 0:NEXP],
                    router_x[:, b, :, :], ALU.add), rt_read, b + 1)
                own(nc.vector.tensor_tensor(r, r, router_bc[:, b, :].unsqueeze(1).to_broadcast([P, NT, NEXP]),
                                            ALU.add))
                own(nc.vector.tensor_reduce(red0[:, b, 0, :], r, axis=AX, op=ALU.max, negate=True))
                tell(nc.vector.tensor_tensor(r, r, red0[:, b, 0, :].unsqueeze(2).to_broadcast([P, NT, NEXP]),
                                             ALU.add), rt_sub, b + 1)
            for b in range(B):
                r = route[:, b, :, :]
                dve.wait_ge(rt_exp, b + 1)
                own(nc.vector.tensor_reduce(red0[:, b, 1, :], r, axis=AX, op=ALU.add))
                own(nc.vector.reciprocal(red0[:, b, 2, :], red0[:, b, 1, :]))
                tell(nc.vector.tensor_tensor(r, r, red0[:, b, 2, :].unsqueeze(2).to_broadcast([P, NT, NEXP]),
                                             ALU.mult), rt_ready, b + 1)

            shift0 = COLS.index("shift_msa")
            keep("ada",
                 lambda: nc.vector.tensor_tensor(
                     ada_cols[:, :, :], bank_of("ada", 4, B),
                     w("w_early", "cols")[:, shift0:shift0 + 4].unsqueeze(2).to_broadcast([P, 4, B]), ALU.add),
                 lambda: nc.vector.tensor_scalar(ada_cols[:, 1:4:2, :], ada_cols[:, 1:4:2, :], 1.0, None, ALU.add))
            gate0, o0 = ROWS.index("gate_msa"), ROWS.index("self_o_b")
            keep("gates", *[
                lambda b=b: nc.vector.tensor_tensor(gates[:, b, :, :], bank_of("gates", 2 * B, C)[:, 2 * b:2 * b + 2, :],
                                                    rows[:, gate0:gate0 + 2, :], ALU.add) for b in range(B)])
            keep("o_bias", lambda: nc.vector.tensor_tensor(o_bias[:, :, :], bank_of("o_bias", 2, C), rows[:, o0:o0 + 2, :],
                                                           ALU.add))
            keep("kTc", lambda: nc.vector.tensor_scalar(kcf[:, :], ps[:, con_bank("kTc"), 0:B * L], col("kv_k"),
                                                        None, ALU.add))
            keep("Vc", *[
                lambda b=b: nc.vector.tensor_copy(
                    Vc[b][0:L, 0:NH * VS].rearrange("p (h s) -> p h s", s=VS)[:, :, 0:D],
                    ps[0:L, con_bank("Vc"), b * C:(b + 1) * C].rearrange("p (h d) -> p h d", d=D)) for b in range(B)])
            own(nc.vector.tensor_copy(kc_parts[:, 0, :], kcf[:, :]))
            own(nc.vector.tensor_tensor(kc_rest[:, :], kcf[:, :], kc_parts[:, 0, :], ALU.subtract))
            own(nc.vector.tensor_copy(kc_parts[:, 1, :], kc_rest[:, :]))
            tell(nc.vector.tensor_tensor(kc_parts[:, 2, :], kc_rest[:, :], kc_parts[:, 1, :], ALU.subtract),
                 kc_split, 1)

            def expert_sum(b):
                dve.wait_ge(g2_raw, b + 1)
                tell(nc.vector.tensor_tensor(gate[:, :, :], grid(PVB, NT, C),
                                             row("gate_b2").unsqueeze(1).to_broadcast([P, NT, C]), ALU.add),
                     g2_sum, b + 1)
                dve.wait_ge(e_bias, b + 1)
                for t in range(NT):
                    n = NT * b + t
                    dve.wait_ge(e2_raw, n + 1)
                    for e in range(NEXP):
                        ins = nc.vector.scalar_tensor_tensor(
                            routed[:, t, :], ps[:, OUT_BANK[b][t], e * C:(e + 1) * C], route[:, b, t, e:e + 1],
                            x_bias[:, b, t, :] if e == 0 else routed[:, t, :], op0=ALU.mult, op1=ALU.add)
                        own(ins) if e < NEXP - 1 else tell(ins, e2_read, n + 1)
                dve.wait_ge(g2_tanh, b + 1)
                own(nc.vector.scalar_tensor_tensor(routed[:, :, :], gate[:, :, :], 1.0, routed[:, :, :],
                                                   op0=ALU.add, op1=ALU.mult))
                tell(nc.vector.scalar_tensor_tensor(x_sb[:, b, :, :], routed[:, :, :], 0.5, x_sb[:, b, :, :],
                                                    op0=ALU.mult, op1=ALU.add), x1_ready, b + 1)

            def split_q(n, bank, bias):
                dve.wait_ge(q_raw, n + 1)
                tell(nc.vector.tensor_scalar(qf[:, :], ps[:, bank, :], bias, None, ALU.add), qf_ready, n + 1)

            def split_q_rest(n):
                dve.wait_ge(q_hi, n + 1)
                own(nc.vector.tensor_tensor(q_rest[:, :], qf[:, :], q_parts[:, 0, :], ALU.subtract))
                own(nc.vector.tensor_tensor(q_parts[:, 1, :], qf[:, :], q_parts[:, 0, :], ALU.subtract))
                tell(nc.vector.tensor_tensor(q_parts[:, 2, :], q_rest[:, :], q_parts[:, 1, :], ALU.subtract),
                     q_split, n + 1)

            def queries_and_keys(b):
                split_q(b, QKV_BANK[b][0], col("qkv_q"))
                dve.wait_ge(k_raw, b + 1)
                if b:
                    dve.wait_ge(k_split, b)
                tell(nc.vector.tensor_scalar(kf[:, :], ps[:, QKV_BANK[b][1], :], col("qkv_k"), None, ALU.add),
                     kf_ready, b + 1)

            expert_sum(0)
            norm_stats(2)
            norm_apply(2)
            queries_and_keys(0)
            split_q_rest(0)
            expert_sum(1)
            norm_stats(3)

            def self_maxima(i):
                b, h, qt = i // (NH * NT), i // NT % NH, i % NT
                dve.wait_ge(max_raw, i + 1)
                nc.vector.tensor_reduce(neg_max[:, b, qt, h:h + 1], ps[:, MAX0 + i % 2, :], axis=AX, op=ALU.max,
                                        negate=True).then_inc(max_read, 1)

            def cross_maxima(j):
                b, h = divmod(j, NH)
                i = SELF_MAX + j
                dve.wait_ge(max_raw, i + 1)
                nc.vector.tensor_reduce(
                    neg_max[:, b, :, h], ps[:, MAX0 + i % 2, :].rearrange("p (t n) -> p t n", t=NT)[:, :, 0:L],
                    axis=AX, op=ALU.max, negate=True).then_inc(max_read, 1)

            def split_maxima(n):
                b, h0, nh = (n // NG, n % NG * HG, HG) if n < SELF_G else (n - SELF_G, 0, NH)
                m = neg_max[:, b, :, h0:h0 + nh]
                rest = max_rest[:, :, 0:nh]
                part = [max_parts[:, :, i * nh:(i + 1) * nh] for i in range(NPART)]
                dve.wait_ge(max_read, NH * (n + 1) if n < SELF_G else SELF_MAX + NH * (n - SELF_G + 1))
                if n:
                    dve.wait_ge(mT_raw, n)
                own(nc.vector.tensor_copy(part[0], m))
                own(nc.vector.tensor_tensor(rest, m, part[0], ALU.subtract))
                own(nc.vector.tensor_copy(part[1], rest))
                tell(nc.vector.tensor_tensor(part[2], rest, part[1], ALU.subtract), max_split, n + 1)

            def normalize_heads(group):
                b, g = (group // NG % B, group % NG)
                dve.wait_ge(pvT_raw, group + 1)
                pv = ps[:, MISC, :].rearrange("p (t j s) -> p t j s", t=NT, j=HG)
                own(nc.vector.reciprocal(inv_sum[:, :, :], pv[:, :, :, D]))
                tell(nc.vector.tensor_tensor(
                    heads[b][:, :, g * HG * D:(g + 1) * HG * D].rearrange("p t (j d) -> p t j d", d=D),
                    pv[:, :, :, 0:D], inv_sum[:, :, :].unsqueeze(3).to_broadcast([P, NT, HG, D]), ALU.mult),
                    heads_ready, group + 1)

            def residual(n):
                b = n % B
                dve.wait_ge(xb_ready, n + 1)
                dve.wait_ge(o_raw, n + 1)
                tell(nc.vector.tensor_tensor(x_sb[:, b, :, :], grid(MISC, NT, C), x_bias[:, b, :, :], ALU.add),
                     x_ready, n + 1)

            def output(b):
                dve.wait_ge(xb_ready, 2 * B + b + 1)
                dve.wait_ge(m2_raw, b + 1)
                tell(nc.vector.tensor_tensor(x_sb[:, b, :, :], grid(MISC, NT, C), x_bias[:, b, :, :], ALU.add),
                     y_ready, b + 1)

            GM = HG * NT
            for i in range(LEAD * GM):
                self_maxima(i)
                if i == 1:
                    norm_apply(3)
                if i == 9:
                    queries_and_keys(1)
                if i == 13:
                    split_q_rest(1)
                if i % GM == GM - 1:
                    split_maxima(i // GM)
            for s in range(SELF_S):
                group, kt = divmod(s, NT)
                if group + LEAD < SELF_G:
                    for i in range(GM * (group + LEAD) + HG * kt, GM * (group + LEAD) + HG * (kt + 1)):
                        self_maxima(i)
                    if kt == NT - 1:
                        split_maxima(group + LEAD)
                for j in cross_heads(s):
                    cross_maxima(j)
                if kt == 2 and group:
                    normalize_heads(group - 1)
                if s == CLOSE:
                    residual(0)
                    norm_stats(4)
                if s == CLOSE + 1:
                    norm_apply(4)
                if s == CLOSE + 3:
                    split_q(2, MISC, col("q_b"))
                    split_q_rest(2)
            split_maxima(SELF_G)
            normalize_heads(SELF_G - 1)
            residual(1)
            normalize_heads(SELF_G)
            norm_stats(5)
            norm_apply(5)
            normalize_heads(SELF_G + 1)
            normalize_heads(SELF_G + 2)
            split_q(3, MISC, col("q_b"))
            split_q_rest(3)
            normalize_heads(SELF_G + 3)
            residual(2)
            norm_stats(6)
            norm_apply(6)
            for j in range(NH, 2 * NH):
                cross_maxima(j)
            split_maxima(SELF_G + 1)
            output(0)
            for g in range(NG):
                normalize_heads(SELF_G + NG + g)
            residual(3)
            norm_stats(7)
            norm_apply(7)
            output(1)

        @block.tensor
        def _(pe):
            reader = {}

            def claim(bank):
                if bank in reader:
                    pe.wait_ge(*reader[bank])

            def read_by(bank, signal, n):
                reader[bank] = (signal, n)

            def tiles_of(t):
                return slice(t * P, (t + 1) * P)

            def mm(out, lhsT, rhs, start=True, stop=True):
                return nc.tensor.matmul(out, lhsT, rhs, start=start, stop=stop)

            def product(name, emit):
                bank = con_bank(name)
                claim(bank)
                emit(bank).then_inc(con_raw, 1)
                read_by(bank, con_sb, made(name))

            pe.wait_ge(early_in, 16)
            product("kT0", lambda bank: mm(ps[:, bank, 0:B * L], w("w_early", "Wk"), ctxT))
            pe.wait_ge(con_sb, made("kT0"))
            product("score_w", lambda bank: mm(ps[:, bank, 0:B * L], w("w_early", "WqT"), kT0[:, :]))

            def per_sequence(bank, rhs):
                for b in range(B):
                    last = mm(ps[0:L, bank, b * C:(b + 1) * C], ctxT[:, b * L:(b + 1) * L], rhs)
                return last

            product("v0", lambda bank: per_sequence(bank, w("w_early", "Wv")))

            def transpose_normed(n):
                k, b = LN_ORDER[n]
                bank = SIDE[b] if k == 0 else MISC
                pe.wait_ge(normed_ready, n + 1)
                claim(bank)
                for t in range(NT):
                    last = nc.tensor.transpose(ps[:, bank, tiles_of(t)], normed[b][:, t, :], ident[:, :])
                last.then_inc(nT_raw, 1)
                read_by(bank, nT_ready, n + 1)

            pe.wait_ge(const_in, 48)
            for b in range(B):
                transpose_normed(b)
            pe.wait_ge(con_sb, made("score_w"))
            for b in range(B):
                pe.wait_ge(nT_ready, b + 1)
                claim(SIDE[b])
                for t in range(NT):
                    last = mm(ps[:, SIDE[b], t * P:t * P + L + NEXP], nT[b][:, tiles_of(t)], score_w[:, b, :])
                last.then_inc(s0_raw, 1)
                read_by(SIDE[b], s0_sub, b + 1)

            def hidden_bias(bank):
                cond = w("w_early", "cols")[:, 0:B]
                for c in range(HC):
                    mm(ps[:, bank, B * c:B * (c + 1)], hidden_w(c, 2), cond)
                for b in range(B):
                    last = mm(ps[:, bank, 16 + NEXP * b:16 + NEXP * (b + 1)], spread(col(f"cond{b}")),
                              router_w[:, 2, :])
                return last

            pe.wait_ge(hidden_in, 16)
            product("hidden_b", hidden_bias)

            def chunk_products(bank, n, lhsT, rhs):
                for i in range(n):
                    last = mm(ps[:, bank, i * C:(i + 1) * C], lhsT(i), rhs(i))
                return last

            def hidden_tokens(b, c):
                claim(EXP0 + c % 4)
                mm(ps[:, EXP0 + c % 4, :], hidden_w(c, 0), nT[b][:, :], stop=False)

            def hidden_evidence(b, c):
                mm(ps[:, EXP0 + c % 4, :], hidden_w(c, 1), evT[b], start=False).then_inc(hid_raw, 1)
                read_by(EXP0 + c % 4, hid_ready, HC * b + c + 1)

            def hidden_layer(b, chunks):
                for c in chunks:
                    hidden_tokens(b, c)
                    hidden_evidence(b, c)

            for b in range(B):
                pe.wait_ge(s0_norm, b + 1)
                claim(SIDE[b])
                for t in range(NT):
                    last = nc.tensor.transpose(ps[0:LP, SIDE[b], tiles_of(t)], attn0[b][:, t, :], ident[:, :])
                last.then_inc(s0T_raw, 1)
                read_by(SIDE[b], s0T_ready, b + 1)
            pe.wait_ge(out_in, 16)
            product("e_out_b", lambda bank: chunk_products(bank, NEXP, lambda i: spread(col(f"e_b2_{i}")),
                                                           lambda i: w("w_out", "out_w")))
            pe.wait_ge(con_sb, made("v0"))
            for b in range(B):
                pe.wait_ge(s0T_ready, b + 1)
                claim(SIDE[b])
                mm(ps[:, SIDE[b], :], v0[:, b, :], attn0T[b][:, :]).then_inc(ev_raw, 1)
                read_by(SIDE[b], ev_ready, b + 1)
            e_w2T = w("w_out", "e_w2T")
            product("e_out_w0", lambda bank: chunk_products(bank, 4, lambda i: e_w2T[:, tiles_of(i)],
                                                            lambda i: w("w_out", "out_w")))
            product("e_out_w1", lambda bank: chunk_products(bank, 2, lambda i: e_w2T[:, tiles_of(4 + i)],
                                                            lambda i: w("w_out", "out_w")))
            for b in range(B):
                pe.wait_ge(ev_ready, b + 1)
                claim(SIDE[b])
                for t in range(NT):
                    last = mm(ps[:, SIDE[b], 4 * t:4 * t + NEXP], evT[b][:, tiles_of(t)], router_w[:, 1, :])
                last.then_inc(rt_raw, 1)
                read_by(SIDE[b], rt_read, b + 1)

            def expert_outputs(b):
                pe.wait_ge(hid_ready, HC * (b + 1))
                claim(PVB)
                for t in range(NT):
                    last = mm(ps[:, PVB, tiles_of(t)], hidden[:, HC - 1, tiles_of(t)], w("w_out", "gate_w2"))
                last.then_inc(g2_raw, 1)
                read_by(PVB, g2_sum, b + 1)
                pe.wait_ge(con_sb, made("e_out_w1"))
                for t in range(NT):
                    bank = OUT_BANK[b][t]
                    claim(bank)
                    for e in range(NEXP):
                        for k in range(2):
                            last = mm(ps[:, bank, e * C:(e + 1) * C], hidden[:, 2 * e + k, tiles_of(t)],
                                      e_out_w[:, 2 * e + k, :], start=k == 0, stop=k == 1)
                    last.then_inc(e2_raw, 1)
                    read_by(bank, e2_read, NT * b + t + 1)

            def queries_keys_values(b):
                pe.wait_ge(nT_ready, 2 + b + 1)
                banks = QKV_BANK[b]
                claim(banks[0])
                mm(ps[:, banks[0], :], w("w_attn", "wq"), nT[b][:, :]).then_inc(q_raw, 1)
                read_by(banks[0], qf_ready, b + 1)
                claim(banks[1])
                mm(ps[:, banks[1], :], w("w_attn", "wk"), nT[b][:, :]).then_inc(k_raw, 1)
                read_by(banks[1], kf_ready, b + 1)
                claim(banks[2])
                for t in range(NT):
                    last = mm(ps[:, banks[2], tiles_of(t)], nT[b][:, tiles_of(t)], w("w_attn", "wv"))
                last.then_inc(v_raw, 1)
                read_by(banks[2], v_ready, b + 1)

            hidden_layer(0, range(HC))
            pe.wait_ge(attn_in, 16)
            pe.wait_ge(silu_done, 1)

            def ada_columns(bank):
                for j, k in enumerate(ADA_COLS):
                    last = mm(ps[:, bank, B * j:B * (j + 1)], ada_w[:, k, :], silu_cond[:, :])
                return last

            product("ada", ada_columns)
            product("gates", lambda bank: chunk_products(bank, 2 * B, lambda i: spread(silu_cond[:, i // 2:i // 2 + 1]),
                                                         lambda i: ada_w[:, ADA_ROWS[i % 2], :]))
            product("o_bias", lambda bank: chunk_products(bank, 2, lambda i: spread(col(("qkv_v", "kv_v")[i])),
                                                          lambda i: w("w_attn", ("self_o", "cross_o")[i])))
            product("kTc", lambda bank: mm(ps[:, bank, 0:B * L], w("w_attn", "kv_k"), ctxT))
            product("Vc", lambda bank: per_sequence(bank, w("w_attn", "kv_v")))
            expert_outputs(0)
            hidden_layer(1, range(4))
            transpose_normed(2)
            hidden_layer(1, range(4, 5))
            queries_keys_values(0)
            hidden_layer(1, range(5, HC))
            expert_outputs(1)

            def self_max_scores(i):
                b, h, qt = i // (NH * NT), i // NT % NH, i % NT
                if i % (NH * NT) == 0:
                    pe.wait_ge(stack_in[b], 16 * 2 * NPART)
                claim(MAX0 + i % 2)
                mm(ps[:, MAX0 + i % 2, :], Qs[b][:, h, tiles_of(qt)], Ks[b][:, h, :]).then_inc(max_raw, 1)
                read_by(MAX0 + i % 2, max_read, i + 1)

            def cross_max_scores(j):
                b, h = divmod(j, NH)
                i = SELF_MAX + j
                if h == 0:
                    pe.wait_ge(kc_in, 16 * NPART)
                    pe.wait_ge(q_zero, 16 * (b + 1))
                    pe.wait_ge(stack_in[B + b], 16 * NPART)
                claim(MAX0 + i % 2)
                for t in range(NT):
                    last = mm(ps[:, MAX0 + i % 2, t * P:t * P + L], Qs[b][:, h, tiles_of(t)], Kc[:, h, b, 0:L])
                last.then_inc(max_raw, 1)
                read_by(MAX0 + i % 2, max_read, i + 1)

            def transpose_maxima(n):
                nr = NPART * (HG if n < SELF_G else NH)
                pe.wait_ge(max_split, n + 1)
                claim(MISC)
                for t in range(NT):
                    last = nc.tensor.transpose(ps[0:nr, MISC, :].bitcast(BF16)[:, tiles_of(t)],
                                               max_parts[:, t, 0:nr], ident16[:, :])
                last.then_inc(mT_raw, 1)
                read_by(MISC, mT_ready, n + 1)

            def exp_scores(s, pr):
                cross, b, g, kt, group = tile(s)
                if pr == 0 and kt == 0:
                    n = group if not cross else SELF_G + b
                    pe.wait_ge(m_in[n % 2], 16 * (n // 2 + 1))
                e = 2 * s + pr
                for j in range(2):
                    h = HG * g + 2 * pr + j
                    bank = EXP0 + 2 * (e % 2) + j
                    claim(bank)
                    if cross:
                        last = mm(ps[0:LP, bank, :], Kc[:, h, b, :], Qs[b][:, h, :])
                    else:
                        last = mm(ps[:, bank, :], Ks[b][:, h, tiles_of(kt)], Qs[b][:, h, :])
                    read_by(bank, exp_ready, e + 1)
                last.then_inc(exp_raw, 1)

            def weigh_values(s):
                cross, b, g, kt, group = tile(s)
                pe.wait_ge(exp_ready, 2 * s + 2)
                if kt == 0:
                    if not cross and g == 0:
                        pe.wait_ge(v_ready, b + 1)
                    claim(PVB)
                for j in range(HG):
                    h = HG * g + j
                    if cross:
                        last = mm(ps[32 * j:32 * j + 32, PVB, :], Vc[b][:, VS * h:VS * h + 32],
                                  probs[0:LP, s % UNITS, j, :])
                    else:
                        last = mm(ps[32 * j:32 * j + 32, PVB, :], V[b][:, kt, VS * h:VS * h + 32],
                                  probs[:, s % UNITS, j, :], start=kt == 0, stop=kt == NT - 1)
                last.then_inc(pv_raw, 1)
                read_by(PVB, pv_ready, group + 1)

            def transpose_heads(group):
                pe.wait_ge(pv_ready, group + 1)
                claim(MISC)
                for t in range(NT):
                    last = nc.tensor.transpose(ps[:, MISC, tiles_of(t)], pv_sb[:, tiles_of(t)], ident[:, :])
                last.then_inc(pvT_raw, 1)
                read_by(MISC, heads_ready, group + 1)

            def project_heads(n):
                b = n % B
                pe.wait_ge(heads_ready, NG * (n + 1))
                claim(MISC)
                for t in range(NT):
                    last = nc.tensor.transpose(ps[:, MISC, tiles_of(t)], heads[b][:, t, :], ident[:, :])
                last.then_inc(hT_raw, 1)
                read_by(MISC, hT_ready, n + 1)
                if n < B:
                    pe.wait_ge(folded, b + 1)
                claim(MISC)
                for t in range(NT):
                    last = mm(ps[:, MISC, tiles_of(t)], headsT[:, tiles_of(t)],
                              self_o[:, b, :] if n < B else w("w_attn", "cross_o"))
                last.then_inc(o_raw, 1)
                read_by(MISC, x_ready, n + 1)

            def cross_queries(b):
                pe.wait_ge(nT_ready, 2 * B + b + 1)
                claim(MISC)
                mm(ps[:, MISC, :], w("w_attn", "q_w"), nT[b][:, :]).then_inc(q_raw, 1)
                read_by(MISC, qf_ready, B + b + 1)

            def mlp_up(b):
                pe.wait_ge(nT_ready, 3 * B + b + 1)
                pe.wait_ge(mlp_in, 16)
                for c in range(MC):
                    claim(EXP0 + c)
                    mm(ps[:, EXP0 + c, :], mlp_w1[:, c, :], nT[b][:, :]).then_inc(m1_raw, 1)
                    read_by(EXP0 + c, m1_ready, MC * b + c + 1)

            def mlp_down(b):
                pe.wait_ge(m1_ready, MC * (b + 1))
                claim(MISC)
                for t in range(NT):
                    for c in range(MC):
                        last = mm(ps[:, MISC, tiles_of(t)], mlp_h[b][:, c, tiles_of(t)], mlp_w2g[:, b, c, :],
                                  start=c == 0, stop=c == MC - 1)
                last.then_inc(m2_raw, 1)
                read_by(MISC, y_ready, b + 1)

            GM = HG * NT
            pe.wait_ge(pad_in, 16 * (2 * B + 1))
            for i in range(LEAD * GM):
                self_max_scores(i)
                if i == 5:
                    transpose_normed(3)
                if i == 9:
                    queries_keys_values(1)
                if i % GM == GM - 1:
                    transpose_maxima(i // GM)
            for s in range(SELF_S):
                group, kt = divmod(s, NT)
                first = GM * (group + LEAD) + HG * kt
                maxima = range(first, first + HG) if group + LEAD < SELF_G else ()
                exp_scores(s, 0)
                for i in maxima[:2]:
                    self_max_scores(i)
                for j in cross_heads(s)[:2]:
                    cross_max_scores(j)
                if s >= LAG:
                    weigh_values(s - LAG)
                for i in maxima[2:]:
                    self_max_scores(i)
                for j in cross_heads(s)[2:]:
                    cross_max_scores(j)
                exp_scores(s, 1)
                if kt == 0 and LEAD <= group + 1 < SELF_G:
                    transpose_maxima(group + 1)
                if kt == 2 and group:
                    transpose_heads(group - 1)
                if s == CLOSE:
                    project_heads(0)
                if s == CLOSE + 2:
                    transpose_normed(4)
                if s == CLOSE + 3:
                    cross_queries(0)
            for s in range(SELF_S - LAG, SELF_S):
                weigh_values(s)
            transpose_maxima(SELF_G)
            transpose_heads(SELF_G - 1)

            def cross_tile(s):
                for pr in range(2):
                    exp_scores(s, pr)

            cross_tile(SELF_S)
            cross_tile(SELF_S + 1)
            weigh_values(SELF_S)
            project_heads(1)
            transpose_heads(SELF_G)
            cross_tile(SELF_S + 2)
            weigh_values(SELF_S + 1)
            transpose_normed(5)
            transpose_heads(SELF_G + 1)
            cross_tile(SELF_S + 3)
            weigh_values(SELF_S + 2)
            transpose_heads(SELF_G + 2)
            cross_queries(1)
            weigh_values(SELF_S + 3)
            transpose_heads(SELF_G + 3)
            project_heads(2)
            transpose_normed(6)
            mlp_up(0)
            for j in range(NH, 2 * NH):
                cross_max_scores(j)
            transpose_maxima(SELF_G + 1)
            mlp_down(0)
            for g in range(NG):
                cross_tile(SELF_S + NG + g)
                if g:
                    weigh_values(SELF_S + NG + g - 1)
                    transpose_heads(SELF_G + NG + g - 1)
            weigh_values(SELF_S + 2 * NG - 1)
            transpose_heads(SELF_G + 2 * NG - 1)
            project_heads(3)
            transpose_normed(7)
            mlp_up(1)
            mlp_down(1)


def kernel(**inputs):
    import numpy as np
    import ml_dtypes
    import concourse.bacc as bacc
    from concourse.bass_utils import run_bass_kernel_spmd

    a = {k: np.asarray(v) for k, v in inputs.items()}
    l0 = {k[len("L0_xcond_"):]: v for k, v in a.items() if k.startswith("L0_xcond_")}
    l1 = {k[len("L1_xcond_"):]: v for k, v in a.items() if k.startswith("L1_xcond_")}

    def by_dim(v):
        return v.reshape(v.shape[:-1] + (NH, D)).swapaxes(-1, -2).reshape(v.shape)

    def rows_first(v, k):
        return v.reshape(k, P, -1).transpose(1, 0, 2).reshape(P, -1)

    qkv_b = l1["qkv_b"].reshape(3, C)
    kv_b = l1["kv_b"].reshape(2, C)
    ada_b = l1["ada_b"].reshape(6, C)
    e_b1 = l0["e_b1"].reshape(HC - 1, P)
    mlp_b1 = l1["mlp_b1"].reshape(MC, P)
    columns = {
        "cond0": a["cond_1024"][0], "cond1": a["cond_1024"][1], "ln_gamma": l0["ln_gamma"],
        "ln_beta": l0["ln_beta"], "gate_b1": l0["gate_b1"], "shift_msa": ada_b[0], "scale_msa": ada_b[1],
        "shift_mlp": ada_b[3], "scale_mlp": ada_b[4], "qkv_q": by_dim(qkv_b[0]), "qkv_k": by_dim(qkv_b[1]),
        "qkv_v": qkv_b[2], "norm2_g": l1["norm2_g"], "norm2_b": l1["norm2_b"], "q_b": by_dim(l1["q_b"]),
        "kv_k": by_dim(kv_b[0]), "kv_v": kv_b[1],
        **{f"e_b1_{i}": e_b1[i] for i in range(HC - 1)}, **{f"mlp_b1_{i}": mlp_b1[i] for i in range(MC)},
        **{f"e_b2_{i}": l0["e_b2"][i] for i in range(NEXP)},
    }
    free_rows = {
        "gate_b2": l0["gate_b2"], "out_b": l0["out_b"], "gate_msa": ada_b[2], "gate_mlp": ada_b[5],
        "self_o_b": l1["self_o_b"], "cross_o_b": l1["cross_o_b"], "mlp_b2": l1["mlp_b2"],
    }
    qkv_w, kv_w = l1["qkv_w"], l1["kv_w"]
    parts = {
        "cols": np.stack([columns[n] for n in COLS], axis=1),
        "ctxT": a["ctx_1024"].transpose(2, 0, 1).reshape(C, B * L),
        "WqT": l0["Wq"].T, "Wk": l0["Wk"], "Wv": l0["Wv"], "router": rows_first(l0["router_W"], 3),
        "gate_w1": rows_first(l0["gate_w1"], 3),
        "e_w1": l0["e_w1"].reshape(NEXP, 3, P, RH).transpose(2, 0, 1, 3).reshape(P, -1),
        "e_w2T": l0["e_w2"].transpose(2, 0, 1).reshape(C, NEXP * RH), "out_w": l0["out_w"],
        "gate_w2": l0["gate_w2"], "ada": l1["ada_w"],
        "wq": by_dim(qkv_w[:, 0:C]), "wk": by_dim(qkv_w[:, C:2 * C]), "wv": qkv_w[:, 2 * C:3 * C],
        "self_o": l1["self_o_w"], "q_w": by_dim(l1["q_w"]), "kv_k": by_dim(kv_w[:, 0:C]),
        "kv_v": kv_w[:, C:2 * C], "cross_o": l1["cross_o_w"], "w1": l1["mlp_w1"],
        "w2": rows_first(l1["mlp_w2"], MC),
    }
    pad = np.zeros((2, KS - MROW, T), ml_dtypes.bfloat16)
    pad[0, 0:NPART] = 1
    arrays = {"x": a["x"], "rows": np.concatenate([free_rows[n] for n in ROWS]),
              "router_b": l0["router_b"], "ident": np.eye(P, dtype=np.float32),
              "ident16": np.eye(P, dtype=ml_dtypes.bfloat16), "pad": pad}
    for pack, fields in PACKS.items():
        arrays[pack] = np.concatenate([parts[n] for n, _ in fields], axis=1)

    nc = bacc.Bacc("TRN2", target_bir_lowering=False, num_devices=1)
    arrays = {f"in_{n}": np.ascontiguousarray(v) for n, v in arrays.items()}
    d = {n[3:]: nc.dram_tensor(n, v.shape, mybir.dt.from_np(v.dtype), kind="ExternalInput").ap()
         for n, v in arrays.items()}
    out = nc.dram_tensor("out_0", (B, T, C), mybir.dt.float32, kind="ExternalOutput").ap()
    mixed_expert_attention_kernel(nc, d["x"], {n: d[n] for n in PACKS},
                                  d["rows"].rearrange("(r c) -> r c", c=C), d["router_b"], d["ident"],
                                  d["ident16"], d["pad"], out)
    result = run_bass_kernel_spmd(nc, [arrays], core_ids=[0])
    return result.results[0]["out_0"]
```

```python
import concourse.bass as bass
from concourse import mybir
from contextlib import ExitStack

B, T, C, L = 2, 512, 128, 77
P = 128
NT = T // P
NEXP = 3
RH = 2 * C
HC = NEXP * RH // P + 1
NH = 16
D = C // NH
NTU = NT // 2
TU = NTU * P
NU = B * NT // NTU
HG = 8
NG = NH // HG
CT = 4
CH = 2
MC = 4 * C // P
VS = D + 1
VW = NH * VS + 32 - VS
NPART = 3
MROW = NPART * NPART * D
KS = 96
LP = 96
LN_EPS = (1e-5, 1e-6, 1e-6, 1e-6)
UNITS = 4

COLS = ["cond0", "cond1", "ln_gamma", "ln_beta", "e_b1_0", "e_b1_1", "e_b1_2", "e_b1_3", "e_b1_4", "e_b1_5",
        "gate_b1", "shift_msa", "scale_msa", "shift_mlp", "scale_mlp", "qkv_q", "qkv_k", "qkv_v", "norm2_g",
        "norm2_b", "q_b", "kv_k", "kv_v", "mlp_b1_0", "mlp_b1_1", "mlp_b1_2", "mlp_b1_3", "e_b2_0", "e_b2_1",
        "e_b2_2"]
ROWS = ["gate_b2", "out_b", "gate_msa", "gate_mlp", "self_o_b", "cross_o_b", "mlp_b2"]
PACKS = {
    "w_early": [("cols", len(COLS)), ("ctxT", B * L), ("WqT", C), ("Wk", C), ("Wv", C), ("router", 3 * NEXP)],
    "w_hidden": [("gate_w1", 3 * C), ("e_w1", 3 * NEXP * RH)],
    "w_out": [("e_w2T", NEXP * RH), ("out_w", C), ("gate_w2", C)],
    "w_attn": [("ada", 6 * C), ("wq", C), ("wk", C), ("wv", C), ("self_o", C), ("q_w", C), ("kv_k", C),
               ("kv_v", C), ("cross_o", C)],
    "w_mlp": [("w1", MC * C), ("w2", MC * C)],
}


def spans(pack):
    at, found = 0, {}
    for name, n in PACKS[pack]:
        found[name] = (at, at + n)
        at += n
    return found, at


def mixed_expert_attention_kernel(nc, d_x, d_w, d_rows, d_router_b, d_ident, d_ident16, d_pad, d_out):
    F32, BF16 = mybir.dt.float32, mybir.dt.bfloat16
    ALU, ACT, AX = mybir.AluOpType, mybir.ActivationFunctionType, mybir.AxisListType.X

    with ExitStack() as ctx:
        def sb(name, shape, dt=F32):
            return ctx.enter_context(nc.sbuf_tensor(name, shape, dt))

        def sem(name):
            return ctx.enter_context(nc.semaphore(name))

        x_sb = sb("x_sb", [P, B, NT, C])
        w_tiles = {n: sb(n, [P, spans(n)[1]]) for n in PACKS if n != "w_hidden"}
        rows = sb("rows", [P, len(ROWS), C])
        router_b = sb("router_b", [P, NEXP])
        ident = sb("ident", [P, P])
        ident16 = sb("ident16", [P, P], BF16)

        region = sb("region", [P, UNITS * HG * TU])
        at = [0]

        def carve(n):
            at[0] += n
            assert at[0] <= UNITS * HG * TU
            return region[:, at[0] - n:at[0]]

        w_hidden = carve(spans("w_hidden")[1])
        hidden = carve(HC * T).rearrange("p (c n) -> p c n", c=HC)
        evT = [carve(T) for _ in range(B)]
        attn0 = [carve(NT * LP).rearrange("p (t l) -> p t l", t=NT) for _ in range(B)]
        probs = region[:, :].rearrange("p (u j n) -> p u j n", u=UNITS, j=HG)

        def w(pack, name):
            a, z = spans(pack)[0][name]
            return w_hidden[:, a:z] if pack == "w_hidden" else w_tiles[pack][:, a:z]

        def col(name):
            return w("w_early", "cols")[:, COLS.index(name):COLS.index(name) + 1]

        def row(name):
            return rows[:, ROWS.index(name), :]

        ctxT = w("w_early", "ctxT")
        router_w = w("w_early", "router").rearrange("p (k e) -> p k e", k=3)
        gate_w1 = w("w_hidden", "gate_w1").rearrange("p (k m) -> p k m", k=3)
        e_w1 = w("w_hidden", "e_w1").rearrange("p (e k r) -> p e k r", e=NEXP, k=3)
        mlp_w1 = w("w_mlp", "w1").rearrange("p (c m) -> p c m", c=MC)
        mlp_w2 = w("w_mlp", "w2").rearrange("p (c m) -> p c m", c=MC)
        ada_w = w("w_attn", "ada").rearrange("p (k m) -> p k m", k=6)
        ADA_COLS, ADA_ROWS = (0, 1, 3, 4), (2, 5)

        def hidden_w(c, k):
            if c == HC - 1:
                return gate_w1[:, k, :]
            return e_w1[:, c // 2, k, (c % 2) * P:(c % 2 + 1) * P]

        kT0 = sb("kT0", [P, B * L])
        score_w = sb("score_w", [P, B, L + NEXP])
        v0 = sb("v0", [LP, B, C])
        hidden_b = sb("hidden_b", [P, HC, B])
        router_bc = sb("router_bc", [P, B, NEXP])
        e_out_b = sb("e_out_b", [P, NEXP, C])
        e_out_w = sb("e_out_w", [P, NEXP * RH // P, C])
        silu_cond = sb("silu_cond", [P, B])
        ada_cols = sb("ada_cols", [P, 4, B])
        gates = sb("gates", [P, B, 2, C])
        o_bias = sb("o_bias", [P, 2, C])
        self_o = sb("self_o", [P, B, C])
        self_ob = sb("self_ob", [P, B, C])
        mlp_w2g = sb("mlp_w2g", [P, B, MC, C])
        mlp_b2g = sb("mlp_b2g", [P, B, C])

        stats = sb("stats", [P, B, NT, 6])
        mean_var = sb("mean_var", [P, B, NT, 2])
        var_eps = sb("var_eps", [P, B, NT])
        rstd = sb("rstd", [P, B, NT])
        minus_half = sb("minus_half", [P, NT])
        table = sb("table", [P, 1])
        normed = [sb(f"normed{b}", [P, NT, C]) for b in range(B)]
        nT = [sb(f"nT{b}", [P, T]) for b in range(B)]
        red0 = sb("red0", [P, B, 3, NT])
        router_x = sb("router_x", [P, B, NT, NEXP])
        route = sb("route", [P, B, NT, NEXP])
        attn0T = [sb(f"attn0T{b}", [LP, T]) for b in range(B)]
        gate = sb("gate", [P, NT, C])
        routed = sb("routed", [P, NT, C])
        pool_tmp = sb("pool_tmp", [P, NT, C])
        x_bias = sb("x_bias", [P, B, NT, C])
        qkf = sb("qkf", [P, 2, T])
        q_rest = sb("q_rest", [P, T])
        k_rest = sb("k_rest", [P, T])
        q_parts = sb("q_parts", [P, NPART, T], BF16)
        k_parts = sb("k_parts", [P, NPART, T], BF16)
        kcf = sb("kcf", [P, B * L])
        kc_rest = sb("kc_rest", [P, B * L])
        kc_parts = sb("kc_parts", [P, NPART, B * L], BF16)
        Qs = [sb(f"Qs{u}", [KS, NH, TU], BF16) for u in range(NU)]
        k_room = [sb(f"k_room{b}", [P, NH * T], BF16) for b in range(B)]
        Ks = [k[0:KS, :].rearrange("p (h n) -> p h n", h=NH) for k in k_room]
        Kc = sb("Kc", [KS, NH, B, LP], BF16)
        mlp_room = k_room[0][:, :].bitcast(F32).rearrange("p (u c n) -> p u c n", u=NU, c=MC)
        mlp_h = [mlp_room[:, u, :, :] for u in range(NU)]
        V = [sb(f"V{b}", [P, NT, VW]) for b in range(B)]
        Vc = [sb(f"Vc{b}", [LP, VW]) for b in range(B)]
        neg_max = sb("neg_max", [P, B, NT, NH])
        max_rest = sb("max_rest", [P, NTU, NH])
        max_parts = sb("max_parts", [P, NTU, NPART * NH], BF16)
        max_rows = sb("max_rows", [NPART * NH, 2, TU], BF16)
        zero16 = sb("zero16", [P, 1], BF16)
        pv_sb = sb("pv_sb", [P, T])
        inv_sum = sb("inv_sum", [P, NTU, HG])
        heads = [sb(f"heads{b}", [P, NT, C]) for b in range(B)]
        headsT = sb("headsT", [P, TU])

        q_scr = nc.dram_tensor("q_scr", (2 * NU, NPART, P, TU), BF16, kind="Internal").ap()
        k_scr = nc.dram_tensor("k_scr", (B, NPART, P, T), BF16, kind="Internal").ap()
        kc_scr = nc.dram_tensor("kc_scr", (NPART, P, B * L), BF16, kind="Internal").ap()

        ps = ctx.enter_context(nc.psum_tensor("ps", [P, 8, T], F32))
        MAX0, EXP0, PVB, MISC = 0, 2, 6, 7

        early_in, x_in, const_in, hidden_in, out_in, rows_in, attn_in, mlp_in, pad_in = (
            sem(n) for n in ("early_in", "x_in", "const_in", "hidden_in", "out_in", "rows_in", "attn_in", "mlp_in",
                             "pad_in"))
        x1_in = sem("x1_in")
        vec_own, pool_own = sem("vec_own"), sem("pool_own")
        zeroed, ones_set, con_raw, con_sb, silu_done, folded = (
            sem(n) for n in ("zeroed", "ones_set", "con_raw", "con_sb", "silu_done", "folded"))
        var_ready, rstd_ready, normed_ready, nT_raw, nT_ready = (
            sem(n) for n in ("var_ready", "rstd_ready", "normed_ready", "nT_raw", "nT_ready"))
        s0_raw, s0_sub, s0_exp, s0_norm, s0T_raw, s0T_ready = (
            sem(n) for n in ("s0_raw", "s0_sub", "s0_exp", "s0_norm", "s0T_raw", "s0T_ready"))
        ev_raw, ev_ready, rt_raw, rt_read, rt_sub, rt_exp, rt_ready = (
            sem(n) for n in ("ev_raw", "ev_ready", "rt_raw", "rt_read", "rt_sub", "rt_exp", "rt_ready"))
        hid_raw, hid_ready, g2_raw, g2_sum, g2_tanh, e2_raw, e2_read, e_bias, x1_ready = (
            sem(n) for n in ("hid_raw", "hid_ready", "g2_raw", "g2_sum", "g2_tanh", "e2_raw", "e2_read", "e_bias",
                             "x1_ready"))
        q_raw, k_raw, v_raw, qf_ready, kf_ready, v_ready, q_hi, k_hi, q_split, k_split, kc_split = (
            sem(n) for n in ("q_raw", "k_raw", "v_raw", "qf_ready", "kf_ready", "v_ready", "q_hi", "k_hi",
                             "q_split", "k_split", "kc_split"))
        q_out, k_out, kc_out, kc_in = (sem(n) for n in ("q_out", "k_out", "kc_out", "kc_in"))
        q_in = [sem(f"q_in{i}") for i in range(2 * NU)]
        k_in = [sem(f"k_in{i}") for i in range(B * NG)]
        max_raw, max_read, max_split, mT_raw, mT_ready = (
            sem(n) for n in ("max_raw", "max_read", "max_split", "mT_raw", "mT_ready"))
        m_in = [sem("m_in0"), sem("m_in1")]
        exp_raw, exp_ready, pv_raw, pv_ready, pvT_raw, heads_ready = (
            sem(n) for n in ("exp_raw", "exp_ready", "pv_raw", "pv_ready", "pvT_raw", "heads_ready"))
        hT_raw, hT_ready, o_raw, x_ready, xb_ready = (
            sem(n) for n in ("hT_raw", "hT_ready", "o_raw", "x_ready", "xb_ready"))
        m1_raw, m1_ready, m2_raw, y_ready, out_done = (
            sem(n) for n in ("m1_raw", "m1_ready", "m2_raw", "y_ready", "out_done"))

        CON = ["kT0", "score_w", "v0", "hidden_b", "router_b", "e_out_b", "e_out_w0", "e_out_w1", "ada", "gates",
               "o_bias", "kTc", "Vc"]

        def made(name):
            return CON.index(name) + 1

        def con_bank(name):
            return MAX0 + CON.index(name) % 2

        SIDE = (MISC, PVB)
        OUT_BANK = [[MAX0, MAX0 + 1, MISC, EXP0 + 3], [EXP0 + t for t in range(NT)]]
        QKV_BANK = [(PVB, MISC, MAX0), (MISC, MISC, MISC)]

        def spread(column):
            return column.to_broadcast([P, P])

        def unit_tiles(u):
            return u * NTU // NT, slice(u * NTU % NT, u * NTU % NT + NTU)

        LAG = 2
        LEAD = 24
        GROUP_MAX = HG * NTU
        MAX_PER_TILE = GROUP_MAX // NT

        def plan():
            stages, tiles, groups = [], [], []
            due = {}
            crossing = []
            slot, maxima = 0, 0

            def split_maxima(group):
                for waiting in due.values():
                    for stage in [x for x in waiting if x[0] == "max_T"]:
                        waiting.remove(stage)
                        stages.append(stage)
                stages.append(("max_split", group))
                due.setdefault(slot + 1, []).append(("max_T", group))

            def more_maxima(n):
                nonlocal maxima
                for _ in range(n):
                    if maxima == GROUP_MAX * NU * NG:
                        break
                    stages.append(("max", maxima))
                    maxima += 1
                    if maxima % GROUP_MAX == 0:
                        split_maxima(("self",) + divmod(maxima // GROUP_MAX - 1, NG))

            def finish(kind, u):
                def later(after, stage, n):
                    due.setdefault(slot + after, []).append((stage, n))

                k = 2 if kind == "self" else 3
                for stage in ("heads_T", "project"):
                    later(DELAY[stage], stage, (kind, u))
                for stage in ("stats", "apply", "norm_T"):
                    later(DELAY[stage], stage, (k, u))
                if kind == "self":
                    later(DELAY["query"], "query", u)
                    for i in range(NH // CH):
                        later(DELAY["cross_max"] + i // PER_SLOT, "cross_max", (u, i))
                    last = DELAY["cross_max"] + (NH // CH - 1) // PER_SLOT
                    later(last, "max_split", ("cross", u, 0))
                    crossing.append((slot + last + DELAY["rows"], u))
                else:
                    for j in range(MC // 2):
                        later(DELAY["mlp_up"], "mlp_up", (u, j))
                    later(DELAY["mlp_down"], "mlp_down", u)

            def weigh(s, r):
                stages.append(("weigh", (s, r)))
                kind, u, g, kt = tiles[s]
                if r == 1 and (kind == "cross" or kt == NT - 1):
                    stages.append(("keep", (kind, u, g)))
                    due.setdefault(slot + DELAY["values_T"], []).append(("values_T", (kind, u, g)))
                    if g == NG - 1:
                        finish(kind, u)

            def close_slot():
                nonlocal slot
                for stage in sorted(due.pop(slot, []), key=lambda x: x[0] != "max_T"):
                    if stage[0] == "max_split":
                        split_maxima(stage[1])
                    else:
                        stages.append(stage)
                slot += 1

            stages += [("scores", 0), ("bias", 0), ("scores_norm", 0), ("scores_T", 0), ("scores", 1),
                       ("evidence", 0), ("bias", 1), ("route", 0), ("route_norm", 0), ("hidden", (0, 0)),
                       ("scores_norm", 1), ("scores_T", 1)]
            stages.extend(("hidden", (0, c)) for c in range(1, 4))
            stages += [("weights", 0), ("weights", 1)]
            stages.extend(("hidden", (0, c)) for c in range(4, HC))
            stages += [("evidence", 1), ("gate", 0)]
            stages.extend(("expert", (0, t)) for t in range(NT))
            stages += [("gated", 0), ("stats", (1, 0)), ("route", 1), ("route_norm", 1)]
            stages.extend(("hidden", (1, c)) for c in range(4))
            stages += [("apply", (1, 0)), ("norm_T", (1, 0)), ("hidden", (1, 4)), ("keys", 0), ("queries", 0),
                       ("values", 0)]
            stages.extend(("hidden", (1, c)) for c in range(5, HC))
            stages += [("gate", 1), ("weights", 2)]
            stages.extend(("expert", (1, t)) for t in range(NT))
            stages += [("gated", 1), ("load_exp", 0)]
            more_maxima(GROUP_MAX)
            stages.extend(due.pop(1))
            more_maxima(LEAD - GROUP_MAX)
            for at, stage in enumerate((("stats", (1, 1)), ("apply", (1, 1)), ("norm_T", (1, 1)), ("keys", 1),
                                        ("queries", 1), ("values", 1))):
                due.setdefault(NEXT[at], []).append(stage)

            left = [("self", u, g, kt) for u in range(NU) for g in range(NG) for kt in range(NT)]

            def next_tile(tile):
                tiles.append(tile)
                if tile[0:3] not in groups:
                    groups.append(tile[0:3])
                return len(tiles) - 1

            while left:
                if crossing and crossing[0][0] <= slot and left[0][3] == 0:
                    u = crossing.pop(0)[1]
                    left[0:0] = [("cross", u, g, 0) for g in range(NG)]
                s = next_tile(left.pop(0))
                few = MAX_PER_TILE // 4 if tiles[s][0] == "self" else 0
                for r in range(2):
                    stages.append(("exp", (s, r)))
                    more_maxima(few)
                    if s >= LAG:
                        weigh(s - LAG, r)
                    more_maxima(few)
                    close_slot()

            def now(*these):
                for stage in these:
                    if stage not in stages:
                        stages.append(stage)

            def weigh_now(s):
                now(("weigh", (s, 0)), ("weigh", (s, 1)))
                kind, u, g, kt = tiles[s]
                if kind == "cross" or kt == NT - 1:
                    now(("keep", (kind, u, g)))

            def cross_tile(u, g):
                s = next_tile(("cross", u, g, 0))
                now(("exp", (s, 0)), ("exp", (s, 1)))
                return s

            def cross_max_stages(u):
                now(*[("cross_max", (u, i)) for i in range(NH // CH)])
                now(("max_split", ("cross", u, 0)))

            first, middle, final = range(NU - 3, NU)
            for s in range(len(tiles) - LAG, len(tiles)):
                weigh_now(s)
            cross_max_stages(middle)
            now(("values_T", ("self", final, NG - 1)), ("max_T", ("cross", middle, 0)), ("heads_T", ("self", final)))
            now(("project", ("cross", first)), ("stats", (3, first)), ("apply", (3, first)), ("norm_T", (3, first)))
            s0 = cross_tile(middle, 0)
            now(("project", ("self", final)), ("stats", (2, final)))
            weigh_now(s0)
            now(("apply", (2, final)), ("norm_T", (2, final)), ("query", final))
            s1 = cross_tile(middle, 1)
            now(("values_T", ("cross", middle, 0)))
            weigh_now(s1)
            now(("mlp_up", (first, 0)), ("mlp_up", (first, 1)), ("load_exp", 1))
            cross_max_stages(final)
            now(("values_T", ("cross", middle, 1)), ("max_T", ("cross", final, 0)), ("mlp_down", first))
            s0 = cross_tile(final, 0)
            now(("heads_T", ("cross", middle)))
            s1 = cross_tile(final, 1)
            now(("project", ("cross", middle)), ("stats", (3, middle)))
            weigh_now(s0)
            now(("values_T", ("cross", final, 0)))
            weigh_now(s1)
            now(("apply", (3, middle)), ("norm_T", (3, middle)))
            now(("values_T", ("cross", final, 1)), ("heads_T", ("cross", final)), ("project", ("cross", final)),
                ("mlp_up", (middle, 0)), ("mlp_up", (middle, 1)), ("stats", (3, final)), ("apply", (3, final)),
                ("norm_T", (3, final)), ("mlp_up", (final, 0)), ("mlp_up", (final, 1)), ("mlp_down", middle),
                ("mlp_down", final))
            return stages, tiles, groups

        DELAY = dict(values_T=1, heads_T=2, project=3, stats=3, apply=5, norm_T=6, query=7, cross_max=13, rows=4,
                     mlp_up=7, mlp_down=10)
        NEXT = (0, 2, 3, 5, 7, 8)
        PER_SLOT = 5
        STAGES, TILES, GROUPS = plan()

        def turns(*kinds):
            return {stage: i for i, stage in enumerate(x for x in STAGES if x[0] in kinds)}

        MAX_TURN = turns("max", "cross_max")
        Q_SPLITS = turns("queries", "query")
        Q_WRITES = {stage: sum(2 if x[0] == "queries" else 1 for x in list(Q_SPLITS)[:i + 1])
                    for stage, i in Q_SPLITS.items()}
        SPLIT_TURN = turns("max_split")
        NORM_TURN = {(k, b): b for k, b in ((0, 0), (0, 1))}
        NORM_TURN.update({stage[1]: B + i for stage, i in turns("norm_T").items()})
        PROJECT_TURN = {stage[1]: i for stage, i in turns("project").items()}
        MLP_UP_TURN = turns("mlp_up")
        UP_BANK = [(MISC, MAX0)] * (NU - 3) + [(EXP0, EXP0 + 1)] * 2 + [(EXP0 + 2, EXP0 + 3)]
        DOWN_BANK = [MISC] * (NU - 3) + [MAX0, MAX0 + 1, MISC]
        MLP_TURN = {stage[1]: i for stage, i in turns("mlp_down").items()}
        BIAS_TURN = {(stage[0], stage[1]): i for stage, i in turns("project", "mlp_down").items()}

        def max_place(i):
            group, rest = divmod(i, GROUP_MAX)
            u, g = divmod(group, NG)
            b, tiles = unit_tiles(u)
            return b, tiles.start + rest % NTU, g * HG + rest // NTU

        def last_tile(group):
            return max(s for s, t in enumerate(TILES) if t[0:3] == group)

        def norm_tiles(k, n):
            return (n, slice(0, NT)) if k < 2 else unit_tiles(n)

        block = ctx.enter_context(nc.Block())

        @block.sync
        def _(sp):
            sp.dma_start(w_tiles["w_early"][:, :], d_w["w_early"]).then_inc(early_in, 16)
            sp.dma_start(x_sb[:, 0, :, :], d_x[0].rearrange("(p t) c -> p t c", t=NT)).then_inc(x_in, 16)
            sp.dma_start(x_sb[:, 1, :, :], d_x[1].rearrange("(p t) c -> p t c", t=NT)).then_inc(x1_in, 16)
            sp.dma_start(ident[:, :], d_ident).then_inc(const_in, 16)
            sp.dma_start(ident16[:, :], d_ident16).then_inc(const_in, 16)
            sp.dma_start(router_b[:, :], d_router_b.partition_broadcast(P)).then_inc(const_in, 16)
            sp.dma_start(w_hidden, d_w["w_hidden"]).then_inc(hidden_in, 16)
            sp.dma_start(w_tiles["w_out"][:, :], d_w["w_out"]).then_inc(out_in, 16)
            sp.dma_start(rows[:, :, :], d_rows.partition_broadcast(P)).then_inc(rows_in, 16)
            sp.dma_start(w_tiles["w_attn"][:, :], d_w["w_attn"]).then_inc(attn_in, 16)
            sp.dma_start(w_tiles["w_mlp"][:, :], d_w["w_mlp"]).then_inc(mlp_in, 16)
            sp.wait_ge(zeroed, 1)
            sp.dma_start(Kc[MROW:KS, :, :, 0:L].rearrange("p h b n -> p (h b) n"),
                         d_pad[0][:, 0:L].unsqueeze(1).to_broadcast([KS - MROW, NH * B, L])).then_inc(pad_in, 16)
            for b in range(B):
                sp.dma_start(Ks[b][MROW:KS, :, :],
                             d_pad[0].unsqueeze(1).to_broadcast([KS - MROW, NH, T])).then_inc(pad_in, 16)
            for u in range(NU):
                sp.dma_start(Qs[u][MROW:KS, :, :],
                             d_pad[1][:, 0:TU].unsqueeze(1).to_broadcast([KS - MROW, NH, TU])).then_inc(pad_in, 16)

            def q_rows(u, n):
                sp.dma_start(Qs[u][0:MROW, :, :].rearrange("p h n -> p (h n)"),
                             q_scr[n].rearrange("i (d h) n -> (i d) (h n)", d=D).unsqueeze(0)
                             .to_broadcast([NPART, NPART * D, NH * TU])).then_inc(q_in[n], 16)

            def k_rows(b, g):
                for j in range(NPART):
                    sp.dma_start(Ks[b][NPART * D * j:NPART * D * (j + 1), g * HG:(g + 1) * HG, :]
                                 .rearrange("p h n -> p (h n)"),
                                 k_scr[b, j].rearrange("(d h) n -> d (h n)", d=D)[:, g * HG * T:(g + 1) * HG * T]
                                 .unsqueeze(0).to_broadcast([NPART, D, HG * T])).then_inc(k_in[NG * b + g], 16)

            def restack_self(b):
                units = (2 * b, 2 * b + 1)
                sp.wait_ge(k_split, b + 1)
                sp.dma_start(k_scr[b].rearrange("i p n -> p i n"), k_parts[:, :, :]).then_inc(k_out, 16)
                sp.wait_ge(q_split, Q_SPLITS[("queries", b)] + 1)
                for u in units:
                    sp.dma_start(q_scr[u].rearrange("i p n -> p i n"),
                                 q_parts[:, :, u % 2 * TU:(u % 2 + 1) * TU]).then_inc(q_out, 16)
                sp.wait_ge(k_out, 16 * (b + 1))
                k_rows(b, 0)
                sp.wait_ge(q_out, 16 * Q_WRITES[("queries", b)])
                q_rows(units[0], units[0])
                k_rows(b, 1)
                q_rows(units[1], units[1])

            def restack_cross(u):
                sp.wait_ge(q_split, Q_SPLITS[("query", u)] + 1)
                sp.dma_start(q_scr[NU + u].rearrange("i p n -> p i n"), q_parts[:, :, 0:TU]).then_inc(q_out, 16)
                sp.wait_ge(exp_raw, 2 * (last_tile(("self", u, NG - 1)) + 1))
                sp.wait_ge(q_out, 16 * Q_WRITES[("query", u)])
                q_rows(u, NU + u)

            def restack_context():
                sp.wait_ge(kc_split, 1)
                sp.dma_start(kc_scr.rearrange("i p n -> p i n"), kc_parts[:, :, :]).then_inc(kc_out, 16)
                sp.wait_ge(kc_out, 16)
                for row in range(0, MROW, D):
                    sp.dma_start(Kc[row:row + D, :, :, 0:L].rearrange("p h b n -> p (h b) n"),
                                 kc_scr[row // (NPART * D)].rearrange("(d h) (b n) -> d (h b) n", d=D,
                                                                      b=B)).then_inc(kc_in, 16)

            for stage, n in STAGES:
                if stage == "queries":
                    restack_self(n)
                elif stage == "weights" and n == 2:
                    restack_context()
                elif stage == "query":
                    restack_cross(n)
                elif stage == "mlp_down":
                    b, tiles = unit_tiles(n)
                    sp.wait_ge(y_ready, MLP_TURN[n] + 1)
                    sp.dma_start(d_out[b].rearrange("(p t) c -> p t c", t=NT)[:, tiles, :],
                                 x_sb[:, b, tiles, :]).then_inc(out_done, 16)
            sp.wait_ge(out_done, 16 * NU)

        @block.gpsimd
        def _(pool):
            count = [0]

            def own(ins):
                count[0] += 1
                ins.then_inc(pool_own, 1)
                pool.wait_ge(pool_own, count[0])

            def tell(ins, signal, n):
                ins.then_inc(signal, 1)
                pool.wait_ge(signal, n)

            def over_tiles(v):
                return v.unsqueeze(1).to_broadcast([P, NT, C])

            def inverse_deviation(k, n):
                b, tiles = norm_tiles(k, n)
                turn = NORM_TURN[(k, n)]
                pool.wait_ge(var_ready, turn + 1)
                tell(nc.gpsimd.tensor_tensor(rstd[:, b, tiles], var_eps[:, b, tiles],
                                             minus_half[:, 0:tiles.stop - tiles.start], ALU.pow), rstd_ready, turn + 1)

            own(nc.gpsimd.memset(minus_half[:, :], -0.5))
            inverse_deviation(0, 0)
            inverse_deviation(0, 1)
            tell(nc.gpsimd.memset(Kc[:, :, :, :].rearrange("p h b n -> p (h b n)").bitcast(F32), 0.0), zeroed, 1)

            def expert_bias(b):
                pool.wait_ge(con_sb, made("e_out_b"))
                pool.wait_ge(rt_ready, b + 1)
                for e in range(NEXP):
                    dst = x_bias[:, b, :, :] if e == 0 else pool_tmp[:, :, :]
                    own(nc.gpsimd.tensor_tensor(dst, over_tiles(e_out_b[:, e, :]),
                                                route[:, b, :, e:e + 1].to_broadcast([P, NT, C]), ALU.mult))
                    if e:
                        ins = nc.gpsimd.tensor_tensor(x_bias[:, b, :, :], x_bias[:, b, :, :], pool_tmp[:, :, :],
                                                      ALU.add)
                        own(ins) if e < NEXP - 1 else tell(ins, e_bias, b + 1)


            def fold_gates(b):
                pool.wait_ge(con_sb, made("o_bias"))
                pool.wait_ge(mlp_in, 16)
                own(nc.gpsimd.tensor_tensor(self_o[:, b, :], w("w_attn", "self_o"), gates[:, b, 0, :], ALU.mult))
                own(nc.gpsimd.tensor_tensor(self_ob[:, b, :], o_bias[:, 0, :], gates[:, b, 0, :], ALU.mult))
                own(nc.gpsimd.tensor_tensor(mlp_w2g[:, b, :, :], mlp_w2,
                                            gates[:, b, 1, :].unsqueeze(1).to_broadcast([P, MC, C]), ALU.mult))
                tell(nc.gpsimd.tensor_tensor(mlp_b2g[:, b, :], row("mlp_b2"), gates[:, b, 1, :], ALU.mult),
                     folded, b + 1)

            def add_bias(stage, kind, u):
                b, tiles = unit_tiles(u)
                if kind == "self":
                    pool.wait_ge(x1_ready, b + 1)
                    bias = self_ob[:, b, :]
                elif kind == "cross":
                    pool.wait_ge(x_ready, PROJECT_TURN[("self", u)] + 1)
                    bias = o_bias[:, 1, :]
                else:
                    pool.wait_ge(x_ready, PROJECT_TURN[("cross", u)] + 1)
                    bias = mlp_b2g[:, b, :]
                turn = BIAS_TURN[(stage, u if kind == "mlp" else (kind, u))]
                tell(nc.gpsimd.tensor_tensor(x_bias[:, b, tiles, :], x_sb[:, b, tiles, :],
                                             bias.unsqueeze(1).to_broadcast([P, NTU, C]), ALU.add), xb_ready, turn + 1)

            def split_second(parts, i, hi_ready, turn, signal):
                rest = (k_rest, q_rest)[i]
                pool.wait_ge(hi_ready, turn + 1)
                if i:
                    pool.wait_ge(q_split, turn)
                else:
                    pool.wait_ge(k_split, 1)
                own(nc.gpsimd.tensor_tensor(rest[:, :], qkf[:, i, :], parts[:, 0, :], ALU.subtract))
                own(nc.gpsimd.tensor_tensor(parts[:, 1, :], qkf[:, i, :], parts[:, 0, :], ALU.subtract))
                tell(nc.gpsimd.tensor_tensor(parts[:, 2, :], rest[:, :], parts[:, 1, :], ALU.subtract), signal,
                     turn + 1)

            for stage, n in STAGES:
                if stage == "gate":
                    expert_bias(n)
                elif stage == "stats":
                    inverse_deviation(*n)
                elif stage == "keys" and n == 1:
                    split_second(k_parts, 0, k_hi, 1, k_split)
                elif stage == "queries" and n == 1:
                    split_second(q_parts, 1, q_hi, Q_SPLITS[("queries", 1)], q_split)
                elif stage == "weights" and n == 2:
                    fold_gates(0)
                    fold_gates(1)
                elif stage == "project":
                    add_bias(stage, *n)
                elif stage == "mlp_down":
                    add_bias(stage, "mlp", n)

        @block.scalar
        def _(act):
            def norm_affine(k, n):
                b, tiles = norm_tiles(k, n)
                act.wait_ge(nT_raw, NORM_TURN[(k, n)] + 1)
                if k == 0:
                    act.wait_ge(early_in, 16)
                if k == 1:
                    act.wait_ge(con_sb, made("ada"))
                scale, bias = {
                    0: (col("ln_gamma"), col("ln_beta")),
                    1: (ada_cols[:, 1, b:b + 1], ada_cols[:, 0, b:b + 1]),
                    2: (col("norm2_g"), col("norm2_b")),
                    3: (ada_cols[:, 3, b:b + 1], ada_cols[:, 2, b:b + 1]),
                }[k]
                bank = SIDE[b] if k == 0 else MISC
                cols = slice(tiles.start * P, tiles.stop * P)
                nc.scalar.activation(nT[b][:, cols], ps[:, bank, 0:cols.stop - cols.start], ACT.Identity, scale=scale,
                                     bias=bias).then_inc(nT_ready, 1)

            norm_affine(0, 0)
            norm_affine(0, 1)

            def exp_context(b):
                act.wait_ge(s0_sub, b + 1)
                nc.scalar.activation(attn0[b][:, :, 0:L], attn0[b][:, :, 0:L], ACT.Exp,
                                     scale=float(C) ** -0.5).then_inc(s0_exp, 1)

            def keep_evidence(b):
                act.wait_ge(ev_raw, b + 1)
                nc.scalar.activation(evT[b], ps[:, SIDE[b], :], ACT.Copy).then_inc(ev_ready, 1)

            def exp_route(b):
                act.wait_ge(rt_sub, b + 1)
                nc.scalar.activation(route[:, b, :, :], route[:, b, :, :], ACT.Exp).then_inc(rt_exp, 1)
                if b == 0:
                    nc.scalar.activation(silu_cond[:, :], w("w_early", "cols")[:, 0:B],
                                         ACT.Silu).then_inc(silu_done, 1)

            def hidden_layer(b, c):
                if c == 0:
                    act.wait_ge(con_sb, made("hidden_b"))
                    if b:
                        act.wait_ge(e2_raw, NT * b)
                act.wait_ge(hid_raw, HC * b + c + 1)
                nc.scalar.activation(hidden[:, c, :], ps[:, EXP0 + c % 4, :], ACT.Silu,
                                     bias=hidden_b[:, c, b:b + 1]).then_inc(hid_ready, 1)

            def gate_tanh(b):
                act.wait_ge(g2_sum, b + 1)
                nc.scalar.activation(gate[:, :, :], gate[:, :, :], ACT.Tanh, scale=0.5).then_inc(g2_tanh, 1)

            def high_part_q(stage, bank, bias, width):
                turn = Q_SPLITS[stage]
                act.wait_ge(q_raw, turn + 1)
                if turn:
                    act.wait_ge(q_out, 16 * Q_WRITES[list(Q_SPLITS)[turn - 1]])
                if stage == ("queries", 1):
                    nc.scalar.activation(qkf[:, 1, :], ps[:, bank, :], ACT.Identity, bias=bias)
                nc.scalar.activation(q_parts[:, 0, 0:width], ps[:, bank, 0:width], ACT.Identity,
                                     bias=bias).then_inc(q_hi, 1)

            def high_part_k(b):
                if b:
                    act.wait_ge(k_out, 16 * b)
                act.wait_ge(k_raw, b + 1)
                if b:
                    nc.scalar.activation(qkf[:, 0, :], ps[:, QKV_BANK[b][1], :], ACT.Identity, bias=col("qkv_k"))
                nc.scalar.activation(k_parts[:, 0, :], ps[:, QKV_BANK[b][1], :], ACT.Identity,
                                     bias=col("qkv_k")).then_inc(k_hi, 1)

            def keep_v(b):
                act.wait_ge(v_raw, b + 1)
                act.wait_ge(ones_set, B)
                nc.scalar.activation(
                    V[b][:, :, 0:NH * VS].rearrange("p t (h s) -> p t h s", s=VS)[:, :, :, 0:D],
                    ps[:, QKV_BANK[b][2], :].rearrange("p (t h d) -> p t h d", t=NT, d=D), ACT.Copy).then_inc(v_ready, 1)

            def maximum_rows(kind, u, g):
                n = SPLIT_TURN[("max_split", (kind, u, g))]
                h0, nh = (g * HG, HG) if kind == "self" else (0, NH)
                act.wait_ge(mT_raw, n + 1)
                if n >= 2:
                    act.wait_ge(m_in[n % 2], 16 * (n // 2))
                nc.scalar.activation(max_rows[0:NPART * nh, n % 2, :],
                                     ps[0:NPART * nh, MISC, :].bitcast(BF16)[:, 0:TU], ACT.Copy).then_inc(mT_ready, 1)
                act.wait_ge(mT_ready, n + 1)
                act.dma_start(Qs[u][MROW:MROW + NPART, h0:h0 + nh, :],
                              max_rows[0:NPART * nh, n % 2, :]).then_inc(m_in[n % 2], 16)

            def exps(s, pr):
                rows_ = P if TILES[s][0] == "self" else LP
                if s >= UNITS:
                    act.wait_ge(pv_raw, 2 * (s - UNITS) + pr + 1)
                e = 2 * s + pr
                act.wait_ge(exp_raw, e + 1)
                bank = EXP0 + 2 * (e % 2)
                nc.scalar.activation(probs[0:rows_, s % UNITS, CT * pr:CT * (pr + 1), :],
                                     ps[0:rows_, bank:bank + 2, :].rearrange("p a (j n) -> p (a j) n", n=TU),
                                     ACT.Exp, scale=float(D) ** -0.5).then_inc(exp_ready, 1)

            def keep_values(*group):
                n = GROUPS.index(group)
                act.wait_ge(pv_raw, 2 * last_tile(group) + 2)
                if n:
                    act.wait_ge(pvT_raw, n)
                nc.scalar.activation(pv_sb[:, :], ps[:, PVB, :], ACT.Copy).then_inc(pv_ready, 1)

            def keep_headsT(n):
                act.wait_ge(hT_raw, n + 1)
                if n:
                    act.wait_ge(o_raw, n)
                nc.scalar.activation(headsT[:, :], ps[:, MISC, 0:TU], ACT.Copy).then_inc(hT_ready, 1)

            def gelu(u, j):
                act.wait_ge(m1_raw, MLP_UP_TURN[("mlp_up", (u, j))] + 1)
                for i in range(2):
                    c = 2 * j + i
                    nc.scalar.activation(mlp_h[u][:, c, :], ps[:, UP_BANK[u][j], i * TU:(i + 1) * TU],
                                         ACT.Gelu_apprx_tanh, bias=col(f"mlp_b1_{c}")).then_inc(m1_ready, 1)

            for stage, n in STAGES:
                if stage == "scores":
                    exp_context(n)
                elif stage == "evidence":
                    keep_evidence(n)
                elif stage == "route":
                    exp_route(n)
                elif stage == "hidden":
                    hidden_layer(*n)
                elif stage == "gate":
                    gate_tanh(n)
                elif stage == "load_exp":
                    nc.scalar.activation(table[:, :], minus_half[:, 0:1], ACT.Exp)
                elif stage == "norm_T":
                    norm_affine(*n)
                elif stage == "keys":
                    high_part_k(n)
                elif stage == "queries":
                    high_part_q(("queries", n), QKV_BANK[n][0], col("qkv_q"), T)
                elif stage == "values":
                    keep_v(n)
                elif stage == "max_T":
                    maximum_rows(*n)
                elif stage == "exp":
                    if n == (0, 0):
                        act.wait_ge(e2_raw, NT * B)
                    exps(*n)
                elif stage == "keep":
                    keep_values(*n)
                elif stage == "heads_T":
                    keep_headsT(PROJECT_TURN[n])
                elif stage == "query":
                    high_part_q(("query", n), MISC, col("q_b"), TU)
                elif stage == "mlp_up":
                    gelu(*n)

        @block.vector
        def _(dve):
            count = [0]

            def own(ins):
                count[0] += 1
                ins.then_inc(vec_own, 1)
                dve.wait_ge(vec_own, count[0])

            def tell(ins, signal, n):
                ins.then_inc(signal, 1)
                dve.wait_ge(signal, n)

            def norm_stats(k, n):
                b, tiles = norm_tiles(k, n)
                if k == 0:
                    dve.wait_ge((x_in, x1_in)[b], 16)
                for t in range(NT)[tiles]:
                    last = nc.vector.bn_stats(stats[:, b, t, :], x_sb[:, b, t, :])
                own(last)
                for t in range(NT)[tiles]:
                    last = nc.vector.bn_aggr(mean_var[:, b, t, :], stats[:, b, t, :])
                own(last)
                nc.vector.tensor_scalar(var_eps[:, b, tiles], mean_var[:, b, tiles, 1], LN_EPS[k], None,
                                        ALU.add).then_inc(var_ready, 1)

            def norm_apply(k, n):
                b, tiles = norm_tiles(k, n)
                turn = NORM_TURN[(k, n)]
                dve.wait_ge(rstd_ready, turn + 1)
                before = [v for (k_, n_), v in NORM_TURN.items() if v < turn and norm_tiles(k_, n_)[0] == b]
                if before:
                    dve.wait_ge(nT_raw, max(before) + 1)
                for t in range(NT)[tiles]:
                    last = nc.vector.tensor_scalar(normed[b][:, t, :], x_sb[:, b, t, :], mean_var[:, b, t, 0:1],
                                                   rstd[:, b, t:t + 1], ALU.subtract, ALU.mult)
                last.then_inc(normed_ready, 1)

            def keep(name, *steps):
                dve.wait_ge(con_raw, made(name))
                for step in steps[:-1]:
                    own(step())
                tell(steps[-1](), con_sb, made(name))

            def grid(bank, a, n, p=P):
                return ps[0:p, bank, 0:a * n].rearrange("p (a n) -> p a n", a=a)

            def bank_of(name, a, n, p=P):
                return grid(con_bank(name), a, n, p)

            for b in range(B):
                own(nc.vector.memset(attn0[b][:, :, L:LP], 0.0))
                own(nc.vector.memset(Vc[b][64:LP, :], 0.0))
                own(nc.vector.memset(Vc[b][64:L, :], 1.0))
                own(nc.vector.memset(Vc[b][0:64, :], 1.0))
            own(nc.vector.memset(v0[64:LP, :, :], 0.0))
            own(nc.vector.memset(zero16[:, :], 0.0))
            norm_stats(0, 0)
            keep("kT0", lambda: nc.vector.tensor_copy(kT0[:, :], ps[:, con_bank("kT0"), 0:B * L]))
            norm_stats(0, 1)
            norm_apply(0, 0)
            keep("score_w",
                 lambda: nc.vector.tensor_copy(score_w[:, :, L:L + NEXP],
                                               router_w[:, 0:1, :].to_broadcast([P, B, NEXP])),
                 lambda: nc.vector.tensor_copy(score_w[:, :, 0:L], bank_of("score_w", B, L)))
            norm_apply(0, 1)
            keep("v0", lambda: nc.vector.tensor_copy(v0[0:L, :, :], bank_of("v0", B, C, L)))
            for b in range(B):
                nc.vector.memset(V[b][:, :, :], 1.0).then_inc(ones_set, 1)

            def first_softmax(b):
                dve.wait_ge(s0_raw, b + 1)
                scores = ps[:, SIDE[b], :].rearrange("p (t n) -> p t n", t=NT)
                own(nc.vector.tensor_reduce(red0[:, b, 0, :], scores[:, :, 0:L], axis=AX, op=ALU.max, negate=True))
                own(nc.vector.tensor_copy(router_x[:, b, :, :], scores[:, :, L:L + NEXP]))
                tell(nc.vector.tensor_tensor(attn0[b][:, :, 0:L], scores[:, :, 0:L],
                                             red0[:, b, 0, :].unsqueeze(2).to_broadcast([P, NT, L]), ALU.add),
                     s0_sub, b + 1)

            def first_softmax_norm(b):
                dve.wait_ge(s0_exp, b + 1)
                own(nc.vector.tensor_reduce(red0[:, b, 1, :], attn0[b][:, :, 0:L], axis=AX, op=ALU.add))
                own(nc.vector.reciprocal(red0[:, b, 2, :], red0[:, b, 1, :]))
                tell(nc.vector.tensor_tensor(attn0[b][:, :, 0:L], attn0[b][:, :, 0:L],
                                             red0[:, b, 2, :].unsqueeze(2).to_broadcast([P, NT, L]), ALU.mult),
                     s0_norm, b + 1)

            def keep_attention(b):
                dve.wait_ge(s0T_raw, b + 1)
                nc.vector.tensor_copy(attn0T[b][:, :], ps[0:LP, SIDE[b], :]).then_inc(s0T_ready, 1)

            def keep_hidden_bias():
                keep("hidden_b", lambda: nc.vector.tensor_tensor(
                    hidden_b[:, :, :], bank_of("hidden_b", HC, B),
                    w("w_early", "cols")[:, COLS.index("e_b1_0"):COLS.index("e_b1_0") + HC].unsqueeze(2)
                    .to_broadcast([P, HC, B]), ALU.add))

            def keep_router_bias():
                dve.wait_ge(const_in, 48)
                keep("router_b", lambda: nc.vector.tensor_tensor(
                    router_bc[:, :, :], bank_of("router_b", B, NEXP),
                    router_b[:, :].unsqueeze(1).to_broadcast([P, B, NEXP]), ALU.add))

            def route_logits(b):
                dve.wait_ge(rt_raw, b + 1)
                r = route[:, b, :, :]
                tell(nc.vector.tensor_tensor(
                    r, ps[:, SIDE[b], 0:4 * NT].rearrange("p (t n) -> p t n", n=4)[:, :, 0:NEXP],
                    router_x[:, b, :, :], ALU.add), rt_read, b + 1)
                own(nc.vector.tensor_tensor(r, r, router_bc[:, b, :].unsqueeze(1).to_broadcast([P, NT, NEXP]),
                                            ALU.add))
                own(nc.vector.tensor_reduce(red0[:, b, 0, :], r, axis=AX, op=ALU.max, negate=True))
                tell(nc.vector.tensor_tensor(r, r, red0[:, b, 0, :].unsqueeze(2).to_broadcast([P, NT, NEXP]),
                                             ALU.add), rt_sub, b + 1)

            def route_norm(b):
                r = route[:, b, :, :]
                dve.wait_ge(rt_exp, b + 1)
                own(nc.vector.tensor_reduce(red0[:, b, 1, :], r, axis=AX, op=ALU.add))
                own(nc.vector.reciprocal(red0[:, b, 2, :], red0[:, b, 1, :]))
                tell(nc.vector.tensor_tensor(r, r, red0[:, b, 2, :].unsqueeze(2).to_broadcast([P, NT, NEXP]),
                                             ALU.mult), rt_ready, b + 1)

            def expert_weights():
                dve.wait_ge(rows_in, 16)
                keep("e_out_b", lambda: nc.vector.tensor_tensor(
                    e_out_b[:, :, :], bank_of("e_out_b", NEXP, C),
                    row("out_b").unsqueeze(1).to_broadcast([P, NEXP, C]), ALU.add))
                keep("e_out_w0", lambda: nc.vector.tensor_copy(e_out_w[:, 0:4, :], bank_of("e_out_w0", 4, C)))
                keep("e_out_w1", lambda: nc.vector.tensor_copy(e_out_w[:, 4:6, :], bank_of("e_out_w1", 2, C)))

            def condition_columns():
                shift0 = COLS.index("shift_msa")
                keep("ada",
                     lambda: nc.vector.tensor_tensor(
                         ada_cols[:, :, :], bank_of("ada", 4, B),
                         w("w_early", "cols")[:, shift0:shift0 + 4].unsqueeze(2).to_broadcast([P, 4, B]), ALU.add),
                     lambda: nc.vector.tensor_scalar(ada_cols[:, 1:4:2, :], ada_cols[:, 1:4:2, :], 1.0, None, ALU.add))

            def folded_weights():
                gate0, o0 = ROWS.index("gate_msa"), ROWS.index("self_o_b")
                keep("gates", *[
                    lambda b=b: nc.vector.tensor_tensor(gates[:, b, :, :], bank_of("gates", 2 * B, C)[:, 2 * b:2 * b + 2, :],
                                                        rows[:, gate0:gate0 + 2, :], ALU.add) for b in range(B)])
                keep("o_bias", lambda: nc.vector.tensor_tensor(o_bias[:, :, :], bank_of("o_bias", 2, C), rows[:, o0:o0 + 2, :],
                                                               ALU.add))
                keep("kTc", lambda: nc.vector.tensor_scalar(kcf[:, :], ps[:, con_bank("kTc"), 0:B * L], col("kv_k"),
                                                            None, ALU.add))
                keep("Vc", *[
                    lambda b=b: nc.vector.tensor_copy(
                        Vc[b][0:L, 0:NH * VS].rearrange("p (h s) -> p h s", s=VS)[:, :, 0:D],
                        ps[0:L, con_bank("Vc"), b * C:(b + 1) * C].rearrange("p (h d) -> p h d", d=D)) for b in range(B)])
                own(nc.vector.tensor_copy(kc_parts[:, 0, :], kcf[:, :]))
                own(nc.vector.tensor_tensor(kc_rest[:, :], kcf[:, :], kc_parts[:, 0, :], ALU.subtract))
                own(nc.vector.tensor_copy(kc_parts[:, 1, :], kc_rest[:, :]))
                tell(nc.vector.tensor_tensor(kc_parts[:, 2, :], kc_rest[:, :], kc_parts[:, 1, :], ALU.subtract),
                     kc_split, 1)

            def gate_sum(b):
                dve.wait_ge(g2_raw, b + 1)
                if b:
                    dve.wait_ge(x1_ready, b)
                tell(nc.vector.tensor_tensor(gate[:, :, :], grid(PVB, NT, C),
                                             row("gate_b2").unsqueeze(1).to_broadcast([P, NT, C]), ALU.add),
                     g2_sum, b + 1)

            def expert_sum(b, pair):
                if pair == 0:
                    dve.wait_ge(e_bias, b + 1)
                for e in range(NEXP):
                    for t in (2 * pair, 2 * pair + 1):
                        n = NT * b + t
                        if e == 0:
                            dve.wait_ge(e2_raw, n + 1)
                        ins = nc.vector.scalar_tensor_tensor(
                            routed[:, t, :], ps[:, OUT_BANK[b][t], e * C:(e + 1) * C], route[:, b, t, e:e + 1],
                            x_bias[:, b, t, :] if e == 0 else routed[:, t, :], op0=ALU.mult, op1=ALU.add)
                        if e == NEXP - 1:
                            ins.then_inc(e2_read, 1)
                    if e < NEXP - 1:
                        own(ins)
                dve.wait_ge(e2_read, n + 1)

            def gated_sum(b):
                dve.wait_ge(g2_tanh, b + 1)
                own(nc.vector.scalar_tensor_tensor(routed[:, :, :], gate[:, :, :], 1.0, routed[:, :, :],
                                                   op0=ALU.add, op1=ALU.mult))
                tell(nc.vector.scalar_tensor_tensor(x_sb[:, b, :, :], routed[:, :, :], 0.5, x_sb[:, b, :, :],
                                                    op0=ALU.mult, op1=ALU.add), x1_ready, b + 1)

            def lower_parts(parts, rest, bank, bias, width):
                hi, mid, lo = (parts[:, i, 0:width] for i in range(NPART))
                for out_ in (rest[:, 0:width], mid):
                    ins = nc.vector.scalar_tensor_tensor(out_, ps[:, bank, 0:width], bias, hi, op0=ALU.add,
                                                         op1=ALU.subtract)
                return ins, lambda: nc.vector.tensor_tensor(lo, rest[:, 0:width], mid, ALU.subtract)

            def split_q(stage, bank, bias, width):
                n = Q_SPLITS[stage]
                dve.wait_ge(q_hi, n + 1)
                ins, lowest = lower_parts(q_parts, q_rest, bank, bias, width)
                tell(ins, qf_ready, max(n, 1))
                tell(lowest(), q_split, n + 1)

            def split_k(b):
                dve.wait_ge(k_hi, b + 1)
                ins, lowest = lower_parts(k_parts, k_rest, QKV_BANK[b][1], col("qkv_k"), T)
                tell(ins, kf_ready, b + 1)
                tell(lowest(), k_split, b + 1)

            def self_maxima(i):
                b, t, h = max_place(i)
                turn = MAX_TURN[("max", i)]
                dve.wait_ge(max_raw, turn + 1)
                nc.vector.tensor_reduce(neg_max[:, b, t, h:h + 1], ps[:, MAX0 + turn % 2, :], axis=AX, op=ALU.max,
                                        negate=True).then_inc(max_read, 1)

            def cross_maxima(u, i):
                b, tiles = unit_tiles(u)
                turn = MAX_TURN[("cross_max", (u, i))]
                dve.wait_ge(max_raw, turn + 1)
                nc.vector.tensor_reduce(
                    neg_max[:, b, tiles, CH * i:CH * (i + 1)],
                    ps[:, MAX0 + turn % 2, :].rearrange("p (t h n) -> p t h n", t=NTU, n=P)[:, :, :, 0:L],
                    axis=AX, op=ALU.max, negate=True).then_inc(max_read, 1)

            def split_maxima(kind, u, g):
                b, tiles = unit_tiles(u)
                n = SPLIT_TURN[("max_split", (kind, u, g))]
                h0, nh = (g * HG, HG) if kind == "self" else (0, NH)
                m = neg_max[:, b, tiles, h0:h0 + nh]
                rest = max_rest[:, :, 0:nh]
                part = [max_parts[:, :, i * nh:(i + 1) * nh] for i in range(NPART)]
                last = (("max", GROUP_MAX * (NG * u + g + 1) - 1) if kind == "self" else
                        ("cross_max", (u, NH // CH - 1)))
                dve.wait_ge(max_read, MAX_TURN[last] + 1)
                if n:
                    dve.wait_ge(mT_raw, n)
                own(nc.vector.tensor_copy(part[0], m))
                own(nc.vector.tensor_tensor(rest, m, part[0], ALU.subtract))
                own(nc.vector.tensor_copy(part[1], rest))
                tell(nc.vector.tensor_tensor(part[2], rest, part[1], ALU.subtract), max_split, n + 1)

            def normalize_values(*group):
                _, u, g = group
                n = GROUPS.index(group)
                b, tiles = unit_tiles(u)
                dve.wait_ge(pvT_raw, n + 1)
                pv = ps[:, MISC, :].rearrange("p (t j s) -> p t j s", t=NTU, j=HG)
                own(nc.vector.reciprocal(inv_sum[:, :, :], pv[:, :, :, D]))
                tell(nc.vector.tensor_tensor(
                    heads[b][:, tiles, g * HG * D:(g + 1) * HG * D].rearrange("p t (j d) -> p t j d", d=D),
                    pv[:, :, :, 0:D], inv_sum[:, :, :].unsqueeze(3).to_broadcast([P, NTU, HG, D]), ALU.mult),
                    heads_ready, n + 1)

            def residual(kind, u):
                b, tiles = unit_tiles(u)
                n = PROJECT_TURN[(kind, u)]
                dve.wait_ge(xb_ready, BIAS_TURN[("project", (kind, u))] + 1)
                dve.wait_ge(o_raw, n + 1)
                tell(nc.vector.tensor_tensor(x_sb[:, b, tiles, :], grid(MISC, NTU, C), x_bias[:, b, tiles, :],
                                             ALU.add), x_ready, n + 1)

            def output(u):
                b, tiles = unit_tiles(u)
                n = MLP_TURN[u]
                dve.wait_ge(xb_ready, BIAS_TURN[("mlp_down", u)] + 1)
                dve.wait_ge(m2_raw, n + 1)
                tell(nc.vector.tensor_tensor(x_sb[:, b, tiles, :], grid(DOWN_BANK[u], NTU, C), x_bias[:, b, tiles, :],
                                             ALU.add), y_ready, n + 1)

            for stage, n in STAGES:
                if stage == "scores":
                    first_softmax(n)
                elif stage == "scores_norm":
                    first_softmax_norm(n)
                elif stage == "scores_T":
                    keep_attention(n)
                elif stage == "bias":
                    (keep_hidden_bias, keep_router_bias)[n]()
                elif stage == "route":
                    route_logits(n)
                elif stage == "route_norm":
                    route_norm(n)
                elif stage == "weights":
                    (expert_weights, condition_columns, folded_weights)[n]()
                elif stage == "gate":
                    gate_sum(n)
                elif stage == "expert":
                    if n[1] % 2:
                        expert_sum(n[0], n[1] // 2)
                elif stage == "gated":
                    gated_sum(n)
                elif stage == "stats":
                    norm_stats(*n)
                elif stage == "apply":
                    norm_apply(*n)
                elif stage == "keys" and n == 0:
                    split_k(n)
                elif stage == "queries" and n == 0:
                    split_q(("queries", n), QKV_BANK[n][0], col("qkv_q"), T)
                elif stage == "max":
                    self_maxima(n)
                elif stage == "max_split":
                    split_maxima(*n)
                elif stage == "values_T":
                    normalize_values(*n)
                elif stage == "project":
                    residual(*n)
                elif stage == "query":
                    split_q(("query", n), MISC, col("q_b"), TU)
                elif stage == "cross_max":
                    cross_maxima(*n)
                elif stage == "mlp_down":
                    output(n)

        @block.tensor
        def _(pe):
            reader = {}

            def claim(bank):
                for signal, n in reader.get(bank, ()):
                    pe.wait_ge(signal, n)

            def read_by(bank, signal, n, *others):
                reader[bank] = ((signal, n),) + others

            def tiles_of(t):
                return slice(t * P, (t + 1) * P)

            def mm(out, lhsT, rhs, start=True, stop=True):
                return nc.tensor.matmul(out, lhsT, rhs, start=start, stop=stop)

            def product(name, emit):
                bank = con_bank(name)
                claim(bank)
                emit(bank).then_inc(con_raw, 1)
                read_by(bank, con_sb, made(name))

            pe.wait_ge(early_in, 16)
            product("kT0", lambda bank: mm(ps[:, bank, 0:B * L], w("w_early", "Wk"), ctxT))
            pe.wait_ge(con_sb, made("kT0"))
            product("score_w", lambda bank: mm(ps[:, bank, 0:B * L], w("w_early", "WqT"), kT0[:, :]))

            def per_sequence(bank, rhs):
                for b in range(B):
                    last = mm(ps[0:L, bank, b * C:(b + 1) * C], ctxT[:, b * L:(b + 1) * L], rhs)
                return last

            product("v0", lambda bank: per_sequence(bank, w("w_early", "Wv")))

            def transpose_normed(k, n):
                b, tiles = norm_tiles(k, n)
                turn = NORM_TURN[(k, n)]
                bank = SIDE[b] if k == 0 else MISC
                pe.wait_ge(normed_ready, turn + 1)
                claim(bank)
                for i, t in enumerate(range(NT)[tiles]):
                    last = nc.tensor.transpose(ps[:, bank, tiles_of(i)], normed[b][:, t, :], ident[:, :])
                last.then_inc(nT_raw, 1)
                read_by(bank, nT_ready, turn + 1)

            pe.wait_ge(const_in, 48)
            for b in range(B):
                transpose_normed(0, b)

            def context_scores(b):
                if b == 0:
                    pe.wait_ge(con_sb, made("score_w"))
                pe.wait_ge(nT_ready, b + 1)
                claim(SIDE[b])
                for t in range(NT):
                    last = mm(ps[:, SIDE[b], t * P:t * P + L + NEXP], nT[b][:, tiles_of(t)], score_w[:, b, :])
                last.then_inc(s0_raw, 1)
                read_by(SIDE[b], s0_sub, b + 1)

            def hidden_bias(bank):
                for c in range(HC):
                    last = mm(ps[:, bank, B * c:B * (c + 1)], hidden_w(c, 2), w("w_early", "cols")[:, 0:B])
                return last

            def router_bias(bank):
                for b in range(B):
                    last = mm(ps[:, bank, NEXP * b:NEXP * (b + 1)], spread(col(f"cond{b}")), router_w[:, 2, :])
                return last

            def input_bias(n):
                if n == 0:
                    pe.wait_ge(hidden_in, 16)
                product(*(("hidden_b", hidden_bias), ("router_b", router_bias))[n])

            def chunk_products(bank, n, lhsT, rhs):
                for i in range(n):
                    last = mm(ps[:, bank, i * C:(i + 1) * C], lhsT(i), rhs(i))
                return last

            def hidden_layer(b, c):
                bank = EXP0 + c % 4
                claim(bank)
                mm(ps[:, bank, :], hidden_w(c, 0), nT[b][:, :], stop=False)
                mm(ps[:, bank, :], hidden_w(c, 1), evT[b], start=False).then_inc(hid_raw, 1)
                read_by(bank, hid_ready, HC * b + c + 1)

            def transpose_scores(b):
                pe.wait_ge(s0_norm, b + 1)
                claim(SIDE[b])
                for t in range(NT):
                    last = nc.tensor.transpose(ps[0:LP, SIDE[b], tiles_of(t)], attn0[b][:, t, :], ident[:, :])
                last.then_inc(s0T_raw, 1)
                read_by(SIDE[b], s0T_ready, b + 1)

            def evidence(b):
                if b == 0:
                    pe.wait_ge(con_sb, made("v0"))
                pe.wait_ge(s0T_ready, b + 1)
                claim(SIDE[b])
                mm(ps[:, SIDE[b], :], v0[:, b, :], attn0T[b][:, :]).then_inc(ev_raw, 1)
                read_by(SIDE[b], ev_ready, b + 1)

            def route_scores(b):
                pe.wait_ge(ev_ready, b + 1)
                claim(SIDE[b])
                for t in range(NT):
                    last = mm(ps[:, SIDE[b], 4 * t:4 * t + NEXP], evT[b][:, tiles_of(t)], router_w[:, 1, :])
                last.then_inc(rt_raw, 1)
                read_by(SIDE[b], rt_read, b + 1)

            def gate_output(b):
                pe.wait_ge(hid_ready, HC * (b + 1))
                claim(PVB)
                for t in range(NT):
                    last = mm(ps[:, PVB, tiles_of(t)], hidden[:, HC - 1, tiles_of(t)], w("w_out", "gate_w2"))
                last.then_inc(g2_raw, 1)
                read_by(PVB, g2_sum, b + 1)

            def expert_output(b, t):
                pe.wait_ge(con_sb, made("e_out_w1"))
                bank = OUT_BANK[b][t]
                claim(bank)
                for e in range(NEXP):
                    for k in range(2):
                        last = mm(ps[:, bank, e * C:(e + 1) * C], hidden[:, 2 * e + k, tiles_of(t)],
                                  e_out_w[:, 2 * e + k, :], start=k == 0, stop=k == 1)
                last.then_inc(e2_raw, 1)
                read_by(bank, e2_read, NT * b + t + 1)

            def keys(b):
                bank = QKV_BANK[b][1]
                pe.wait_ge(nT_ready, NORM_TURN[(1, b)] + 1)
                claim(bank)
                mm(ps[:, bank, :], w("w_attn", "wk"), nT[b][:, :]).then_inc(k_raw, 1)
                read_by(bank, *((k_hi, 2) if b else (kf_ready, 1)))

            def queries(b):
                bank = QKV_BANK[b][0]
                claim(bank)
                mm(ps[:, bank, :], w("w_attn", "wq"), nT[b][:, :]).then_inc(q_raw, 1)
                read_by(bank, *((q_hi, Q_SPLITS[("queries", 1)] + 1) if b else (qf_ready, 1)))

            def values(b):
                bank = QKV_BANK[b][2]
                claim(bank)
                for t in range(NT):
                    last = mm(ps[:, bank, tiles_of(t)], nT[b][:, tiles_of(t)], w("w_attn", "wv"))
                last.then_inc(v_raw, 1)
                read_by(bank, v_ready, b + 1)

            def fold_expert_weights():
                e_w2T = w("w_out", "e_w2T")
                pe.wait_ge(out_in, 16)
                product("e_out_b", lambda bank: chunk_products(bank, NEXP, lambda i: spread(col(f"e_b2_{i}")),
                                                               lambda i: w("w_out", "out_w")))
                product("e_out_w0", lambda bank: chunk_products(bank, 4, lambda i: e_w2T[:, tiles_of(i)],
                                                                lambda i: w("w_out", "out_w")))
                product("e_out_w1", lambda bank: chunk_products(bank, 2, lambda i: e_w2T[:, tiles_of(4 + i)],
                                                                lambda i: w("w_out", "out_w")))

            def condition_columns():
                pe.wait_ge(attn_in, 16)
                pe.wait_ge(silu_done, 1)

                def ada_columns(bank):
                    for j, k in enumerate(ADA_COLS):
                        last = mm(ps[:, bank, B * j:B * (j + 1)], ada_w[:, k, :], silu_cond[:, :])
                    return last

                product("ada", ada_columns)

            def fold_weights():
                product("gates", lambda bank: chunk_products(bank, 2 * B, lambda i: spread(silu_cond[:, i // 2:i // 2 + 1]),
                                                             lambda i: ada_w[:, ADA_ROWS[i % 2], :]))
                product("o_bias", lambda bank: chunk_products(bank, 2, lambda i: spread(col(("qkv_v", "kv_v")[i])),
                                                              lambda i: w("w_attn", ("self_o", "cross_o")[i])))
                product("kTc", lambda bank: mm(ps[:, bank, 0:B * L], w("w_attn", "kv_k"), ctxT))
                product("Vc", lambda bank: per_sequence(bank, w("w_attn", "kv_v")))

            def self_max_scores(i):
                b, t, h = max_place(i)
                u, first = i // (GROUP_MAX * NG), i % (GROUP_MAX * NG)
                if first == 0:
                    pe.wait_ge(q_in[u], 16)
                if first % GROUP_MAX == 0:
                    pe.wait_ge(k_in[NG * b + first // GROUP_MAX], 16 * NPART)
                turn = MAX_TURN[("max", i)]
                claim(MAX0 + turn % 2)
                mm(ps[:, MAX0 + turn % 2, :], Qs[u][:, h, tiles_of(t % NTU)], Ks[b][:, h, :]).then_inc(max_raw, 1)
                read_by(MAX0 + turn % 2, max_read, turn + 1)

            def cross_max_scores(u, i):
                b, _ = unit_tiles(u)
                if i == 0:
                    pe.wait_ge(kc_in, 16 * MROW // D)
                    pe.wait_ge(q_in[NU + u], 16)
                turn = MAX_TURN[("cross_max", (u, i))]
                claim(MAX0 + turn % 2)
                for t in range(NTU):
                    for j in range(CH):
                        h, at_ = CH * i + j, (CH * t + j) * P
                        last = mm(ps[:, MAX0 + turn % 2, at_:at_ + L], Qs[u][0:MROW, h, tiles_of(t)],
                                  Kc[0:MROW, h, b, 0:L])
                last.then_inc(max_raw, 1)
                read_by(MAX0 + turn % 2, max_read, turn + 1)

            def transpose_maxima(kind, u, g):
                n = SPLIT_TURN[("max_split", (kind, u, g))]
                nr = NPART * (HG if kind == "self" else NH)
                pe.wait_ge(max_split, n + 1)
                claim(MISC)
                for t in range(NTU):
                    last = nc.tensor.transpose(ps[0:nr, MISC, :].bitcast(BF16)[:, tiles_of(t)],
                                               max_parts[:, t, 0:nr], ident16[:, :])
                last.then_inc(mT_raw, 1)
                read_by(MISC, mT_ready, n + 1)

            def exp_scores(s, pr):
                kind, u, g, kt = TILES[s]
                b, _ = unit_tiles(u)
                if pr == 0 and kt == 0:
                    n = SPLIT_TURN[("max_split", (kind, u, g if kind == "self" else 0))]
                    pe.wait_ge(m_in[n % 2], 16 * (n // 2 + 1))
                e = 2 * s + pr
                for j in range(CT):
                    h = HG * g + CT * pr + j
                    bank, at_ = EXP0 + 2 * (e % 2) + j // 2, j % 2 * TU
                    claim(bank)
                    if kind == "cross":
                        last = mm(ps[0:LP, bank, at_:at_ + TU], Kc[:, h, b, :], Qs[u][:, h, :])
                    else:
                        last = mm(ps[:, bank, at_:at_ + TU], Ks[b][:, h, tiles_of(kt)], Qs[u][:, h, :])
                for j in range(2):
                    read_by(EXP0 + 2 * (e % 2) + j, exp_ready, e + 1)
                last.then_inc(exp_raw, 1)

            def weigh_values(s, r):
                kind, u, g, kt = TILES[s]
                b, _ = unit_tiles(u)
                pe.wait_ge(exp_ready, 2 * s + r + 1)
                if kt == 0 and r == 0:
                    if kind == "self" and g == 0:
                        pe.wait_ge(v_ready, b + 1)
                    claim(PVB)
                    if kind == "self":
                        mm(ps[:, PVB, :], spread(zero16[:, :]), zero16[:, :].to_broadcast([P, T]), stop=False)
                for c in range(CT):
                    j = CT * r + c
                    h = HG * g + j
                    out_ = ps[32 * c:32 * c + 32, PVB, r * TU:(r + 1) * TU]
                    if kind == "cross":
                        last = mm(out_, Vc[b][:, VS * h:VS * h + 32], probs[0:LP, s % UNITS, j, :])
                    else:
                        last = mm(out_, V[b][:, kt, VS * h:VS * h + 32], probs[:, s % UNITS, j, :], start=False,
                                  stop=kt == NT - 1 and r == 1)
                last.then_inc(pv_raw, 1)
                read_by(PVB, pv_ready, GROUPS.index((kind, u, g)) + 1)

            def transpose_values(*group):
                n = GROUPS.index(group)
                pe.wait_ge(pv_ready, n + 1)
                claim(MISC)
                for r in range(HG // CT):
                    for t in range(NTU):
                        last = nc.tensor.transpose(ps[:, MISC, tiles_of(HG // CT * t + r)],
                                                   pv_sb[:, tiles_of(NTU * r + t)], ident[:, :])
                last.then_inc(pvT_raw, 1)
                read_by(MISC, heads_ready, n + 1)

            def transpose_heads(kind, u):
                b, tiles = unit_tiles(u)
                n = PROJECT_TURN[(kind, u)]
                pe.wait_ge(heads_ready, GROUPS.index((kind, u, NG - 1)) + 1)
                claim(MISC)
                for i, t in enumerate(range(NT)[tiles]):
                    last = nc.tensor.transpose(ps[:, MISC, tiles_of(i)], heads[b][:, t, :], ident[:, :])
                last.then_inc(hT_raw, 1)
                read_by(MISC, hT_ready, n + 1)

            def project(kind, u):
                b, _ = unit_tiles(u)
                n = PROJECT_TURN[(kind, u)]
                if kind == "self":
                    pe.wait_ge(folded, b + 1)
                claim(MISC)
                for t in range(NTU):
                    last = mm(ps[:, MISC, tiles_of(t)], headsT[:, tiles_of(t)],
                              self_o[:, b, :] if kind == "self" else w("w_attn", "cross_o"))
                last.then_inc(o_raw, 1)
                read_by(MISC, x_ready, n + 1)

            def cross_queries(u):
                b, tiles = unit_tiles(u)
                pe.wait_ge(nT_ready, NORM_TURN[(2, u)] + 1)
                claim(MISC)
                mm(ps[:, MISC, 0:TU], w("w_attn", "q_w"), nT[b][:, tiles.start * P:tiles.stop * P]).then_inc(q_raw, 1)
                read_by(MISC, qf_ready, Q_SPLITS[("query", u)])

            def mlp_up(u, j):
                b, tiles = unit_tiles(u)
                turn = MLP_UP_TURN[("mlp_up", (u, j))]
                bank = UP_BANK[u][j]
                pe.wait_ge(nT_ready, NORM_TURN[(3, u)] + 1)
                pe.wait_ge(mlp_in, 16)
                claim(bank)
                for i in range(2):
                    last = mm(ps[:, bank, i * TU:(i + 1) * TU], mlp_w1[:, 2 * j + i, :],
                              nT[b][:, tiles.start * P:tiles.stop * P])
                last.then_inc(m1_raw, 1)
                read_by(bank, m1_ready, 2 * (turn + 1))

            def mlp_down(u):
                b, _ = unit_tiles(u)
                pe.wait_ge(m1_ready, 2 * (MLP_UP_TURN[("mlp_up", (u, MC // 2 - 1))] + 1))
                claim(DOWN_BANK[u])
                for t in range(NTU):
                    for c in range(MC):
                        last = mm(ps[:, DOWN_BANK[u], tiles_of(t)], mlp_h[u][:, c, tiles_of(t)], mlp_w2g[:, b, c, :],
                                  start=c == 0, stop=c == MC - 1)
                last.then_inc(m2_raw, 1)
                read_by(DOWN_BANK[u], y_ready, MLP_TURN[u] + 1)

            for stage, n in STAGES:
                if stage == "scores":
                    context_scores(n)
                elif stage == "bias":
                    input_bias(n)
                elif stage == "scores_T":
                    transpose_scores(n)
                elif stage == "evidence":
                    evidence(n)
                elif stage == "route":
                    route_scores(n)
                elif stage == "hidden":
                    hidden_layer(*n)
                elif stage == "weights":
                    (fold_expert_weights, condition_columns, fold_weights)[n]()
                elif stage == "gate":
                    gate_output(n)
                elif stage == "expert":
                    expert_output(*n)
                elif stage == "norm_T":
                    transpose_normed(*n)
                elif stage == "keys":
                    keys(n)
                elif stage == "queries":
                    queries(n)
                elif stage == "values":
                    values(n)
                elif stage == "max":
                    if n == 0:
                        pe.wait_ge(pad_in, 16 * (B + NU + 1))
                    self_max_scores(n)
                elif stage == "max_T":
                    transpose_maxima(*n)
                elif stage == "exp":
                    exp_scores(*n)
                elif stage == "weigh":
                    weigh_values(*n)
                elif stage == "values_T":
                    transpose_values(*n)
                elif stage == "heads_T":
                    transpose_heads(*n)
                elif stage == "project":
                    project(*n)
                elif stage == "query":
                    cross_queries(n)
                elif stage == "cross_max":
                    cross_max_scores(*n)
                elif stage == "mlp_up":
                    mlp_up(*n)
                elif stage == "mlp_down":
                    mlp_down(n)


def kernel(**inputs):
    import numpy as np
    import ml_dtypes
    import concourse.bacc as bacc
    from concourse.bass_utils import run_bass_kernel_spmd

    a = {k: np.asarray(v) for k, v in inputs.items()}
    l0 = {k[len("L0_xcond_"):]: v for k, v in a.items() if k.startswith("L0_xcond_")}
    l1 = {k[len("L1_xcond_"):]: v for k, v in a.items() if k.startswith("L1_xcond_")}

    def by_dim(v):
        return v.reshape(v.shape[:-1] + (NH, D)).swapaxes(-1, -2).reshape(v.shape)

    def rows_first(v, k):
        return v.reshape(k, P, -1).transpose(1, 0, 2).reshape(P, -1)

    qkv_b = l1["qkv_b"].reshape(3, C)
    kv_b = l1["kv_b"].reshape(2, C)
    ada_b = l1["ada_b"].reshape(6, C)
    e_b1 = l0["e_b1"].reshape(HC - 1, P)
    mlp_b1 = l1["mlp_b1"].reshape(MC, P)
    columns = {
        "cond0": a["cond_1024"][0], "cond1": a["cond_1024"][1], "ln_gamma": l0["ln_gamma"],
        "ln_beta": l0["ln_beta"], "gate_b1": l0["gate_b1"], "shift_msa": ada_b[0], "scale_msa": ada_b[1],
        "shift_mlp": ada_b[3], "scale_mlp": ada_b[4], "qkv_q": by_dim(qkv_b[0]), "qkv_k": by_dim(qkv_b[1]),
        "qkv_v": qkv_b[2], "norm2_g": l1["norm2_g"], "norm2_b": l1["norm2_b"], "q_b": by_dim(l1["q_b"]),
        "kv_k": by_dim(kv_b[0]), "kv_v": kv_b[1],
        **{f"e_b1_{i}": e_b1[i] for i in range(HC - 1)}, **{f"mlp_b1_{i}": mlp_b1[i] for i in range(MC)},
        **{f"e_b2_{i}": l0["e_b2"][i] for i in range(NEXP)},
    }
    free_rows = {
        "gate_b2": l0["gate_b2"], "out_b": l0["out_b"], "gate_msa": ada_b[2], "gate_mlp": ada_b[5],
        "self_o_b": l1["self_o_b"], "cross_o_b": l1["cross_o_b"], "mlp_b2": l1["mlp_b2"],
    }
    qkv_w, kv_w = l1["qkv_w"], l1["kv_w"]
    parts = {
        "cols": np.stack([columns[n] for n in COLS], axis=1),
        "ctxT": a["ctx_1024"].transpose(2, 0, 1).reshape(C, B * L),
        "WqT": l0["Wq"].T, "Wk": l0["Wk"], "Wv": l0["Wv"], "router": rows_first(l0["router_W"], 3),
        "gate_w1": rows_first(l0["gate_w1"], 3),
        "e_w1": l0["e_w1"].reshape(NEXP, 3, P, RH).transpose(2, 0, 1, 3).reshape(P, -1),
        "e_w2T": l0["e_w2"].transpose(2, 0, 1).reshape(C, NEXP * RH), "out_w": l0["out_w"],
        "gate_w2": l0["gate_w2"], "ada": l1["ada_w"],
        "wq": by_dim(qkv_w[:, 0:C]), "wk": by_dim(qkv_w[:, C:2 * C]), "wv": qkv_w[:, 2 * C:3 * C],
        "self_o": l1["self_o_w"], "q_w": by_dim(l1["q_w"]), "kv_k": by_dim(kv_w[:, 0:C]),
        "kv_v": kv_w[:, C:2 * C], "cross_o": l1["cross_o_w"], "w1": l1["mlp_w1"],
        "w2": rows_first(l1["mlp_w2"], MC),
    }
    pad = np.zeros((2, KS - MROW, T), ml_dtypes.bfloat16)
    pad[0, 0:NPART] = 1
    arrays = {"x": a["x"], "rows": np.concatenate([free_rows[n] for n in ROWS]),
              "router_b": l0["router_b"], "ident": np.eye(P, dtype=np.float32),
              "ident16": np.eye(P, dtype=ml_dtypes.bfloat16), "pad": pad}
    for pack, fields in PACKS.items():
        arrays[pack] = np.concatenate([parts[n] for n, _ in fields], axis=1)

    nc = bacc.Bacc("TRN2", target_bir_lowering=False, num_devices=1)
    arrays = {f"in_{n}": np.ascontiguousarray(v) for n, v in arrays.items()}
    d = {n[3:]: nc.dram_tensor(n, v.shape, mybir.dt.from_np(v.dtype), kind="ExternalInput").ap()
         for n, v in arrays.items()}
    out = nc.dram_tensor("out_0", (B, T, C), mybir.dt.float32, kind="ExternalOutput").ap()
    mixed_expert_attention_kernel(nc, d["x"], {n: d[n] for n in PACKS},
                                  d["rows"].rearrange("(r c) -> r c", c=C), d["router_b"], d["ident"],
                                  d["ident16"], d["pad"], out)
    result = run_bass_kernel_spmd(nc, [arrays], core_ids=[0])
    return result.results[0]["out_0"]
```
